# Optimizing a Trainium2 kernel written in Bass

```python
import numpy as np
import jax
import jax.numpy as jnp

def _softmax(x, axis=-1):
    return jax.nn.softmax(x, axis=axis)

def _gelu(x):
    return jax.nn.gelu(x, approximate=True)

def _silu(x):
    return jax.nn.silu(x)

def _sigmoid(x):
    return jax.nn.sigmoid(x)

def _layernorm(x, axis=-1, eps=1e-05):
    m = jnp.mean(x, axis=axis, keepdims=True)
    v = jnp.var(x, axis=axis, keepdims=True)
    return (x - m) / jnp.sqrt(v + eps)

def _scatter_add(tgt, idx, src, axis=0):
    return tgt.at[idx].add(src)

def _segment_sum(src, seg, n):
    return jax.ops.segment_sum(src, seg, n)
kernel_name = 'mk_xattn_ffn_d4_seqx_r8_9103e9'

def setup_inputs(seed: int=0):
    np.random.seed(seed)
    _w = jnp.asarray

    def _rec_inputs():
        import jax
        import jax.numpy as jnp
        _rk = jax.random.key(seed)
        x = -0.0003929 + 0.9999 * jax.random.normal(jax.random.fold_in(_rk, 1), (64, 64, 256), jnp.float32)
        _lenS = 64 - jax.random.randint(jax.random.fold_in(_rk, 7), (64,), 0, max(1, 64 // 4) + 1, jnp.int32)
        _lenS2 = 64 - jax.random.randint(jax.random.fold_in(_rk, 8), (64,), 0, max(1, 64 // 4) + 1, jnp.int32)
        _ctx_2048P = jax.random.normal(jax.random.fold_in(_rk, 11), (64, 16, 256), jnp.float32)
        _ctx_2048c = jax.random.dirichlet(jax.random.fold_in(_rk, 511), 0.3 * jnp.ones((16,), jnp.float32), (64, 64))
        _ctx_2048t = jnp.einsum('bsk,bkd->bsd', _ctx_2048c, _ctx_2048P)
        _ctx_2048t = _ctx_2048t * jax.lax.rsqrt(jnp.mean(jnp.square(_ctx_2048t)) + 1e-12) * 0.953939
        ctx_2048 = -0.000514642 + 1.00011 * (_ctx_2048t + 0.3 * jax.random.normal(jax.random.fold_in(_rk, 611), (64, 64, 256), jnp.float32))
        _validS = jnp.arange(64)[None, :] < _lenS[:, None]
        _validS2 = jnp.arange(64)[None, :] < _lenS2[:, None]
        _causal = jnp.tril(jnp.ones((64, 64), dtype=bool))
        mask_BxSxS2_ff0 = jnp.where(jnp.ones((64, 64, 64), dtype=bool), 0.0, -1000000000.0).astype(jnp.float32)
        mask_BxS2_bk0 = jnp.logical_not(jnp.broadcast_to(_validS2[:, :], (64, 64)))
        return (x, ctx_2048, mask_BxSxS2_ff0, mask_BxS2_bk0)
    x, ctx_2048, mask_BxSxS2_ff0, mask_BxS2_bk0 = _rec_inputs()

    def _L0_xattn_setup():
        import jax, jax.numpy as jnp
        import numpy as np
        NUM_HEADS = 16
        EPS = 1e-08

        def _dyn_quant(x):
            s = jnp.maximum(jnp.max(jnp.abs(x), axis=-1, keepdims=True) / 127.0, EPS)
            q = jnp.clip(jnp.round(x / s), -127.0, 127.0)
            return (q, s)

        def _quant_weight(w):
            s = jnp.maximum(jnp.max(jnp.abs(w), axis=1, keepdims=True) / 127.0, EPS)
            q = jnp.clip(jnp.round(w / s), -127.0, 127.0)
            return (q, s)

        def _w8a8_linear(x, w, b):
            qx, sx = _dyn_quant(x)
            qw, sw = _quant_weight(w)
            y = jnp.einsum('bnc,oc->bno', qx, qw) * (sx * sw[:, 0])
            return y + b
        key = jax.random.key(seed)
        ks = jax.random.split(key, 9)
        B, N, L, C = (2, 512, 64, 256)
        sc = 0.02
        return {'x': jax.random.normal(ks[0], (B, N, C), jnp.float32), 'cond': jax.random.normal(ks[1], (B, L, C), jnp.float32), 'mask': jnp.zeros((B, N, L), jnp.float32), 'wq': jax.random.normal(ks[2], (C, C), jnp.float32) * sc, 'bq': jnp.zeros((C,), jnp.float32), 'wk': jax.random.normal(ks[3], (C, C), jnp.float32) * sc, 'bk': jnp.zeros((C,), jnp.float32), 'wv': jax.random.normal(ks[4], (C, C), jnp.float32) * sc, 'bv': jnp.zeros((C,), jnp.float32), 'wo': jax.random.normal(ks[5], (C, C), jnp.float32) * sc, 'bo': jnp.zeros((C,), jnp.float32)}
    _L0_xattn_all = _L0_xattn_setup()
    _L0_xattn_in = {k: v for k, v in _L0_xattn_all.items() if k in ('wq', 'bq', 'wk', 'bk', 'wv', 'bv', 'wo', 'bo')}
    del _L0_xattn_all

    def _L0_ffn_setup():
        import jax, jax.numpy as jnp
        import numpy as np
        B, T, D = (2, 128, 256)
        H, K, DK = (4, 8, 64)
        E = 2048
        NK = 128
        key = jax.random.key(seed)
        k1, k2, k3, k4, k5 = jax.random.split(key, 5)
        x = jax.random.normal(k1, (B, T, D), dtype=jnp.float32)
        Wq = jax.random.normal(k2, (D, 2 * H * DK), dtype=jnp.float32) * 0.02
        keys = jax.random.normal(k3, (H, NK, 2, DK), dtype=jnp.float32) * 0.02
        e_down = jax.random.normal(k4, (E, D), dtype=jnp.float32) * 0.01
        e_up = jax.random.normal(k5, (E, D), dtype=jnp.float32) * 0.01
        return {'x': x, 'Wq': Wq, 'keys': keys, 'e_down': e_down, 'e_up': e_up}
    _L0_ffn_all = _L0_ffn_setup()
    _L0_ffn_in = {k: v for k, v in _L0_ffn_all.items() if k in ('Wq', 'keys', 'e_down', 'e_up')}
    del _L0_ffn_all

    def _L1_xattn_setup():
        import jax, jax.numpy as jnp
        import numpy as np
        EPS = 1e-06
        NUM_HEADS = 16

        def _feature_map(x):
            return jnp.where(x > 0, x + 1.0, jnp.exp(x))
        key = jax.random.key(seed)
        ks = jax.random.split(key, 7)
        B, L, S, D = (4, 512, 512, 256)
        sc = 1.0 / np.sqrt(D)
        return {'query': jax.random.normal(ks[0], (B, L, D), jnp.float32), 'kv': jax.random.normal(ks[1], (B, S, D), jnp.float32), 'Wq': jax.random.normal(ks[2], (D, D), jnp.float32) * sc, 'Wg': jax.random.normal(ks[3], (D, D), jnp.float32) * sc, 'bg': jnp.ones((D,), jnp.float32), 'Wkv': jax.random.normal(ks[4], (2 * D, D), jnp.float32) * sc, 'Wo': jax.random.normal(ks[5], (D, D), jnp.float32) * sc}
    _L1_xattn_all = _L1_xattn_setup()
    _L1_xattn_in = {k: v for k, v in _L1_xattn_all.items() if k in ('Wq', 'Wg', 'bg', 'Wkv', 'Wo')}
    del _L1_xattn_all

    def _L1_ffn_setup():
        import jax, jax.numpy as jnp
        import numpy as np
        BLOCK = 64

        def dequant4bit(q, scale):
            return (q.astype(jnp.float32) - 7.5) * jnp.repeat(scale, BLOCK, axis=1)
        key = jax.random.key(seed)
        ks = jax.random.split(key, 11)
        B, S, D, H, R = (4, 256, 256, 1024, 16)
        return {'x1': jax.random.normal(ks[0], (B, S, D), jnp.float32), 'w_up_q': jax.random.randint(ks[1], (H, D), 0, 16, dtype=jnp.int32), 'w_up_scale': jax.random.uniform(ks[2], (H, D // BLOCK), jnp.float32) * 0.02, 'b_up': jax.random.normal(ks[3], (H,), jnp.float32) * 0.01, 'w_up_lora_a': jax.random.normal(ks[4], (D, R), jnp.float32) * 0.02, 'w_up_lora_b': jax.random.normal(ks[5], (R, H), jnp.float32) * 0.02, 'w_down_q': jax.random.randint(ks[6], (D, H), 0, 16, dtype=jnp.int32), 'w_down_scale': jax.random.uniform(ks[7], (D, H // BLOCK), jnp.float32) * 0.02, 'b_down': jax.random.normal(ks[8], (D,), jnp.float32) * 0.01, 'w_down_lora_a': jax.random.normal(ks[9], (H, R), jnp.float32) * 0.02, 'w_down_lora_b': jax.random.normal(ks[10], (R, D), jnp.float32) * 0.02}
    _L1_ffn_all = _L1_ffn_setup()
    _L1_ffn_in = {k: v for k, v in _L1_ffn_all.items() if k in ('w_up_q', 'w_up_scale', 'b_up', 'w_up_lora_a', 'w_up_lora_b', 'w_down_q', 'w_down_scale', 'b_down', 'w_down_lora_a', 'w_down_lora_b')}
    del _L1_ffn_all

    def _L2_xattn_setup():
        import jax, jax.numpy as jnp
        import numpy as np
        key = jax.random.key(seed)
        k1, k2, k3 = jax.random.split(key, 3)
        B, S, D, M = (8, 256, 256, 128)
        hidden_states = jax.random.normal(k1, (B, S, D), dtype=jnp.float32)
        memory_tokens = jax.random.normal(k2, (B, M, D), dtype=jnp.float32)
        memory_mask = jax.random.randint(k3, (B, M), 0, 2).astype(jnp.bool_)
        return {'hidden_states': hidden_states, 'memory_tokens': memory_tokens, 'memory_mask': memory_mask}
    _L2_xattn_all = _L2_xattn_setup()
    _L2_xattn_in = {k: v for k, v in _L2_xattn_all.items() if k in ()}
    del _L2_xattn_all

    def _L2_ffn_setup():
        import jax, jax.numpy as jnp
        import numpy as np
        B, S, D = (2, 256, 256)
        H, HD = (16, 128)
        E, K, I = (16, 6, 176)
        SI = 352
        EPS = 1e-06

        def rmsnorm(x, w):
            v = jnp.mean(jnp.square(x), axis=-1, keepdims=True)
            return x * jax.lax.rsqrt(v + EPS) * w
        key = jax.random.key(seed)
        ks = jax.random.split(key, 14)
        s = 0.02
        return {'hidden_states': jax.random.normal(ks[0], (B, S, D), jnp.float32), 'ln1_w': jnp.ones((D,), jnp.float32), 'ln2_w': jnp.ones((D,), jnp.float32), 'wq': jax.random.normal(ks[1], (D, H * HD), jnp.float32) * s, 'wk': jax.random.normal(ks[2], (D, H * HD), jnp.float32) * s, 'wv': jax.random.normal(ks[3], (D, H * HD), jnp.float32) * s, 'wo': jax.random.normal(ks[4], (H * HD, D), jnp.float32) * s, 'gate_w': jax.random.normal(ks[5], (E, D), jnp.float32) * s, 'eg_w': jax.random.normal(ks[6], (E, I, D), jnp.float32) * s, 'eu_w': jax.random.normal(ks[7], (E, I, D), jnp.float32) * s, 'ed_w': jax.random.normal(ks[8], (E, D, I), jnp.float32) * s, 'sg_w': jax.random.normal(ks[9], (SI, D), jnp.float32) * s, 'su_w': jax.random.normal(ks[10], (SI, D), jnp.float32) * s, 'sd_w': jax.random.normal(ks[11], (D, SI), jnp.float32) * s}
    _L2_ffn_all = _L2_ffn_setup()
    _L2_ffn_in = {k: v for k, v in _L2_ffn_all.items() if k in ('ln1_w', 'ln2_w', 'wq', 'wk', 'wv', 'wo', 'gate_w', 'eg_w', 'eu_w', 'ed_w', 'sg_w', 'su_w', 'sd_w')}
    del _L2_ffn_all

    def _L3_xattn_setup():
        import jax, jax.numpy as jnp
        import numpy as np
        H = 256
        NH = 16
        HD = H // NH
        EPS = 1e-06

        def rmsnorm(x, w, eps=EPS):
            var = jnp.mean(x * x, axis=-1, keepdims=True)
            return x * jax.lax.rsqrt(var + eps) * w
        key = jax.random.key(seed)
        ks = jax.random.split(key, 9)
        B, L, M = (4, 512, 32)
        s = 1.0 / np.sqrt(H)
        return {'hidden_states': jax.random.normal(ks[0], (B, L, H), dtype=jnp.float32), 'memory_tokens': jax.random.normal(ks[1], (B, M, H), dtype=jnp.float32), 'memory_mask': jax.random.randint(ks[2], (B, M), 0, 2).astype(bool), 'norm_w': jnp.ones((H,), dtype=jnp.float32), 'wq': jax.random.normal(ks[3], (H, H), dtype=jnp.float32) * s, 'wk': jax.random.normal(ks[4], (H, H), dtype=jnp.float32) * s, 'wv': jax.random.normal(ks[5], (H, H), dtype=jnp.float32) * s, 'wo': jax.random.normal(ks[6], (H, H), dtype=jnp.float32) * s, 'wg': jax.random.normal(ks[7], (H, H), dtype=jnp.float32) * s}
    _L3_xattn_all = _L3_xattn_setup()
    _L3_xattn_in = {k: v for k, v in _L3_xattn_all.items() if k in ('norm_w', 'wq', 'wk', 'wv', 'wo', 'wg')}
    del _L3_xattn_all

    def _L3_ffn_setup():
        import jax, jax.numpy as jnp
        import numpy as np
        H = 256
        I = 128
        E = 16
        K = 2
        B, S = (4, 128)
        key = jax.random.key(seed)
        ks = jax.random.split(key, 5)
        scale = 0.02
        x = jax.random.normal(ks[0], (B, S, H), dtype=jnp.float32)
        gate_w = jax.random.normal(ks[1], (E, H), dtype=jnp.float32) * scale
        wg = jax.random.normal(ks[2], (E, H, I), dtype=jnp.float32) * scale
        wu = jax.random.normal(ks[3], (E, H, I), dtype=jnp.float32) * scale
        wd = jax.random.normal(ks[4], (E, I, H), dtype=jnp.float32) * scale
        return {'x': x, 'gate_w': gate_w, 'wg': wg, 'wu': wu, 'wd': wd}
    _L3_ffn_all = _L3_ffn_setup()
    _L3_ffn_in = {k: v for k, v in _L3_ffn_all.items() if k in ('gate_w', 'wg', 'wu', 'wd')}
    del _L3_ffn_all
    return {'x': x, 'ctx_2048': ctx_2048, 'mask_BxSxS2_ff0': mask_BxSxS2_ff0, 'mask_BxS2_bk0': mask_BxS2_bk0, 'L0_xattn_wq': _L0_xattn_in['wq'], 'L0_xattn_bq': _L0_xattn_in['bq'], 'L0_xattn_wk': _L0_xattn_in['wk'], 'L0_xattn_bk': _L0_xattn_in['bk'], 'L0_xattn_wv': _L0_xattn_in['wv'], 'L0_xattn_bv': _L0_xattn_in['bv'], 'L0_xattn_wo': _L0_xattn_in['wo'], 'L0_xattn_bo': _L0_xattn_in['bo'], 'L0_ffn_Wq': _L0_ffn_in['Wq'], 'L0_ffn_keys': _L0_ffn_in['keys'], 'L0_ffn_e_down': _L0_ffn_in['e_down'], 'L0_ffn_e_up': _L0_ffn_in['e_up'], 'L1_xattn_Wq': _L1_xattn_in['Wq'], 'L1_xattn_Wg': _L1_xattn_in['Wg'], 'L1_xattn_bg': _L1_xattn_in['bg'], 'L1_xattn_Wkv': _L1_xattn_in['Wkv'], 'L1_xattn_Wo': _L1_xattn_in['Wo'], 'L1_ffn_w_up_q': _L1_ffn_in['w_up_q'], 'L1_ffn_w_up_scale': _L1_ffn_in['w_up_scale'], 'L1_ffn_b_up': _L1_ffn_in['b_up'], 'L1_ffn_w_up_lora_a': _L1_ffn_in['w_up_lora_a'], 'L1_ffn_w_up_lora_b': _L1_ffn_in['w_up_lora_b'], 'L1_ffn_w_down_q': _L1_ffn_in['w_down_q'], 'L1_ffn_w_down_scale': _L1_ffn_in['w_down_scale'], 'L1_ffn_b_down': _L1_ffn_in['b_down'], 'L1_ffn_w_down_lora_a': _L1_ffn_in['w_down_lora_a'], 'L1_ffn_w_down_lora_b': _L1_ffn_in['w_down_lora_b'], 'L2_ffn_ln1_w': _L2_ffn_in['ln1_w'], 'L2_ffn_ln2_w': _L2_ffn_in['ln2_w'], 'L2_ffn_wq': _L2_ffn_in['wq'], 'L2_ffn_wk': _L2_ffn_in['wk'], 'L2_ffn_wv': _L2_ffn_in['wv'], 'L2_ffn_wo': _L2_ffn_in['wo'], 'L2_ffn_gate_w': _L2_ffn_in['gate_w'], 'L2_ffn_eg_w': _L2_ffn_in['eg_w'], 'L2_ffn_eu_w': _L2_ffn_in['eu_w'], 'L2_ffn_ed_w': _L2_ffn_in['ed_w'], 'L2_ffn_sg_w': _L2_ffn_in['sg_w'], 'L2_ffn_su_w': _L2_ffn_in['su_w'], 'L2_ffn_sd_w': _L2_ffn_in['sd_w'], 'L3_xattn_norm_w': _L3_xattn_in['norm_w'], 'L3_xattn_wq': _L3_xattn_in['wq'], 'L3_xattn_wk': _L3_xattn_in['wk'], 'L3_xattn_wv': _L3_xattn_in['wv'], 'L3_xattn_wo': _L3_xattn_in['wo'], 'L3_xattn_wg': _L3_xattn_in['wg'], 'L3_ffn_gate_w': _L3_ffn_in['gate_w'], 'L3_ffn_wg': _L3_ffn_in['wg'], 'L3_ffn_wu': _L3_ffn_in['wu'], 'L3_ffn_wd': _L3_ffn_in['wd']}

def reference(x, ctx_2048, mask_BxSxS2_ff0, mask_BxS2_bk0, L0_xattn_wq, L0_xattn_bq, L0_xattn_wk, L0_xattn_bk, L0_xattn_wv, L0_xattn_bv, L0_xattn_wo, L0_xattn_bo, L0_ffn_Wq, L0_ffn_keys, L0_ffn_e_down, L0_ffn_e_up, L1_xattn_Wq, L1_xattn_Wg, L1_xattn_bg, L1_xattn_Wkv, L1_xattn_Wo, L1_ffn_w_up_q, L1_ffn_w_up_scale, L1_ffn_b_up, L1_ffn_w_up_lora_a, L1_ffn_w_up_lora_b, L1_ffn_w_down_q, L1_ffn_w_down_scale, L1_ffn_b_down, L1_ffn_w_down_lora_a, L1_ffn_w_down_lora_b, L2_ffn_ln1_w, L2_ffn_ln2_w, L2_ffn_wq, L2_ffn_wk, L2_ffn_wv, L2_ffn_wo, L2_ffn_gate_w, L2_ffn_eg_w, L2_ffn_eu_w, L2_ffn_ed_w, L2_ffn_sg_w, L2_ffn_su_w, L2_ffn_sd_w, L3_xattn_norm_w, L3_xattn_wq, L3_xattn_wk, L3_xattn_wv, L3_xattn_wo, L3_xattn_wg, L3_ffn_gate_w, L3_ffn_wg, L3_ffn_wu, L3_ffn_wd):
    import jax
    import jax.numpy as jnp

    def _L0_xattn_ref(x, cond, mask, wq, bq, wk, bk, wv, bv, wo, bo):
        import jax, jax.numpy as jnp
        import numpy as np
        NUM_HEADS = 16
        EPS = 1e-08

        def _dyn_quant(x):
            s = jnp.maximum(jnp.max(jnp.abs(x), axis=-1, keepdims=True) / 127.0, EPS)
            q = jnp.clip(jnp.round(x / s), -127.0, 127.0)
            return (q, s)

        def _quant_weight(w):
            s = jnp.maximum(jnp.max(jnp.abs(w), axis=1, keepdims=True) / 127.0, EPS)
            q = jnp.clip(jnp.round(w / s), -127.0, 127.0)
            return (q, s)

        def _w8a8_linear(x, w, b):
            qx, sx = _dyn_quant(x)
            qw, sw = _quant_weight(w)
            y = jnp.einsum('bnc,oc->bno', qx, qw) * (sx * sw[:, 0])
            return y + b
        B, N, C = x.shape
        L = cond.shape[1]
        H = NUM_HEADS
        D = C // H
        inv_sqrt_d = np.float32(1.0 / np.sqrt(D))
        q = _w8a8_linear(x, wq, bq).reshape(B, N, H, D).transpose(0, 2, 1, 3)
        k = (cond @ wk.T + bk).reshape(B, L, H, D).transpose(0, 2, 1, 3)
        v = (cond @ wv.T + bv).reshape(B, L, H, D).transpose(0, 2, 1, 3)
        scores = jnp.einsum('bhnd,bhld->bhnl', q, k) * inv_sqrt_d + mask[:, None]
        attn = jax.nn.softmax(scores, axis=-1)
        o = jnp.einsum('bhnl,bhld->bhnd', attn, v)
        o = o.transpose(0, 2, 1, 3).reshape(B, N, C)
        return _w8a8_linear(o, wo, bo)

    def _L0_ffn_ref(x, Wq, keys, e_down, e_up):
        import jax, jax.numpy as jnp
        import numpy as np
        B, T, D = (2, 128, 256)
        H, K, DK = (4, 8, 64)
        E = 2048
        NK = 128
        b, t, d = x.shape
        q = (x @ Wq).reshape(b, t, H, 2, DK)
        q1, q2 = (q[..., 0, :], q[..., 1, :])
        sim1 = jnp.einsum('bthd,hkd->bthk', q1, keys[:, :, 0, :])
        sim2 = jnp.einsum('bthd,hkd->bthk', q2, keys[:, :, 1, :])
        s1, i1 = jax.lax.top_k(sim1, K)
        s2, i2 = jax.lax.top_k(sim2, K)
        all_scores = (s1[..., :, None] + s2[..., None, :]).reshape(b, t, H, K * K)
        all_indices = (i1[..., :, None] * NK + i2[..., None, :]).reshape(b, t, H, K * K)
        final_scores, pk_idx = jax.lax.top_k(all_scores, K)
        final_indices = jnp.take_along_axis(all_indices, pk_idx, axis=-1)
        w_down = e_down[final_indices]
        w_up = e_up[final_indices]
        hidden = jnp.einsum('btd,bthkd->bthk', x, w_down)
        hidden = jax.nn.silu(hidden)
        hidden = hidden * jax.nn.relu(final_scores)
        out = jnp.einsum('bthk,bthkd->btd', hidden, w_up)
        return out

    def _L1_xattn_ref(query, kv, Wq, Wg, bg, Wkv, Wo):
        import jax, jax.numpy as jnp
        import numpy as np
        EPS = 1e-06
        NUM_HEADS = 16

        def _feature_map(x):
            return jnp.where(x > 0, x + 1.0, jnp.exp(x))
        B, L, D = query.shape
        S = kv.shape[1]
        H = NUM_HEADS
        hd = D // H
        q = query @ Wq.T
        gate = jax.nn.sigmoid(query @ Wg.T + bg)
        kvp = kv @ Wkv.T
        k, v = jnp.split(kvp, 2, axis=-1)
        q = _feature_map(q.reshape(B, L, H, hd).transpose(0, 2, 1, 3))
        k = _feature_map(k.reshape(B, S, H, hd).transpose(0, 2, 1, 3))
        v = v.reshape(B, S, H, hd).transpose(0, 2, 1, 3)
        kv_summary = jnp.einsum('bhsd,bhse->bhde', k, v)
        k_sum = k.sum(axis=-2)
        z = 1.0 / (jnp.einsum('bhld,bhd->bhl', q, k_sum)[..., None] + EPS)
        attn = jnp.einsum('bhld,bhde->bhle', q, kv_summary) * z
        attn = attn.transpose(0, 2, 1, 3).reshape(B, L, D)
        out = attn * gate @ Wo.T
        return out

    def _L1_ffn_ref(x1, w_up_q, w_up_scale, b_up, w_up_lora_a, w_up_lora_b, w_down_q, w_down_scale, b_down, w_down_lora_a, w_down_lora_b):
        import jax, jax.numpy as jnp
        import numpy as np
        BLOCK = 64

        def dequant4bit(q, scale):
            return (q.astype(jnp.float32) - 7.5) * jnp.repeat(scale, BLOCK, axis=1)
        w_up = dequant4bit(w_up_q, w_up_scale).T
        y1 = x1 @ w_up + b_up + x1 @ w_up_lora_a @ w_up_lora_b
        x2 = jax.nn.relu(y1)
        w_down = dequant4bit(w_down_q, w_down_scale).T
        y2 = x2 @ w_down + b_down + x2 @ w_down_lora_a @ w_down_lora_b
        return y2

    def _L2_xattn_ref(hidden_states, memory_tokens, memory_mask):
        import jax, jax.numpy as jnp
        import numpy as np
        B, S, D = hidden_states.shape
        scale = 1.0 / jnp.sqrt(jnp.asarray(D, hidden_states.dtype))
        scores = jnp.einsum('bsd,bmd->bsm', hidden_states, memory_tokens) * scale
        neg_inf = jnp.asarray(-1e+30, scores.dtype)
        scores = jnp.where(memory_mask[:, None, :], scores, neg_inf)
        attn = jax.nn.softmax(scores, axis=-1)
        readout = jnp.einsum('bsm,bmd->bsd', attn, memory_tokens)
        valid_b = jnp.any(memory_mask, axis=-1)
        out = jnp.where(valid_b[:, None, None], readout, jnp.zeros_like(readout))
        return out

    def _L2_ffn_ref(hidden_states, ln1_w, ln2_w, wq, wk, wv, wo, gate_w, eg_w, eu_w, ed_w, sg_w, su_w, sd_w):
        import jax, jax.numpy as jnp
        import numpy as np
        B, S, D = (2, 256, 256)
        H, HD = (16, 128)
        E, K, I = (16, 6, 176)
        SI = 352
        EPS = 1e-06

        def rmsnorm(x, w):
            v = jnp.mean(jnp.square(x), axis=-1, keepdims=True)
            return x * jax.lax.rsqrt(v + EPS) * w
        b, s, d = hidden_states.shape
        x = hidden_states
        h = rmsnorm(x, ln1_w)
        q = (h @ wq).reshape(b, s, H, HD)
        k = (h @ wk).reshape(b, s, H, HD)
        v = (h @ wv).reshape(b, s, H, HD)
        scores = jnp.einsum('bqhd,bkhd->bhqk', q, k) / np.sqrt(HD).astype(np.float32)
        causal = jnp.tril(jnp.ones((s, s), bool))
        scores = jnp.where(causal, scores, jnp.float32(-1000000000.0))
        attn = jax.nn.softmax(scores, axis=-1)
        ao = jnp.einsum('bhqk,bkhd->bqhd', attn, v).reshape(b, s, H * HD) @ wo
        x = x + ao
        h = rmsnorm(x, ln2_w)
        t = h.reshape(-1, d)
        T = t.shape[0]
        logits = t @ gate_w.T
        probs = jax.nn.softmax(logits, axis=-1)
        topv, topi = jax.lax.top_k(probs, K)
        topv = topv / jnp.sum(topv, axis=-1, keepdims=True)
        cw = jnp.zeros((T, E), t.dtype).at[jnp.arange(T)[:, None], topi].add(topv)
        g = jnp.einsum('td,eid->eti', t, eg_w)
        u = jnp.einsum('td,eid->eti', t, eu_w)
        hh = jax.nn.silu(g) * u
        routed = jnp.einsum('eti,edi,te->td', hh, ed_w, cw)
        shared = jax.nn.silu(t @ sg_w.T) * (t @ su_w.T) @ sd_w.T
        out = x + (routed + shared).reshape(b, s, d)
        return out

    def _L3_xattn_ref(hidden_states, memory_tokens, memory_mask, norm_w, wq, wk, wv, wo, wg):
        import jax, jax.numpy as jnp
        import numpy as np
        H = 256
        NH = 16
        HD = H // NH
        EPS = 1e-06

        def rmsnorm(x, w, eps=EPS):
            var = jnp.mean(x * x, axis=-1, keepdims=True)
            return x * jax.lax.rsqrt(var + eps) * w
        B, L, C = hidden_states.shape
        M = memory_tokens.shape[1]
        scale = HD ** (-0.5)
        x = rmsnorm(hidden_states, norm_w)
        q = (x @ wq.T).reshape(B, L, NH, HD)
        k = (memory_tokens @ wk.T).reshape(B, M, NH, HD)
        v = (memory_tokens @ wv.T).reshape(B, M, NH, HD)
        attn = jnp.einsum('blhd,bmhd->bhlm', q, k) * scale
        attn = jnp.where(memory_mask[:, None, None, :], attn, -jnp.inf)
        attn = jax.nn.softmax(attn, axis=-1)
        attn = jnp.nan_to_num(attn, nan=0.0)
        out = jnp.einsum('bhlm,bmhd->blhd', attn, v).reshape(B, L, C)
        out = out @ wo.T
        gate = jax.nn.sigmoid(x @ wg.T)
        return gate * out

    def _L3_ffn_ref(x, gate_w, wg, wu, wd):
        import jax, jax.numpy as jnp
        import numpy as np
        H = 256
        I = 128
        E = 16
        K = 2
        B, S = (4, 128)
        b, s, h = x.shape
        xf = x.reshape(-1, h)
        T = xf.shape[0]
        scores = jax.nn.softmax(xf @ gate_w.T, axis=-1)
        topk_w, topk_idx = jax.lax.top_k(scores, K)
        topk_w = topk_w / (jnp.sum(topk_w, axis=-1, keepdims=True) + 1e-20)
        combine = jnp.zeros((T, E), dtype=xf.dtype).at[jnp.arange(T)[:, None], topk_idx].add(topk_w)
        g = jnp.einsum('th,ehi->tei', xf, wg)
        u = jnp.einsum('th,ehi->tei', xf, wu)
        a = jax.nn.silu(g) * u * combine[:, :, None]
        y = jnp.einsum('tei,eih->th', a, wd)
        return y.reshape(b, s, h)
    x = x + _L0_xattn_ref(_layernorm(x, axis=-1), ctx_2048, mask_BxSxS2_ff0, L0_xattn_wq, L0_xattn_bq, L0_xattn_wk, L0_xattn_bk, L0_xattn_wv, L0_xattn_bv, L0_xattn_wo, L0_xattn_bo)
    x = x + _L0_ffn_ref(_layernorm(x, axis=-1), L0_ffn_Wq, L0_ffn_keys, L0_ffn_e_down, L0_ffn_e_up)
    x = x + _L1_xattn_ref(_layernorm(x, axis=-1), ctx_2048, L1_xattn_Wq, L1_xattn_Wg, L1_xattn_bg, L1_xattn_Wkv, L1_xattn_Wo)
    x = x + _L1_ffn_ref(_layernorm(x, axis=-1), L1_ffn_w_up_q, L1_ffn_w_up_scale, L1_ffn_b_up, L1_ffn_w_up_lora_a, L1_ffn_w_up_lora_b, L1_ffn_w_down_q, L1_ffn_w_down_scale, L1_ffn_b_down, L1_ffn_w_down_lora_a, L1_ffn_w_down_lora_b)
    x = x + _L2_xattn_ref(_layernorm(x, axis=-1), ctx_2048, mask_BxS2_bk0)
    x = x + _L2_ffn_ref(_layernorm(x, axis=-1), L2_ffn_ln1_w, L2_ffn_ln2_w, L2_ffn_wq, L2_ffn_wk, L2_ffn_wv, L2_ffn_wo, L2_ffn_gate_w, L2_ffn_eg_w, L2_ffn_eu_w, L2_ffn_ed_w, L2_ffn_sg_w, L2_ffn_su_w, L2_ffn_sd_w)
    x = x + _L3_xattn_ref(_layernorm(x, axis=-1), ctx_2048, mask_BxS2_bk0, L3_xattn_norm_w, L3_xattn_wq, L3_xattn_wk, L3_xattn_wv, L3_xattn_wo, L3_xattn_wg)
    x = x + _L3_ffn_ref(_layernorm(x, axis=-1), L3_ffn_gate_w, L3_ffn_wg, L3_ffn_wu, L3_ffn_wd)
    return x

_drawn_inputs = setup_inputs


def setup_inputs(seed=0):
    import zlib

    import numpy as np

    out = dict(_drawn_inputs(seed))
    spreads = {'L0_xattn_bq': (0.0, 0.8),
     'L0_xattn_bk': (0.0, 2.0),
     'L0_xattn_bv': (0.0, 0.284),
     'L0_xattn_bo': (0.0, 0.1),
     'L1_xattn_bg': (1.0, 0.6),
     'L2_ffn_ln1_w': (1.0, 0.6),
     'L2_ffn_ln2_w': (1.0, 0.6),
     'L3_xattn_norm_w': (1.0, 0.6)}
    factors = {'L0_xattn_wq': 8.0,
     'L0_xattn_wk': 8.0,
     'L0_ffn_Wq': 8.0,
     'L0_ffn_keys': 8.0,
     'L0_ffn_e_down': 8.0,
     'L0_ffn_e_up': 8.0,
     'L1_xattn_Wq': 15.232,
     'L1_ffn_b_up': 8.0,
     'L1_ffn_w_up_lora_a': 3.003,
     'L1_ffn_w_up_lora_b': 3.009,
     'L1_ffn_b_down': 8.0,
     'L1_ffn_w_down_lora_a': 3.077,
     'L1_ffn_w_down_lora_b': 3.203,
     'L2_ffn_wq': 8.0,
     'L2_ffn_wk': 8.0,
     'L2_ffn_gate_w': 8.0,
     'L2_ffn_eg_w': 8.0,
     'L2_ffn_eu_w': 8.0,
     'L2_ffn_ed_w': 8.0,
     'L2_ffn_sg_w': 7.078,
     'L2_ffn_su_w': 7.011,
     'L2_ffn_sd_w': 6.953,
     'L3_ffn_gate_w': 8.0,
     'L3_ffn_wg': 8.0,
     'L3_ffn_wu': 8.0,
     'L3_ffn_wd': 8.0,
     'L3_xattn_wq': 8.0,
     'L3_xattn_wk': 8.0,
     'L3_xattn_wv': 5.259,
     'L3_xattn_wo': 5.168,
     'L3_xattn_wg': 8.0}
    for name, (base, spread) in spreads.items():
        noise = np.random.default_rng([zlib.crc32(name.encode()), seed]).standard_normal(out[name].shape)
        drawn = base * np.exp(spread * noise) if base else spread * noise
        out[name] = jnp.asarray(drawn.astype(out[name].dtype))
    for name, factor in factors.items():
        out[name] = (out[name] * factor).astype(out[name].dtype)
    return out
```

```python
import concourse.bass as bass
from concourse import mybir
from contextlib import ExitStack

FP32 = mybir.dt.float32
FP32R = mybir.dt.float32r
BF16 = mybir.dt.bfloat16
U8 = mybir.dt.uint8
U32 = mybir.dt.uint32
I32 = mybir.dt.int32
ALU = mybir.AluOpType
ACT = mybir.ActivationFunctionType
AX = mybir.AxisListType

P = 128
B, S, D = 64, 64, 256
T = B * S
NG = T // P
C = D // P
TILE = 512
NT = T // TILE
GT = TILE // P
LN_EPS = 1e-5
MAGIC = 1.5 * 2.0 ** 23
BIG = 1e30


def some(n):
    return not isinstance(n, int) or n > 0


class Chain:

    def __init__(self, sem, per_tile):
        self.sem, self.per_tile, self.k = sem, per_tile, 0

    def begin(self, t, k=0):
        self.t, self.k = t, k

    def next(self):
        self.k += 1
        return self.t * self.per_tile + self.k

    def end(self):
        assert self.k == self.per_tile, (self.k, self.per_tile)


class Core:

    def __init__(self, nc, ctx, args):
        self.nc, self.args = nc, args
        self.x = ctx.enter_context(nc.sbuf_tensor("x", [P, NG * D], FP32))
        self.ident = ctx.enter_context(nc.sbuf_tensor("ident", [P, P], FP32))
        self.identb = ctx.enter_context(nc.sbuf_tensor("identb", [P, P], BF16))
        self.neghalf = ctx.enter_context(nc.sbuf_tensor("neghalf", [P, 16], FP32))
        self.bank = [ctx.enter_context(nc.psum_tensor(f"bank{i}", [P, 512], FP32)) for i in range(8)]


class Stage:

    def __init__(self, core, name):
        self.core, self.nc, self.name = core, core.nc, name
        self.ctx, self.sems = ExitStack(), []

    def sb(self, name, shape, dt=FP32):
        return self.ctx.enter_context(self.nc.sbuf_tensor(f"{self.name}_{name}", shape, dt))

    def passed(self):
        return self.sem("passed")

    def sem(self, name):
        s = self.ctx.enter_context(self.nc.semaphore(f"{self.name}_{name}"))
        self.sems.append(s)
        return s

    def close(self):
        with self.nc.Block() as block:
            @block.gpsimd
            def _(pool):
                for s in self.sems:
                    pool.sem_clear(s)
        self.ctx.close()


def load_block(core):
    nc = core.nc
    st = Stage(core, "init")
    x_in, zeroed, made = st.sem("x_in"), st.sem("zeroed"), st.sem("made")
    with nc.Block() as block:
        @block.sync
        def _(sp):
            for q in range(4):
                n = NG // 4
                sp.dma_start(core.x[:, q * n * D:(q + 1) * n * D].rearrange("p (g d) -> p g d", d=D),
                             core.args["x"][q * n * P:(q + 1) * n * P, :].rearrange("(g p) d -> p g d", p=P)).then_inc(x_in, 16)
            sp.wait_ge(x_in, 64)

        @block.gpsimd
        def _(pool):
            nc.gpsimd.memset(core.neghalf[:], -0.5).then_inc(zeroed, 1)
            nc.gpsimd.memset(core.ident[:], 0.0).then_inc(zeroed, 1)
            pool.wait_ge(zeroed, 2)
            nc.gpsimd.affine_select(out=core.ident[:], in_=core.ident[:], compare_op=ALU.not_equal, fill=1.0,
                                    base=0, pattern=[[-1, P]], channel_multiplier=1).then_inc(made, 1)
            pool.wait_ge(made, 1)
            nc.gpsimd.tensor_copy(core.identb[:], core.ident[:]).then_inc(made, 1)
    st.close()


def store_block(core):
    nc = core.nc
    st = Stage(core, "store")
    out_done = st.sem("out_done")
    with nc.Block() as block:
        @block.sync
        def _(sp):
            sp.dma_start(core.args["out"].rearrange("(g p) d -> p g d", p=P),
                         core.x[:].rearrange("p (g d) -> p g d", d=D)).then_inc(out_done, 16)
            sp.wait_ge(out_done, 16)
    st.ctx.close()


def dequant_block(core, st, wgs, wds, bup, bdn, NB):
    nc, args, bank = core.nc, core.args, core.bank
    H = NB * P
    tmp = Stage(core, st.name + "_dq")
    gq, gs = tmp.sb("gq", [P, C, H], I32), tmp.sb("gs", [P, C, H])
    dq, ds = tmp.sb("dq", [P, NB, D], I32), tmp.sb("ds", [P, NB, D])
    ua, ub = tmp.sb("ua", [16, D]), tmp.sb("ub", [16, H])
    da, db = tmp.sb("da", [16, H]), tmp.sb("db", [16, D])
    wg, wd = tmp.sb("wg", [P, C, H]), tmp.sb("wd", [P, NB, D])
    hi_made = tmp.sem("hi_made")
    q_in, scaled, lora, added = tmp.sem("q_in"), tmp.sem("scaled"), tmp.sem("lora"), tmp.sem("added")
    loads = [(gq[:], args["up_q"].rearrange("(c p) h -> p c h", p=P)),
             (gs[:], args["up_s"].rearrange("(c p) h -> p c h", p=P)),
             (dq[:], args["down_q"].rearrange("(n p) d -> p n d", p=P)),
             (ds[:], args["down_s"].rearrange("(n p) d -> p n d", p=P)),
             (ua[:], args["up_aT"]), (ub[:], args["up_b"]), (da[:], args["down_aT"]), (db[:], args["down_b"]),
             (bup[:], args["bup"]), (bdn[:], args["bdn"])]
    parts = [(ua[:, c * P:(c + 1) * P], ub[:, n * 512:(n + 1) * 512], wg[:, c, n * 512:(n + 1) * 512])
             for c in range(C) for n in range(H // 512)]
    parts += [(da[:, n * P:(n + 1) * P], db[:], wd[:, n, :]) for n in range(NB)]
    with nc.Block() as block:
        @block.sync
        def _(sp):
            for out, in_ in loads:
                sp.dma_start(out, in_).then_inc(q_in, 16)

        @block.tensor
        def _(pe):
            pe.wait_ge(q_in, 16 * len(loads))
            for n, (rows, cols, target) in enumerate(parts):
                if n >= 4:
                    pe.wait_ge(added, n - 3)
                width = cols.shape[-1]
                nc.tensor.matmul(bank[n % 4][:, 0:width], rows, cols, start=True, stop=True).then_inc(lora, 1)

        @block.vector
        def _(dve):
            dve.wait_ge(q_in, 16 * len(loads))
            nc.vector.scalar_tensor_tensor(out=wg[:], in0=gq[:], scalar=7.5, in1=gs[:], op0=ALU.subtract, op1=ALU.mult)
            nc.vector.scalar_tensor_tensor(out=wd[:], in0=dq[:], scalar=7.5, in1=ds[:], op0=ALU.subtract,
                                           op1=ALU.mult).then_inc(scaled, 1)
            dve.wait_ge(scaled, 1)
            for n, (rows, cols, target) in enumerate(parts):
                dve.wait_ge(lora, n + 1)
                width = cols.shape[-1]
                nc.vector.tensor_tensor(out=target, in0=bank[n % 4][:, 0:width], in1=target, op=ALU.add).then_inc(added, 1)
            for n, (w, parts_) in enumerate(((wg, wgs), (wd, wds))):
                dve.wait_ge(hi_made, n + 1)
                nc.vector.tensor_tensor(out=parts_[1][:], in0=w[:], in1=parts_[0][:], op=ALU.subtract)

        @block.scalar
        def _(act):
            act.wait_ge(added, len(parts))
            nc.scalar.activation(wgs[0][:], wg[:], ACT.Copy).then_inc(hi_made, 1)
            nc.scalar.activation(wds[0][:], wd[:], ACT.Copy).then_inc(hi_made, 1)
    tmp.close()


def split_weights_block(core, name, parts):
    nc = core.nc
    tmp = Stage(core, name + "_split")
    RING = 3
    raw = tmp.sb("raw", [P, RING, 1024])
    staged = [tmp.sem(f"staged{i}") for i in range(RING)]
    hi_made, lo_made = tmp.sem("hi_made"), tmp.sem("lo_made")

    def staging(k):
        src, rows, hi, lo = parts[k]
        shape, width = hi.shape, 1
        for n in shape[1:]:
            width *= n
        flat = raw[0:rows, k % RING, 0:width]
        return flat.rearrange("p (n d) -> p n d", d=shape[2]) if len(shape) == 3 else flat

    with nc.Block() as block:
        @block.sync
        def _(sp):
            for k in range(len(parts)):
                if k >= RING:
                    sp.wait_ge(lo_made, k - RING + 1)
                sp.dma_start(staging(k), parts[k][0]).then_inc(staged[k % RING], 16)

        @block.scalar
        def _(act):
            for k in range(len(parts)):
                act.wait_ge(staged[k % RING], 16 * (k // RING + 1))
                nc.scalar.activation(parts[k][2], staging(k), ACT.Copy).then_inc(hi_made, 1)

        @block.vector
        def _(dve):
            for k in range(len(parts)):
                if parts[k][3] is not None:
                    dve.wait_ge(hi_made, k + 1)
                    nc.vector.tensor_tensor(out=parts[k][3], in0=staging(k), in1=parts[k][2],
                                            op=ALU.subtract).then_inc(lo_made, 1)
    tmp.close()


def ffn_stage(core, name, kind, front_kind, blocks, top_k=0, first=0):
    nc, args, bank, x = core.nc, core.args, core.bank, core.x
    st = Stage(core, name)
    sb, sem = st.sb, st.sem
    NB = blocks
    H = NB * P
    E = 16
    gated, peer, relu = kind == "gated", kind == "peer", kind == "relu"
    ln = front_kind == "ln"

    split = gated or relu
    if split:
        wgs = [sb(n, [P, C, H], FP32R) for n in ("wg_hi", "wg_lo")]
        wus = [sb(n, [P, C, H], FP32R) for n in ("wu_hi", "wu_lo")] if gated else None
        wds = [sb(n, [P, NB, D], FP32R) for n in ("wd_hi", "wd_lo")]
        hTs = [sb(n, [P, 2, C, TILE], FP32R) for n in ("hT_hi", "hT_lo")]
        hhs = [sb(n, [P, 2, TILE], FP32R) for n in ("hh_hi", "hh_lo")]
        PARTS = ((0, 0), (0, 1), (1, 0))
        hi_ready, lo_ready, hT_hi_ready = sem("hi_ready"), sem("lo_ready"), sem("hT_hi_ready")
    else:
        wg = sb("wg", [P, C, H])
        wd = sb("wd", [P, NB, D])
        hT = sb("hT", [P, C, TILE])
    hTf = sb("hTf", [P, C, TILE])
    hh = sb("hh", [P, 2, TILE])
    a = sb("a", [P, 2, TILE])
    b = sb("b", [P, 2, TILE]) if gated else None
    G, U, CW, Y, F = bank[0:2], bank[2:4], bank[4], bank[5:7], bank[7]
    RING = [U[0], U[1], F] if peer else [F]
    R = len(RING)

    weights_in = sem("weights_in")
    g_ready, u_ready, cw_ready = sem("g_ready"), sem("u_ready"), sem("cw_ready")
    a_ready, b_ready, hh_ready, hh_used = sem("a_ready"), sem("b_ready"), sem("hh_ready"), sem("hh_used")
    passed = st.passed()
    y_used, hT_ready, hTf_ready = sem("y_used"), sem("hT_ready"), sem("hTf_ready")
    f_filled, f_emptied = sem("f_filled"), sem("f_emptied")
    if ln:
        xn = sb("xn", [P, GT, D])
        stats, mv = sb("stats", [P, GT, 6]), sb("mv", [P, GT, 2])
        ve, rstd = sb("ve", [P, GT]), sb("rstd", [P, GT])
        var_ready, rstd_ready, xn_ready = sem("var_ready"), sem("rstd_ready"), sem("xn_ready")
        ln_chain = Chain(sem("ln_chain"), 2)
    else:
        hTf_in = sem("hTf_in")
    NTR = C if ln else 0
    if gated:
        sel, gw = sb("sel", [32, H], FP32R), sb("gw", [P, C, E])
        shifted, pr, pm, cw = sb("shifted", [P, GT, E]), sb("pr", [P, GT, E]), sb("pm", [P, GT, E]), sb("cw", [P, GT, 32])
        rmax, rsum, m8 = sb("rmax", [P, GT]), sb("rsum", [P, GT]), sb("m8", [P, GT, 8])
        cwTf, cwTs = sb("cwTf", [32, TILE]), [sb(n, [32, 2, TILE], FP32R) for n in ("cwT_hi", "cwT_lo")]
        e_ready, cw_done, cw_zeroed, cw_init, cwTf_ready = sem("e_ready"), sem("cw_done"), sem("cw_zeroed"), sem("cw_init"), sem("cwTf_ready")
        router_chain = Chain(sem("router_chain"), 9)
        NF = NTR + 2
    if relu:
        bup, bdn = sb("bup", [P, NB]), sb("bdn", [P, D])
        y_sum = sem("y_sum")
        NF = NTR
        dequant_block(core, st, wgs, wds, bup, bdn, NB)
    if peer:
        NH = 4
        wq, bdk, qTs = sb("wq", [P, C, NH * P]), sb("bdk", [P, NH, 256]), sb("qTs", [P, NH, TILE])
        sims = sb("sims", [P, NH, 256])
        s8, f8, th = sb("s8", [P, NH, 2, 8]), sb("f8", [P, NH, 8]), sb("th", [P, NH])
        cand, wc, i1, past = sb("cand", [P, NH, 64]), sb("wc", [P, NH, 64]), sb("i1", [P, NH, 8], U32), sb("past", [P, NH, 8])
        rest = sb("rest", [P, 1])
        sums, tmp, wtab = sb("sums", [P, 2, H]), sb("tmp", [P, H]), sb("wtab", [P, H])
        cwT_all = sb("cwT_all", [P, 2, NB, TILE])
        
        sum_ready, sum_used = sem("sum_ready"), sem("sum_used")
        w_ready, cwT_ready, bdk_zero = sem("w_ready"), sem("cwT_ready"), sem("bdk_zero")
        peer_chain = Chain(sem("peer_chain"), GT * (7 + 1 + 6))
        NQ, NS, NW = NH, 2, H // 512
        NF = NTR + NQ + GT * (NS + NW)
        assert NF % R == 0
        SIM_SLOT = {2: 0, 5: 1, 8: 2, 11: 3}
        UNIT_SLOT = {2: [(0, 0)], 3: [(0, 1), (0, 2)], 4: [(0, 3)], 5: [(1, 0)], 6: [(1, 1), (1, 2)], 7: [(1, 3)],
                     8: [(2, 0)], 9: [(2, 1), (2, 2)], 10: [(2, 3)], 11: [(3, 0)], 12: [(3, 1), (3, 2)], 13: [(3, 3)]}
        TAB_SLOT = {5: 0, 8: 1, 11: 2, 14: 3}

    def is_first(t):
        return isinstance(t, int) and t == 0

    def is_last_tile(t):
        return isinstance(t, int) and t == NT - 1

    def group_x(t, g):
        return x[:, bass.ds(t * (GT * D) + g * D, D)]

    def norm_dve(dve, t):
        ln_chain.begin(t)
        for g in range(GT):
            i = nc.vector.bn_stats(stats[:, g, :], group_x(t, g))
        i.then_inc(ln_chain.sem, 1)
        dve.wait_ge(ln_chain.sem, ln_chain.next())
        dve.sem_inc(passed, 1)
        for g in range(GT):
            i = nc.vector.bn_aggr(mv[:, g, :], stats[:, g, :])
        i.then_inc(ln_chain.sem, 1)
        dve.wait_ge(ln_chain.sem, ln_chain.next())
        nc.vector.tensor_scalar(ve[:], mv[:, :, 1], LN_EPS, None, ALU.add).then_inc(var_ready, 1)
        if some((t - 1) * NF + NTR):
            dve.wait_ge(f_filled, (t - 1) * NF + NTR)
        dve.wait_ge(rstd_ready, t + 1)
        for g in range(GT):
            i = nc.vector.tensor_scalar(xn[:, g, :], group_x(t, g), mv[:, g, 0:1], rstd[:, g:g + 1],
                                        ALU.subtract, ALU.mult)
        i.then_inc(xn_ready, 1)
        ln_chain.end()

    def norm_pool(pool, t):
        pool.wait_ge(var_ready, t + 1)
        nc.gpsimd.tensor_tensor(out=rstd[:], in0=ve[:], in1=core.neghalf[:, 0:GT], op=ALU.pow).then_inc(rstd_ready, 1)

    def front_bank(pe, t, k):
        if some(t * NF + k + 1 - R):
            pe.wait_ge(f_emptied, t * NF + k + 1 - R)
        return RING[k % R]

    def transposes_pe(pe, t):
        pe.wait_ge(xn_ready, t + 1)
        for c in range(C):
            F_ = front_bank(pe, t, c)
            for g in range(GT):
                i = nc.tensor.transpose(F_[:, g * P:(g + 1) * P], xn[:, g, c * P:(c + 1) * P], core.ident[:])
            i.then_inc(f_filled, 1)

    def transposes_act(act, t, par):
        if some(t):
            act.wait_ge(hT_ready, t)
        if split and some((t - 1) * NB):
            act.wait_ge(u_ready if gated else g_ready, (t - 1) * NB)
        for c in range(C):
            act.wait_ge(f_filled, t * NF + c + 1)
            if split:
                nc.scalar.activation(hTs[0][:, par, c, :], RING[c % R][:], ACT.Copy)
            nc.scalar.activation(hTf[:, c, :], RING[c % R][:], ACT.Copy).then_inc(f_emptied, 1)

    def loaded_act(act, t, par):
        act.wait_ge(hTf_in, (t + 1) * 16)
        if some((t - 1) * NB):
            act.wait_ge(u_ready, (t - 1) * NB)
        nc.scalar.activation(hTs[0][:, par, :, :], hTf[:], ACT.Copy).then_inc(hT_hi_ready, 1)

    def load_front_sp(sp, t):
        if some(t):
            sp.wait_ge(hT_ready, t)
        sp.dma_start(hTf[:], args["t_scratch"].rearrange("(c p) n -> p c n", p=P)[:, :, bass.ds(t * TILE, TILE)]).then_inc(hTf_in, 16)

    def hTf_wait(eng, t):
        if ln:
            eng.wait_ge(f_emptied, t * NF + NTR)
        else:
            eng.wait_ge(hTf_in, (t + 1) * 16)

    def logits_pe(pe, t):
        hTf_wait(pe, t)
        F_ = front_bank(pe, t, NTR)
        for g in range(GT):
            for c in range(C):
                i = nc.tensor.matmul(F_[:, g * E:(g + 1) * E], hTf[:, c, g * P:(g + 1) * P], gw[:, c, :],
                                     start=(c == 0), stop=(c == C - 1))
        i.then_inc(f_filled, 1)

    def router_dve(dve, t):
        router_chain.begin(t)
        dve.wait_ge(f_filled, t * NF + NTR + 1)
        logits = F[:, 0:GT * E].rearrange("p (g e) -> p g e", e=E)
        wide = [P, GT, E]
        nc.vector.tensor_reduce(out=rmax[:], in_=logits, axis=AX.X, op=ALU.max).then_inc(router_chain.sem, 1)
        dve.wait_ge(router_chain.sem, router_chain.next())
        nc.vector.tensor_tensor(out=shifted[:], in0=logits, in1=rmax[:].unsqueeze(2).broadcast_to(wide),
                                op=ALU.subtract).then_inc(f_emptied, 1)
        dve.wait_ge(e_ready, t + 1)
        nc.vector.tensor_reduce(out=rsum[:], in_=pr[:], axis=AX.X, op=ALU.add).then_inc(router_chain.sem, 1)
        dve.wait_ge(router_chain.sem, router_chain.next())
        nc.vector.reciprocal(rmax[:], rsum[:]).then_inc(router_chain.sem, 1)
        dve.wait_ge(router_chain.sem, router_chain.next())
        nc.vector.tensor_tensor(out=pr[:], in0=pr[:], in1=rmax[:].unsqueeze(2).broadcast_to(wide), op=ALU.mult).then_inc(router_chain.sem, 1)
        dve.wait_ge(router_chain.sem, router_chain.next())
        dve.sem_inc(passed, 1)
        for g in range(GT):
            i = nc.vector.max(m8[:, g, :], pr[:, g, :])
        i.then_inc(router_chain.sem, 1)
        dve.wait_ge(router_chain.sem, router_chain.next())
        nc.vector.tensor_tensor(out=pm[:], in0=pr[:], in1=m8[:, :, top_k - 1:top_k].broadcast_to(wide), op=ALU.is_ge).then_inc(router_chain.sem, 1)
        dve.wait_ge(router_chain.sem, router_chain.next())
        nc.vector.tensor_tensor(out=pm[:], in0=pm[:], in1=pr[:], op=ALU.mult).then_inc(router_chain.sem, 1)
        dve.wait_ge(router_chain.sem, router_chain.next())
        nc.vector.tensor_reduce(out=rsum[:], in_=pm[:], axis=AX.X, op=ALU.add).then_inc(router_chain.sem, 1)
        dve.wait_ge(router_chain.sem, router_chain.next())
        nc.vector.reciprocal(rmax[:], rsum[:]).then_inc(router_chain.sem, 1)
        dve.wait_ge(router_chain.sem, router_chain.next())
        dve.wait_ge(cw_init, 1)
        if some((t - 1) * NF + NF):
            dve.wait_ge(f_filled, (t - 1) * NF + NF)
        nc.vector.tensor_tensor(out=cw[:, :, 0:E], in0=pm[:], in1=rmax[:].unsqueeze(2).broadcast_to(wide),
                                op=ALU.mult).then_inc(cw_done, 1)
        router_chain.end()

    def router_act(act, t):
        act.wait_ge(f_emptied, t * NF + NTR + 1)
        nc.scalar.activation(pr[:], shifted[:], ACT.Exp).then_inc(e_ready, 1)

    def cwT_pe(pe, t):
        pe.wait_ge(cw_done, t + 1)
        F_ = front_bank(pe, t, NF - 1)
        for g in range(GT):
            i = nc.tensor.transpose(F_[0:32, g * P:(g + 1) * P], cw[:, g, :], core.ident[:])
        i.then_inc(f_filled, 1)

    def cwT_act(act, t, par):
        act.wait_ge(f_filled, (t + 1) * NF)
        if some(t):
            act.wait_ge(hT_ready, t)
        if some((t - 1) * NB):
            act.wait_ge(cw_ready, (t - 1) * NB)
        nc.scalar.activation(cwTs[0][:, par, :], F[0:32, :], ACT.Copy)
        nc.scalar.activation(cwTf[:], F[0:32, :], ACT.Copy).then_inc(f_emptied, 1)

    def queries_pe(pe, t):
        hTf_wait(pe, t)
        for h in range(NH):
            F_ = front_bank(pe, t, NTR + h)
            for c in range(C):
                i = nc.tensor.matmul(F_[:], wq[:, c, h * P:(h + 1) * P], hTf[:, c, :], start=(c == 0), stop=(c == C - 1))
            i.then_inc(f_filled, 1)

    def queries_act(act, t):
        for h in range(NH):
            k = NTR + h
            act.wait_ge(f_filled, t * NF + k + 1)
            nc.scalar.activation(qTs[:, h, :], RING[k % R][:], ACT.Copy).then_inc(f_emptied, 1)

    def first_of_group(g):
        order = NTR + NQ
        return order + g * (NS + NW) - (NW if g else 0)

    def first_of_table(g):
        return NTR + NQ + (g + 1) * NS + g * NW + (NS if g < GT - 1 else 0)

    def scores_pe(pe, t, g):
        for n in range(NS):
            k = first_of_group(g) + n
            F_ = front_bank(pe, t, k)
            pe.wait_ge(f_emptied, t * NF + NTR + NQ)
            for h in (2 * n, 2 * n + 1):
                i = nc.tensor.matmul(F_[:, (h % 2) * 256:(h % 2 + 1) * 256], qTs[:, h, g * P:(g + 1) * P], bdk[:, h, :],
                                     start=True, stop=True)
            i.then_inc(f_filled, 1)

    def scores_act(act, t, g):
        if some((t * GT + g) * NH):
            act.wait_ge(sum_ready, (t * GT + g) * NH)
        if some(t * GT + g):
            act.wait_ge(w_ready, t * GT + g)
        for n in range(NS):
            k = first_of_group(g) + n
            act.wait_ge(f_filled, t * NF + k + 1)
            nc.scalar.activation(sims[:, 2 * n:2 * n + 2, :], RING[k % R][:].rearrange("p (h k) -> p h k", h=2),
                                 ACT.Copy).then_inc(f_emptied, 1)

    def pick_dve(dve, t, g):
        dve.wait_ge(f_emptied, t * NF + first_of_group(g) + NS)
        dve.sem_inc(passed, 1)
        for h in range(NH):
            for s in range(2):
                i = nc.vector.max(s8[:, h, s, :], sims[:, h, s * P:(s + 1) * P])
        i.then_inc(peer_chain.sem, 1)
        dve.wait_ge(peer_chain.sem, peer_chain.next())
        dve.sem_inc(passed, 1)
        for h in range(NH):
            nc.vector.max_index(i1[:, h, :], s8[:, h, 0, :], sims[:, h, 0:P])
        nc.vector.tensor_tensor(out=cand[:].rearrange("p h (i j) -> p h i j", j=8),
                                in0=s8[:, :, 0, :].unsqueeze(3).broadcast_to([P, NH, 8, 8]),
                                in1=s8[:, :, 1, :].unsqueeze(2).broadcast_to([P, NH, 8, 8]), op=ALU.add).then_inc(peer_chain.sem, 1)
        dve.wait_ge(peer_chain.sem, peer_chain.next())
        nc.vector.tensor_scalar(past[:], i1[:], float(H // P), None, ALU.is_ge)
        for h in range(NH):
            i = nc.vector.max(f8[:, h, :], cand[:, h, :])
        i.then_inc(peer_chain.sem, 1)
        dve.wait_ge(peer_chain.sem, peer_chain.next())
        nc.vector.tensor_scalar(th[:], f8[:, :, 7], 0.0, None, ALU.max).then_inc(peer_chain.sem, 1)
        dve.wait_ge(peer_chain.sem, peer_chain.next())
        for h in range(NH):
            i = nc.vector.scalar_tensor_tensor(out=wc[:, h, :], in0=cand[:, h, :], scalar=th[:, h:h + 1], in1=cand[:, h, :],
                                               op0=ALU.is_ge, op1=ALU.mult)
        i.then_inc(peer_chain.sem, 1)
        dve.wait_ge(peer_chain.sem, peer_chain.next())
        nc.vector.tensor_tensor(out=wc[:].rearrange("p h (i j) -> p h i j", j=8),
                                in0=wc[:].rearrange("p h (i j) -> p h i j", j=8),
                                in1=past[:].unsqueeze(3).broadcast_to([P, NH, 8, 8]), op=ALU.mult).then_inc(peer_chain.sem, 1)
        dve.wait_ge(peer_chain.sem, peer_chain.next())
        nc.vector.tensor_reduce(out=rest[:], in_=wc[:].rearrange("p h k -> p (h k)"), axis=AX.X, op=ALU.add).then_inc(peer_chain.sem, 1)
        dve.wait_ge(peer_chain.sem, peer_chain.next())

    def sum_pool(pool, t, g, h):
        n = (t * GT + g) * NH + h
        pool.wait_ge(f_emptied, t * NF + first_of_group(g) + NS)
        if some(n + 1 - 2):
            pool.wait_ge(sum_used, n + 1 - 2)
        nc.gpsimd.tensor_tensor(out=sums[:, h % 2, :].rearrange("p (a b) -> p a b", b=P),
                                in0=sims[:, h, P:2 * P].unsqueeze(1).broadcast_to([P, NB, P]),
                                in1=sims[:, h, 0:NB].unsqueeze(2).broadcast_to([P, NB, P]), op=ALU.add).then_inc(sum_ready, 1)

    def table_dve(dve, t, g, h):
        n = (t * GT + g) * NH + h
        dve.wait_ge(sum_ready, n + 1)
        if h == 0:
            if some(t * NF + first_of_table(g - 1) + NW if g else (t - 1) * NF + NF):
                dve.wait_ge(f_filled, t * NF + first_of_table(g - 1) + NW if g else (t - 1) * NF + NF)
        into = wtab if h == 0 else tmp
        nc.vector.scalar_tensor_tensor(out=into[:], in0=sums[:, h % 2, :], scalar=th[:, h:h + 1], in1=sums[:, h % 2, :],
                                       op0=ALU.is_ge, op1=ALU.mult).then_inc(peer_chain.sem, 1)
        dve.wait_ge(peer_chain.sem, peer_chain.next())
        if h:
            nc.vector.tensor_tensor(out=wtab[:], in0=wtab[:], in1=tmp[:], op=ALU.add).then_inc(peer_chain.sem, 1)
            dve.wait_ge(peer_chain.sem, peer_chain.next())
        nc.vector.sem_inc(sum_used, 1)
        if h == NH - 1:
            nc.vector.tensor_tensor(out=wtab[:, H - 1:H], in0=wtab[:, H - 1:H], in1=rest[:], op=ALU.add).then_inc(w_ready, 1)

    def table_pe(pe, t, g):
        pe.wait_ge(w_ready, t * GT + g + 1)
        for n in range(NW):
            F_ = front_bank(pe, t, first_of_table(g) + n)
            for j in range(4):
                blk = 4 * n + j
                i = nc.tensor.transpose(F_[:, j * P:(j + 1) * P], wtab[:, blk * P:(blk + 1) * P], core.ident[:])
            i.then_inc(f_filled, 1)

    def table_act(act, t, par, g):
        for n in range(NW):
            k = first_of_table(g) + n
            act.wait_ge(f_filled, t * NF + k + 1)
            dst = cwT_all[:, par, 4 * n:4 * n + 4, g * P:(g + 1) * P]
            nc.scalar.activation(dst, RING[k % R][:].rearrange("p (b t) -> p b t", t=P), ACT.Copy).then_inc(f_emptied, 1)

    def same_buffer(j):
        return 1 if NB % 2 and j == 0 else 2

    def projected(out, ws, par, j):
        for n, (pw, ph) in enumerate(PARTS):
            for c in range(C):
                i = nc.tensor.matmul(out, ws[pw][:, c, j * P:(j + 1) * P], hTs[ph][:, par, c, :],
                                     start=(n == 0 and c == 0), stop=(n == len(PARTS) - 1 and c == C - 1))
        return i

    def down_pe(pe, t, j):
        pe.wait_ge(lo_ready if split else hh_ready, t * NB + j + 1)
        if j == 0:
            if some(t):
                pe.wait_ge(y_used, t)
        for g in range(GT):
            if split:
                for n, (ph, pw) in enumerate(PARTS):
                    i = nc.tensor.matmul(Y[g // 2][:, (g % 2) * D:(g % 2 + 1) * D], hhs[ph][:, j % 2, g * P:(g + 1) * P],
                                         wds[pw][:, j, :], start=(j == 0 and g % 2 == 0 and n == 0),
                                         stop=(j == NB - 1 and n == len(PARTS) - 1), skip_group_check=True)
            else:
                i = nc.tensor.matmul(Y[g // 2][:, (g % 2) * D:(g % 2 + 1) * D], hh[:, j % 2, g * P:(g + 1) * P], wd[:, j, :],
                                     start=(j == 0 and g % 2 == 0), stop=(j == NB - 1), skip_group_check=True)
        i.then_inc(hh_used, 1)

    def block_pe(pe, t, par, j, before):
        n = t * NB + j + 1
        if j == 0:
            pe.wait_ge(hT_ready, t + 1)
        if some(n - same_buffer(j)):
            pe.wait_ge(hh_ready if relu else a_ready, n - same_buffer(j))
        if split:
            projected(G[j % 2][:], wgs, par, j).then_inc(g_ready, 1)
        else:
            for c in range(C):
                i = nc.tensor.matmul(G[j % 2][:], wg[:, c, j * P:(j + 1) * P], hT[:, c, :], start=(c == 0), stop=(c == C - 1))
            i.then_inc(g_ready, 1)
        if gated:
            if some(n - same_buffer(j)):
                pe.wait_ge(b_ready, n - same_buffer(j))
            projected(U[j % 2][:], wus, par, j).then_inc(u_ready, 1)
            if some(n - 1):
                pe.wait_ge(hh_ready, n - 1)
            for n in range(2):
                i = nc.tensor.matmul(CW[:], sel[:, j * P:(j + 1) * P], cwTs[n][:, par, :], start=(n == 0), stop=(n == 1))
            i.then_inc(cw_ready, 1)
        if before is not None:
            down_pe(pe, *before)

    def block_act(act, t, j):
        n = t * NB + j + 1
        act.wait_ge(g_ready, n)
        if relu:
            if some(n - same_buffer(j)):
                act.wait_ge(hh_used, n - same_buffer(j))
            nc.scalar.activation(hhs[0][:, j % 2, :], G[j % 2][:], ACT.Relu, bias=bup[:, j:j + 1]).then_inc(hi_ready, 1)
            if some(n - same_buffer(j)):
                act.wait_ge(lo_ready, n - same_buffer(j))
            nc.scalar.activation(hh[:, j % 2, :], G[j % 2][:], ACT.Relu, bias=bup[:, j:j + 1]).then_inc(hh_ready, 1)
        else:
            if some(n - same_buffer(j)):
                act.wait_ge(b_ready if gated else hh_ready, n - same_buffer(j))
            nc.scalar.activation(a[:, j % 2, :], G[j % 2][:], ACT.Silu).then_inc(a_ready, 1)
        if gated:
            act.wait_ge(hh_ready, n)
            if some(n - same_buffer(j)):
                act.wait_ge(hh_used, n - same_buffer(j))
            nc.scalar.activation(hhs[0][:, j % 2, :], hh[:, j % 2, :], ACT.Copy).then_inc(hi_ready, 1)

    def block_pool(pool, t, j):
        n = t * NB + j + 1
        pool.wait_ge(hh_ready, n)
        pool.wait_ge(hi_ready, n)
        if some(n - same_buffer(j)):
            pool.wait_ge(hh_used, n - same_buffer(j))
        nc.gpsimd.tensor_tensor(out=hhs[1][:, j % 2, :], in0=hh[:, j % 2, :], in1=hhs[0][:, j % 2, :],
                                op=ALU.subtract).then_inc(lo_ready, 1)

    def block_dve(dve, t, par, j):
        n = t * NB + j + 1
        if peer and j == NB - 1 and not (isinstance(t, int) and t == NT - 1):
            hand_over_dve(dve, t + 1)
        if gated:
            dve.wait_ge(a_ready, n)
            dve.wait_ge(u_ready, n)
            if some(n - same_buffer(j)):
                dve.wait_ge(hh_ready, n - same_buffer(j))
            nc.vector.tensor_tensor(out=b[:, j % 2, :], in0=a[:, j % 2, :], in1=U[j % 2][:], op=ALU.mult).then_inc(b_ready, 1)
            dve.wait_ge(b_ready, n)
            dve.wait_ge(cw_ready, n)
            if some(n - same_buffer(j)):
                dve.wait_ge(lo_ready, n - same_buffer(j))
            nc.vector.tensor_tensor(out=hh[:, j % 2, :], in0=b[:, j % 2, :], in1=CW[:], op=ALU.mult).then_inc(hh_ready, 1)
        if peer:
            if j == 0:
                dve.wait_ge(f_emptied, (t + 1) * NF)
            dve.wait_ge(a_ready, n)
            if some(n - same_buffer(j)):
                dve.wait_ge(hh_used, n - same_buffer(j))
            nc.vector.tensor_tensor(out=hh[:, j % 2, :], in0=a[:, j % 2, :], in1=cwT_all[:, par, j, :], op=ALU.mult).then_inc(hh_ready, 1)

    def hand_over_dve(dve, t):
        hTf_wait(dve, t)
        if some(t * NB):
            dve.wait_ge(g_ready, t * NB)
        nc.vector.tensor_copy(hT[:], hTf[:]).then_inc(hT_ready, 1)

    def low_dve(dve, t, par):
        if not ln:
            dve.wait_ge(hT_hi_ready, t + 1)
        if NF:
            dve.wait_ge(f_emptied, (t + 1) * NF)
        if some((t - 1) * NB):
            dve.wait_ge(g_ready, (t - 1) * NB)
        if gated:
            if some((t - 1) * NB):
                dve.wait_ge(cw_ready, (t - 1) * NB)
            nc.vector.tensor_tensor(out=cwTs[1][:, par, :], in0=cwTf[:], in1=cwTs[0][:, par, :], op=ALU.subtract)
        nc.vector.tensor_tensor(out=hTs[1][:, par, :, :], in0=hTf[:], in1=hTs[0][:, par, :, :],
                                op=ALU.subtract).then_inc(hT_ready, 1)

    def residual_dve(dve, t):
        dve.wait_ge(hh_used, (t + 1) * NB)
        xt = x[:, bass.ds(t * (GT * D), GT * D)]
        half = GT * D // 2
        for n in range(2):
            xt = x[:, bass.ds(t * (GT * D) + n * half, half)]
            i = nc.vector.tensor_tensor(out=xt, in0=Y[n][:], in1=xt, op=ALU.add)
        if relu:
            i.then_inc(y_sum, 1)
            dve.wait_ge(y_sum, t + 1)
            xt = x[:, bass.ds(t * (GT * D), GT * D)].rearrange("p (g d) -> p g d", d=D)
            i = nc.vector.tensor_tensor(out=xt, in0=xt, in1=bdn[:].unsqueeze(1).broadcast_to([P, GT, D]), op=ALU.add)
        i.then_inc(y_used, 1)

    NORM, TRANS, LOGITS, ROUTER, WEIGHTS, LOW = (0, 0, 1, 2, 6, NB) if peer else (0, 3, 4, 5, 8, 9 if gated else 4)

    def front_pe(pe, t, j):
        if ln and j == TRANS:
            transposes_pe(pe, t)
        if gated and j == LOGITS:
            logits_pe(pe, t)
        if gated and j == WEIGHTS:
            cwT_pe(pe, t)
        if peer:
            if j == 1:
                queries_pe(pe, t)
            if j in SIM_SLOT:
                scores_pe(pe, t, SIM_SLOT[j])
            if j in TAB_SLOT:
                table_pe(pe, t, TAB_SLOT[j])

    def front_act(act, t, par, j):
        if j == TRANS:
            if ln:
                transposes_act(act, t, par)
            else:
                loaded_act(act, t, par)
        if gated and j == ROUTER:
            router_act(act, t)
        if gated and j == WEIGHTS:
            cwT_act(act, t, par)
        if peer:
            if j == 1:
                queries_act(act, t)
            if j in SIM_SLOT:
                scores_act(act, t, SIM_SLOT[j])
            if j in TAB_SLOT:
                table_act(act, t, par, TAB_SLOT[j])

    def front_dve(dve, t, par, j):
        if ln and j == NORM:
            norm_dve(dve, t)
        if gated and j == ROUTER:
            router_dve(dve, t)
        if j == LOW:
            low_dve(dve, t, par)
        if peer:
            if j in SIM_SLOT:
                if SIM_SLOT[j] == 0:
                    peer_chain.begin(t)
                pick_dve(dve, t, SIM_SLOT[j])
            for g, h in UNIT_SLOT.get(j, []):
                table_dve(dve, t, g, h)
                if (g, h) == (GT - 1, NH - 1):
                    peer_chain.end()

    def front_pool(pool, t, j):
        if ln and j == 0:
            norm_pool(pool, t)
        if peer:
            for g, h in UNIT_SLOT.get(j, []):
                sum_pool(pool, t, g, h)

    loads = []
    if peer:
        loads = [(wg[:], args["e_downT"].rearrange("(c p) h -> p c h", p=P)), (wd[:], args["e_up"].rearrange("(n p) d -> p n d", p=P)),
                 (wq[:], args["p_wq"].rearrange("(c p) h -> p c h", p=P))]
    if gated:
        loads = [(gw[:], args[name[:4] + "_gate"].rearrange("(c p) e -> p c e", p=P))]
        parts = []
        for w, src in ((wgs, args[name[:4] + "_wg"]), (wus, args[name[:4] + "_wu"])):
            for c in range(C):
                for h in range(0, H, 1024):
                    k = min(h + 1024, H)
                    parts.append((src[c * P:(c + 1) * P, first * P + h:first * P + k], P, w[0][:, c, h:k], w[1][:, c, h:k]))
        for n in range(0, NB, 4):
            k = min(n + 4, NB)
            parts.append((args[name[:4] + "_wd"][(first + n) * P:(first + k) * P, :].rearrange("(n p) d -> p n d", p=P), P,
                          wds[0][:, n:k, :], wds[1][:, n:k, :]))
        for h in range(0, H, 1024):
            k = min(h + 1024, H)
            parts.append((args[name[:4] + "_sel"][:, first * P + h:first * P + k], 32, sel[:, h:k], None))
        split_weights_block(core, name, parts)

    with nc.Block() as block:
        @block.sync
        def _(sp):
            for out, in_ in loads:
                sp.dma_start(out, in_).then_inc(weights_in, 16)
            if peer:
                sp.wait_ge(bdk_zero, 1)
                for s in range(2):
                    sp.dma_start(bdk[64 * s:64 * s + 64, :, P * s:P * (s + 1)],
                                 args["p_keys"][64 * s:64 * s + 64, :, :]).then_inc(weights_in, 16)
            if not ln:
                load_front_sp(sp, 0)
                with sp.Fori(1, NT) as t:
                    load_front_sp(sp, t)

        n_in = 16 * (len(loads) + (2 if peer else 0))

        def all_tiles(eng, tile):
            tile(0, 0)
            with eng.Fori(0, (NT - 2) // 2) as pair:
                tile(pair * 2 + 1, 1)
                tile(pair * 2 + 2, 0)
            tile(NT - 1, 1)

        @block.tensor
        def _(pe):
            if n_in:
                pe.wait_ge(weights_in, n_in)
            for j in range(NB):
                front_pe(pe, 0, j)

            def tile(t, par):
                for j in range(NB):
                    block_pe(pe, t, par, j, (t, j - 1) if j else None if is_first(t) else (t - 1, NB - 1))
                    if not is_last_tile(t):
                        front_pe(pe, t + 1, j)

            all_tiles(pe, tile)
            down_pe(pe, NT - 1, NB - 1)

        @block.scalar
        def _(act):
            for j in range(NB):
                front_act(act, 0, 0, j)

            def tile(t, par):
                for j in range(NB):
                    block_act(act, t, j)
                    if not is_last_tile(t):
                        front_act(act, t + 1, 1 - par, j)

            all_tiles(act, tile)

        @block.vector
        def _(dve):
            for j in range(NB):
                front_dve(dve, 0, 0, j)
            if peer:
                hand_over_dve(dve, 0)

            def tile(t, par):
                for j in range(NB):
                    block_dve(dve, t, par, j)
                    if j == 0 and not is_first(t):
                        residual_dve(dve, t - 1)
                    if not is_last_tile(t):
                        front_dve(dve, t + 1, 1 - par, j)

            all_tiles(dve, tile)
            residual_dve(dve, NT - 1)

        @block.gpsimd
        def _(pool):
            if peer:
                nc.gpsimd.memset(bdk[:], 0.0).then_inc(bdk_zero, 1)
            if gated:
                nc.gpsimd.memset(cw[:], 0.0).then_inc(cw_zeroed, 1)
                pool.wait_ge(cw_zeroed, 1)
                nc.gpsimd.memset(cw[:, :, E:E + 1], 1.0).then_inc(cw_init, 1)
            for j in range(NB):
                front_pool(pool, 0, j)

            def tile(t, par):
                for j in range(NB):
                    if split:
                        block_pool(pool, t, j)
                    if not is_last_tile(t):
                        front_pool(pool, t + 1, j)

            all_tiles(pool, tile)
    st.close()


def self_attention_stage(core):
    nc, args, bank, x = core.nc, core.args, core.bank, core.x
    st = Stage(core, "mha")
    sb, sem = st.sb, st.sem
    NH, HD = 16, 128
    SCALE = float(HD) ** -0.5
    EPS = 1e-6
    QUAD = 4

    wq, wk, wv = sb("wq", [P, C, NH * HD]), sb("wk", [P, C, NH * HD]), sb("wv", [P, C, NH * HD])
    wo = sb("wo", [P, NH, D])
    ln1, ln2, causal = sb("ln1", [P, C]), sb("ln2", [P, C]), sb("causal", [P, P])
    hT, hTf = sb("hT", [P, C, TILE]), sb("hTf", [P, C, TILE])
    xr = sb("xr", [P, GT, D])
    stats, mv, mvb = sb("stats", [P, GT, 6]), sb("mv", [P, GT, 2]), sb("mvb", [P, GT, 2])
    ve, rstd, rstdb, ms, r1, rr = (sb(n, [P, GT]) for n in ("ve", "rstd", "rstdb", "ms", "r1", "rr"))
    qs, ks = sb("qs", [P, 2, TILE]), sb("ks", [P, 2, TILE])
    vs = sb("vs", [P, 2, GT, QUAD * HD])
    pr = sb("pr", [P, 2, GT, P])
    pT, oT = sb("pT", [P, 2, TILE]), sb("oT", [P, 2, TILE])
    smax, ssum = sb("smax", [P, GT]), sb("ssum", [P, GT])
    x1 = sb("x1", [P, GT, D])
    stats2, mv2 = sb("stats2", [P, GT, 6]), sb("mv2", [P, GT, 2])
    ms2, r2 = sb("ms2", [P, GT]), sb("r2", [P, GT])
    tT = sb("tT", [P, C, TILE])
    Q, K, V, Sc, PT, O, Y = bank[0], bank[1], bank[2], bank[3], bank[4], bank[5], bank[6:8]

    weights_in, passed = sem("weights_in"), st.passed()
    var_ready, rstd_ready, ms_ready, r1_ready, xr_ready = (sem(n) for n in ("var_ready", "rstd_ready", "ms_ready", "r1_ready", "xr_ready"))
    v_filled, v_emptied = sem("v_filled"), sem("v_emptied")
    hT_ready = sem("hT_ready")
    q_ready, k_ready, qs_ready, ks_ready = sem("q_ready"), sem("k_ready"), sem("qs_ready"), sem("ks_ready")
    s_ready, s_read, e_ready, p_ready = sem("s_ready"), sem("s_read"), sem("e_ready"), sem("p_ready")
    pT_ready, pTs_ready, o_ready, oT_ready, out_done = (sem(n) for n in ("pT_ready", "pTs_ready", "o_ready", "oT_ready", "out_done"))
    shifted = sem("shifted")
    y_used, ms2_ready, r2_ready, tn_ready, stored = (sem(n) for n in ("y_used", "ms2_ready", "r2_ready", "tn_ready", "stored"))
    norm_chain, soft_chain, tail_chain = Chain(sem("norm_chain"), 3), Chain(sem("soft_chain"), NH * 4), Chain(sem("tail_chain"), 6)

    ms_eps, r1_raw = sem("ms_eps"), sem("r1_raw")
    f_filled, f_emptied = sem("f_filled"), sem("f_emptied")
    t_filled, t_emptied = sem("t_filled"), sem("t_emptied")

    def group_x(t, g):
        return x[:, bass.ds(t * (GT * D) + g * D, D)]

    def front_dve(dve, t):
        norm_chain.begin(t)
        for g in range(GT):
            i = nc.vector.bn_stats(stats[:, g, :], group_x(t, g))
        i.then_inc(norm_chain.sem, 1)
        dve.wait_ge(norm_chain.sem, norm_chain.next())
        dve.sem_inc(passed, 1)
        for g in range(GT):
            i = nc.vector.bn_aggr(mv[:, g, :], stats[:, g, :])
        i.then_inc(norm_chain.sem, 1)
        dve.wait_ge(norm_chain.sem, norm_chain.next())
        nc.vector.tensor_scalar(ve[:], mv[:, :, 1], LN_EPS, None, ALU.add).then_inc(var_ready, 1)
        dve.wait_ge(rstd_ready, t + 1)
        nc.vector.tensor_tensor(out=ms[:], in0=rstd[:], in1=rstd[:], op=ALU.mult).then_inc(norm_chain.sem, 1)
        dve.wait_ge(norm_chain.sem, norm_chain.next())
        nc.vector.tensor_tensor(out=ms[:], in0=ms[:], in1=mv[:, :, 1], op=ALU.mult).then_inc(ms_ready, 1)
        dve.wait_ge(r1_ready, t + 1)
        if some(t * C):
            dve.wait_ge(f_filled, t * C)
        for g in range(GT):
            i = nc.vector.tensor_scalar(xr[:, g, :], group_x(t, g), mv[:, g, 0:1], rr[:, g:g + 1], ALU.subtract, ALU.mult)
        i.then_inc(xr_ready, 1)
        norm_chain.end()

    def front_pool(pool, t):
        pool.wait_ge(var_ready, t + 1)
        nc.gpsimd.tensor_tensor(out=rstd[:], in0=ve[:], in1=core.neghalf[:, 0:GT], op=ALU.pow).then_inc(rstd_ready, 1)
        pool.wait_ge(ms_ready, t + 1)
        pool.sem_inc(passed, 1)
        nc.gpsimd.tensor_scalar(ms[:], ms[:], EPS, None, ALU.add).then_inc(ms_eps, 1)
        pool.wait_ge(ms_eps, t + 1)
        nc.gpsimd.tensor_tensor(out=r1[:], in0=ms[:], in1=core.neghalf[:, 0:GT], op=ALU.pow).then_inc(r1_raw, 1)
        pool.wait_ge(r1_raw, t + 1)
        nc.gpsimd.tensor_tensor(out=rr[:], in0=r1[:], in1=rstd[:], op=ALU.mult).then_inc(r1_ready, 1)

    def front_pe(pe, t):
        pe.wait_ge(xr_ready, t + 1)
        if some((t - 1) * NH + 12):
            pe.wait_ge(v_emptied, (t - 1) * NH + 12)
        for c in range(C):
            if some(t * C + c):
                pe.wait_ge(f_emptied, t * C + c)
            for g in range(GT):
                i = nc.tensor.transpose(V[:, g * P:(g + 1) * P], xr[:, g, c * P:(c + 1) * P], core.ident[:])
            i.then_inc(f_filled, 1)

    def front_act(act, t):
        if some(t):
            act.wait_ge(hT_ready, t)
        for c in range(C):
            act.wait_ge(f_filled, t * C + c + 1)
            nc.scalar.activation(hTf[:, c, :], V[:], ACT.Copy, scale=ln1[:, c:c + 1]).then_inc(f_emptied, 1)

    def hand_over_dve(dve, t):
        dve.wait_ge(f_emptied, (t + 1) * C)
        if some(t * NH):
            dve.wait_ge(v_filled, t * NH)
        if some(t * NH):
            dve.wait_ge(k_ready, t * NH)
        nc.vector.tensor_copy(hT[:], hTf[:]).then_inc(hT_ready, 1)

    def keep_stats_dve(dve, t):
        nc.vector.tensor_copy(mvb[:], mv[:])
        nc.vector.tensor_copy(rstdb[:], rstd[:]).then_inc(mvb_ready, 1)

    mvb_ready = sem("mvb_ready")

    def project_pe(pe, t, s):
        n = t * NH + s
        if s == 0:
            pe.wait_ge(hT_ready, t + 1)
        for w, out, ready, copied in ((wq, Q, q_ready, qs_ready), (wk, K, k_ready, ks_ready)):
            if some(n):
                pe.wait_ge(copied, n)
            for c in range(C):
                i = nc.tensor.matmul(out[:], w[:, c, s * HD:(s + 1) * HD], hT[:, c, :], start=(c == 0), stop=(c == C - 1))
            i.then_inc(ready, 1)
        if s % QUAD == 0:
            if s == 8:
                if some(t * C):
                    pe.wait_ge(t_emptied, t * C)
            if s == 12 and not (isinstance(t, int) and t == NT - 1):
                pe.wait_ge(f_emptied, (t + 2) * C)
            for g in range(GT):
                if some(n + g):
                    pe.wait_ge(v_emptied, n + g)
                for c in range(C):
                    i = nc.tensor.matmul(V[:], hT[:, c, g * P:(g + 1) * P], wv[:, c, s * HD:(s + QUAD) * HD],
                                         start=(c == 0), stop=(c == C - 1))
                i.then_inc(v_filled, 1)

    def project_act(act, t, s):
        n = t * NH + s
        act.wait_ge(q_ready, n + 1)
        if some(n - 1):
            act.wait_ge(s_ready, n - 1)
        nc.scalar.activation(qs[:, s % 2, :], Q[:], ACT.Copy).then_inc(qs_ready, 1)
        if s % QUAD == 0:
            if some(n - QUAD):
                act.wait_ge(o_ready, n - QUAD)
            for g in range(GT):
                act.wait_ge(v_filled, n + g + 1)
                nc.scalar.activation(vs[:, (s // QUAD) % 2, g, :], V[:], ACT.Copy).then_inc(v_emptied, 1)

    def project_dve(dve, t, s):
        n = t * NH + s
        dve.wait_ge(k_ready, n + 1)
        if some(n - 1):
            dve.wait_ge(s_ready, n - 1)
        nc.vector.tensor_copy(ks[:, s % 2, :], K[:]).then_inc(ks_ready, 1)

    def scores_pe(pe, t, s):
        n = t * NH + s
        pe.wait_ge(qs_ready, n + 1)
        pe.wait_ge(ks_ready, n + 1)
        if some(n):
            pe.wait_ge(s_read, n)
        for g in range(GT):
            i = nc.tensor.matmul(Sc[:, g * P:(g + 1) * P], qs[:, s % 2, g * P:(g + 1) * P], ks[:, s % 2, g * P:(g + 1) * P],
                                 start=True, stop=True)
        i.then_inc(s_ready, 1)

    def softmax_dve(dve, t, s):
        n, wide, p_ = t * NH + s, [P, GT, P], pr[:, s % 2, :, :]
        soft_chain.begin(t, 4 * s)
        dve.wait_ge(s_ready, n + 1)
        if some(n - 1):
            dve.wait_ge(pT_ready, n - 1)
        i = nc.vector.scalar_tensor_tensor(out=p_, in0=Sc[:].rearrange("p (g k) -> p g k", k=P), scalar=SCALE,
                                           in1=causal[:].unsqueeze(1).broadcast_to(wide), op0=ALU.mult, op1=ALU.add)
        i.then_inc(s_read, 1)
        dve.wait_ge(s_read, n + 1)
        nc.vector.tensor_reduce(out=smax[:], in_=p_, axis=AX.X, op=ALU.max).then_inc(soft_chain.sem, 1)
        dve.wait_ge(soft_chain.sem, soft_chain.next())
        nc.vector.tensor_tensor(out=p_, in0=p_, in1=smax[:].unsqueeze(2).broadcast_to(wide),
                                op=ALU.subtract).then_inc(shifted, 1)

    def exp_act(act, t, s):
        n, p_ = t * NH + s, pr[:, s % 2, :, :]
        act.wait_ge(shifted, n + 1)
        nc.scalar.activation(p_, p_, ACT.Exp).then_inc(e_ready, 1)

    def normalize_dve(dve, t, s):
        n, wide, p_ = t * NH + s, [P, GT, P], pr[:, s % 2, :, :]
        dve.wait_ge(e_ready, n + 1)
        nc.vector.tensor_reduce(out=ssum[:], in_=p_, axis=AX.X, op=ALU.add).then_inc(soft_chain.sem, 1)
        dve.wait_ge(soft_chain.sem, soft_chain.next())
        nc.vector.reciprocal(ssum[:], ssum[:]).then_inc(soft_chain.sem, 1)
        dve.wait_ge(soft_chain.sem, soft_chain.next())
        nc.vector.tensor_tensor(out=p_, in0=p_, in1=ssum[:].unsqueeze(2).broadcast_to(wide), op=ALU.mult).then_inc(soft_chain.sem, 1)
        dve.wait_ge(soft_chain.sem, soft_chain.next())
        dve.sem_inc(p_ready, 1)
        if s == NH - 1:
            soft_chain.end()

    def transpose_pe(pe, t, s):
        n = t * NH + s
        pe.wait_ge(p_ready, n + 1)
        if some(n):
            pe.wait_ge(pTs_ready, n)
        for g in range(GT):
            i = nc.tensor.transpose(PT[:, g * P:(g + 1) * P], pr[:, s % 2, g, :], core.ident[:])
        i.then_inc(pT_ready, 1)

    def transposed_act(act, t, s):
        n = t * NH + s
        act.wait_ge(pT_ready, n + 1)
        if some(n - 1):
            act.wait_ge(o_ready, n - 1)
        nc.scalar.activation(pT[:, s % 2, :], PT[:], ACT.Copy).then_inc(pTs_ready, 1)

    def apply_pe(pe, t, s):
        n = t * NH + s
        pe.wait_ge(pTs_ready, n + 1)
        if s % QUAD == 0:
            pe.wait_ge(v_emptied, t * NH + s + QUAD)
        if some(n):
            pe.wait_ge(oT_ready, n)
        h = s % QUAD
        for g in range(GT):
            i = nc.tensor.matmul(O[:, g * P:(g + 1) * P], vs[:, (s // QUAD) % 2, g, h * HD:(h + 1) * HD],
                                 pT[:, s % 2, g * P:(g + 1) * P], start=True, stop=True)
        i.then_inc(o_ready, 1)

    def applied_act(act, t, s):
        n = t * NH + s
        act.wait_ge(o_ready, n + 1)
        if some(n - 1):
            act.wait_ge(out_done, n - 1)
        nc.scalar.activation(oT[:, s % 2, :], O[:], ACT.Copy).then_inc(oT_ready, 1)

    def out_pe(pe, t, s):
        n = t * NH + s
        pe.wait_ge(oT_ready, n + 1)
        if s == 0:
            if some(t):
                pe.wait_ge(y_used, t)
        for g in range(GT):
            i = nc.tensor.matmul(Y[g // 2][:, (g % 2) * D:(g % 2 + 1) * D], oT[:, s % 2, g * P:(g + 1) * P], wo[:, s, :],
                                 start=(s == 0 and g % 2 == 0), stop=(s == NH - 1), skip_group_check=True)
        i.then_inc(out_done, 1)

    def tail_dve(dve, t):
        tail_chain.begin(t)
        dve.wait_ge(out_done, (t + 1) * NH)
        dve.wait_ge(t_filled, t * C)
        dve.wait_ge(mvb_ready, t + 1)
        for g in range(GT):
            i = nc.vector.tensor_scalar(x1[:, g, :], group_x(t, g), mvb[:, g, 0:1], rstdb[:, g:g + 1], ALU.subtract, ALU.mult)
        i.then_inc(tail_chain.sem, 1)
        dve.wait_ge(tail_chain.sem, tail_chain.next())
        for n in range(2):
            half = x1[:, 2 * n:2 * n + 2, :].rearrange("p g d -> p (g d)")
            i = nc.vector.tensor_tensor(out=half, in0=Y[n][:], in1=half, op=ALU.add)
        i.then_inc(tail_chain.sem, 1)
        dve.wait_ge(tail_chain.sem, tail_chain.next())
        dve.sem_inc(y_used, 1)
        xt = x[:, bass.ds(t * (GT * D), GT * D)]
        nc.vector.tensor_tensor(out=xt, in0=xt, in1=x1[:].rearrange("p g d -> p (g d)"), op=ALU.add)
        for g in range(GT):
            i = nc.vector.bn_stats(stats2[:, g, :], x1[:, g, :])
        i.then_inc(tail_chain.sem, 1)
        dve.wait_ge(tail_chain.sem, tail_chain.next())
        dve.sem_inc(passed, 1)
        for g in range(GT):
            i = nc.vector.bn_aggr(mv2[:, g, :], stats2[:, g, :])
        i.then_inc(tail_chain.sem, 1)
        dve.wait_ge(tail_chain.sem, tail_chain.next())
        nc.vector.tensor_tensor(out=ms2[:], in0=mv2[:, :, 0], in1=mv2[:, :, 0], op=ALU.mult).then_inc(tail_chain.sem, 1)
        dve.wait_ge(tail_chain.sem, tail_chain.next())
        nc.vector.tensor_tensor(out=ms2[:], in0=ms2[:], in1=mv2[:, :, 1], op=ALU.add).then_inc(tail_chain.sem, 1)
        dve.wait_ge(tail_chain.sem, tail_chain.next())
        nc.vector.tensor_scalar(ms2[:], ms2[:], EPS, None, ALU.add).then_inc(ms2_ready, 1)
        dve.wait_ge(r2_ready, t + 1)
        for g in range(GT):
            i = nc.vector.tensor_scalar(x1[:, g, :], x1[:, g, :], r2[:, g:g + 1], None, ALU.mult)
        i.then_inc(tn_ready, 1)
        tail_chain.end()
        if not (isinstance(t, int) and t == NT - 1):
            keep_stats_dve(dve, t + 1)

    def tail_pool(pool, t):
        pool.wait_ge(ms2_ready, t + 1)
        nc.gpsimd.tensor_tensor(out=r2[:], in0=ms2[:], in1=core.neghalf[:, 0:GT], op=ALU.pow).then_inc(r2_ready, 1)

    def tail_pe(pe, t):
        pe.wait_ge(tn_ready, t + 1)
        pe.wait_ge(v_emptied, (t + 1) * NH + 8 if not (isinstance(t, int) and t == NT - 1) else NT * NH)
        for c in range(C):
            pe.wait_ge(t_emptied, t * C + c)
            for g in range(GT):
                i = nc.tensor.transpose(V[:, g * P:(g + 1) * P], x1[:, g, c * P:(c + 1) * P], core.ident[:])
            i.then_inc(t_filled, 1)

    def tail_act(act, t):
        act.wait_ge(stored, 16 * t)
        for c in range(C):
            act.wait_ge(t_filled, t * C + c + 1)
            nc.scalar.activation(tT[:, c, :], V[:], ACT.Copy, scale=ln2[:, c:c + 1]).then_inc(t_emptied, 1)

    def tail_sp(sp, t):
        sp.wait_ge(t_emptied, (t + 1) * C)
        sp.dma_start(args["t_scratch"].rearrange("(c p) n -> p c n", p=P)[:, :, bass.ds(t * TILE, TILE)], tT[:]).then_inc(stored, 16)

    def prev(t, s, l):
        if s >= l:
            return t, s - l
        if isinstance(t, int) and t == 0:
            return None
        return t - 1, NH + s - l

    def after(t, s, l, f, eng):
        p = prev(t, s, l)
        if p is not None:
            f(eng, *p)

    def step_pe(pe, t, s):
        project_pe(pe, t, s)
        after(t, s, 1, scores_pe, pe)
        after(t, s, 2, transpose_pe, pe)
        after(t, s, 3, apply_pe, pe)
        after(t, s, 4, out_pe, pe)

    def step_act(act, t, s):
        project_act(act, t, s)
        after(t, s, 2, transposed_act, act)
        after(t, s, 1, exp_act, act)
        after(t, s, 3, applied_act, act)

    def step_dve(dve, t, s):
        project_dve(dve, t, s)
        after(t, s, 1, softmax_dve, dve)
        after(t, s, 1, normalize_dve, dve)

    loads = [(w[:], args[n].rearrange("(c p) h -> p c h", p=P)) for w, n in ((wq, "a_wq"), (wk, "a_wk"), (wv, "a_wv"))]
    loads += [(wo[:], args["a_wo"].rearrange("(n p) d -> p n d", p=P)), (ln1[:], args["ln1"]), (ln2[:], args["ln2"]),
              (causal[:], args["causal"])]
    n_in = 16 * len(loads)
    TAIL_DVE, TAIL, FRONT = 3, 5, 9

    def tiles(eng, step, front, tail, hand_over=None):
        def tile(t):
            for s in range(NH):
                if hand_over is not None and s == NH - 1 and not (isinstance(t, int) and t == NT - 1):
                    step(eng, t, s)
                    hand_over(eng, t + 1)
                else:
                    step(eng, t, s)
                if s == (TAIL_DVE if hand_over is not None else TAIL) and not (isinstance(t, int) and t == 0):
                    tail(eng, t - 1)
                if s == FRONT and not (isinstance(t, int) and t == NT - 1):
                    front(eng, t + 1)
        tile(0)
        with eng.Fori(1, NT - 1) as t:
            tile(t)
        tile(NT - 1)

    with nc.Block() as block:
        @block.sync
        def _(sp):
            for out, in_ in loads:
                sp.dma_start(out, in_).then_inc(weights_in, 16)
            tail_sp(sp, 0)
            with sp.Fori(1, NT) as t:
                tail_sp(sp, t)
            sp.wait_ge(stored, 16 * NT)

        @block.tensor
        def _(pe):
            pe.wait_ge(weights_in, n_in)
            front_pe(pe, 0)
            tiles(pe, step_pe, front_pe, tail_pe)
            scores_pe(pe, NT - 1, NH - 1)
            for l in (2, 1):
                transpose_pe(pe, NT - 1, NH - l)
            for l in (3, 2, 1):
                apply_pe(pe, NT - 1, NH - l)
                out_pe(pe, NT - 1, NH - l - 1)
            out_pe(pe, NT - 1, NH - 1)
            tail_pe(pe, NT - 1)

        @block.scalar
        def _(act):
            act.wait_ge(weights_in, n_in)
            front_act(act, 0)
            tiles(act, step_act, front_act, tail_act)
            transposed_act(act, NT - 1, NH - 2)
            exp_act(act, NT - 1, NH - 1)
            applied_act(act, NT - 1, NH - 3)
            transposed_act(act, NT - 1, NH - 1)
            applied_act(act, NT - 1, NH - 2)
            applied_act(act, NT - 1, NH - 1)
            tail_act(act, NT - 1)

        @block.vector
        def _(dve):
            dve.wait_ge(weights_in, n_in)
            front_dve(dve, 0)
            hand_over_dve(dve, 0)
            keep_stats_dve(dve, 0)
            tiles(dve, step_dve, front_dve, tail_dve, hand_over=hand_over_dve)
            softmax_dve(dve, NT - 1, NH - 1)
            normalize_dve(dve, NT - 1, NH - 1)
            tail_dve(dve, NT - 1)

        @block.gpsimd
        def _(pool):
            front_pool(pool, 0)
            front_pool(pool, 1)
            with pool.Fori(1, NT - 1) as t:
                tail_pool(pool, t - 1)
                front_pool(pool, t + 1)
            tail_pool(pool, NT - 2)
            tail_pool(pool, NT - 1)
    st.close()


UNIT = 256
NU = T // UNIT
GU = UNIT // P


def unit_loop(eng, work):
    work(eng, 0, 0)
    with eng.Fori(0, NU // 2 - 1) as pair:
        work(eng, pair * 2 + 1, 1)
        work(eng, pair * 2 + 2, 0)
    work(eng, NU - 1, 1)


def is_last(t):
    return isinstance(t, int) and t == NU - 1


def quantize_weights_block(core, name, srcs):
    nc, bank = core.nc, core.bank
    st = Stage(core, name)
    sb, sem = st.sb, st.sem
    n_w = len(srcs)
    w, wr, qw = sb("w", [P, n_w * C, D]), sb("wr", [P, n_w * C, D]), sb("qw", [P, n_w * C, D], BF16)
    sw, rs = sb("sw", [P, n_w * C]), sb("rs", [P, n_w * C])
    diag, ones = sb("diag", [P, n_w * C, P]), sb("ones", [P, P])
    w_in, q_done, one_done, tr, tr_out, bc = (sem(n) for n in ("w_in", "q_done", "one_done", "tr", "tr_out", "bc"))
    chain = Chain(sem("chain"), 6)
    with nc.Block() as block:
        @block.sync
        def _(sp):
            for n, (src, _, _) in enumerate(srcs):
                sp.dma_start(w[:, n * C:(n + 1) * C, :], src.rearrange("(c p) i -> p c i", p=P)).then_inc(w_in, 16)

        @block.gpsimd
        def _(pool):
            nc.gpsimd.memset(ones[:], 1.0).then_inc(one_done, 1)

        @block.vector
        def _(dve):
            chain.begin(0)
            dve.wait_ge(w_in, 16 * n_w)
            nc.vector.tensor_reduce(out=sw[:], in_=w[:], axis=AX.X, op=ALU.max, apply_absolute_value=True).then_inc(chain.sem, 1)
            dve.wait_ge(chain.sem, chain.next())
            nc.vector.tensor_scalar(sw[:], sw[:], 1.0 / 127.0, 1e-8, ALU.mult, ALU.max).then_inc(chain.sem, 1)
            dve.wait_ge(chain.sem, chain.next())
            nc.vector.reciprocal(rs[:], sw[:]).then_inc(chain.sem, 1)
            dve.wait_ge(chain.sem, chain.next())
            for m in range(n_w * C):
                i = nc.vector.tensor_scalar(wr[:, m, :], w[:, m, :], rs[:, m:m + 1], MAGIC, ALU.mult, ALU.add)
            i.then_inc(chain.sem, 1)
            dve.wait_ge(chain.sem, chain.next())
            nc.vector.tensor_scalar(qw[:], wr[:], MAGIC, None, ALU.subtract).then_inc(chain.sem, 1)
            dve.wait_ge(chain.sem, chain.next())
            for m in range(n_w * C):
                i = nc.vector.tensor_scalar(diag[:, m, :], core.ident[:], sw[:, m:m + 1], None, ALU.mult)
            i.then_inc(chain.sem, 1)
            dve.wait_ge(chain.sem, chain.next())
            chain.end()
            dve.sem_inc(q_done, 1)
            for n, (_, qT, scale) in enumerate(srcs):
                dve.wait_ge(tr, n + 1)
                nc.vector.tensor_copy(qT[:].rearrange("p c o -> p (c o)"), bank[n][:].bitcast(BF16)[:, 0:C * D])
                nc.vector.tensor_copy(scale[:], bank[2 + n][:, 0:D]).then_inc(tr_out, 1)

        @block.tensor
        def _(pe):
            pe.wait_ge(q_done, 1)
            pe.wait_ge(one_done, 1)
            for n in range(n_w):
                for ci in range(C):
                    for co in range(C):
                        nc.tensor.transpose(bank[n][:].bitcast(BF16)[:, ci * D + co * P:ci * D + (co + 1) * P],
                                            qw[:, n * C + co, ci * P:(ci + 1) * P], core.identb[:])
                for co in range(C):
                    i = nc.tensor.matmul(bank[2 + n][:, co * P:(co + 1) * P], ones[:], diag[:, n * C + co, :], start=True, stop=True)
                i.then_inc(tr, 1)
    st.close()


def head_attention_stage(core, name, quant):
    nc, args, bank, x = core.nc, core.args, core.bank, core.x
    st = Stage(core, name)
    sb, sem = st.sb, st.sem
    NH, HD, BU = 16, 16, UNIT // S
    H8 = NH // C
    wdt = BF16 if quant else FP32

    wqT, woT = sb("wqT", [P, C, D], wdt), sb("woT", [P, C, D], wdt)
    wkT, wvT = sb("wkT", [P, C, D]), sb("wvT", [P, C, D])
    hmask = sb("hmask", [P, H8])
    ctxT = [sb(f"ctxT{i}", [P, C, BU, 2, S]) for i in range(2)]
    xn = sb("xn", [P, GU, D])
    stats, mv = sb("stats", [P, GU, 6]), sb("mv", [P, GU, 2])
    ve, rstd = sb("ve", [P, GU]), sb("rstd", [P, GU])
    hT = sb("hT", [P, C, UNIT], wdt)
    qT = [sb(f"qT{i}", [P, C, UNIT]) for i in range(2)]
    kT = sb("kT", [P, C, UNIT])
    km = sb("km", [P, C, BU, H8, S])
    vbd = [sb(f"vbd{i}", [P, BU, NH // 2, 2, HD]) for i in range(2)]
    pr = [sb(f"pr{g}", [P, NH, S]) for g in range(GU)]
    pT = sb("pT", [P, NH // 2, P])
    smax, rsum = sb("smax", [P, GU, NH]), sb("rsum", [P, GU, NH])
    o = sb("o", [P, D])
    oT = sb("oT", [P, C, P], wdt)
    y = sb("y", [P, D])

    weights_in, passed = sem("weights_in"), st.passed()
    ctx_in = [sem(f"ctx_in{i}") for i in range(2)]
    zeroed = sem("zeroed")
    var_ready, rstd_ready, xn_ready = sem("var_ready"), sem("rstd_ready"), sem("xn_ready")
    filled = [sem(f"filled{i}") for i in range(2)]
    emptied = [sem(f"emptied{i}") for i in range(2)]
    km_ready, scored, s_read, shifted, e_ready = (sem(n) for n in ("km_ready", "scored", "s_read", "shifted", "e_ready"))
    sums_ready, pT_ready, pTs_ready, o_ready, o_read = (sem(n) for n in ("sums_ready", "pT_ready", "pTs_ready", "o_ready", "o_read"))
    on_ready, oT_filled, oT_ready, y_ready, y_used = (sem(n) for n in ("on_ready", "oT_filled", "oT_ready", "y_ready", "y_used"))
    soft_chain = Chain(sem("soft_chain"), GU * 4)
    out_chain = Chain(sem("out_chain"), GU * (6 if quant else 1))
    if quant:
        swq, swo = sb("swq", [P, D]), sb("swo", [P, D])
        bq, bk, bv, bo = sb("bq", [P, D]), sb("bk", [P, C]), sb("bv", [P, D]), sb("bo", [P, D])
        sx, rsx = sb("sx", [P, GU]), sb("rsx", [P, GU])
        sxu = sb("sxu", [P, GU])
        qx, qf = sb("qx", [P, GU, D], BF16), sb("qf", [P, GU, D])
        so, rso, oq = sb("so", [P, 1]), sb("rso", [P, 1]), sb("oq", [P, D], BF16)
        mask = [sb(f"mask{i}", [P, GU, S]) for i in range(2)]
        qf_ready = sem("qf_ready")
        norm_chain = Chain(sem("norm_chain"), 7)
        q_chain = Chain(sem("q_chain"), 1)
        quantize_weights_block(core, name + "_qw", [(args["wq"], wqT, swq), (args["wo"], woT, swo)])
    else:
        wgT, norm_w = sb("wgT", [P, C, D]), sb("norm_w", [P, C])
        ms, r1, rr = sb("ms", [P, GU]), sb("r1", [P, GU]), sb("rr", [P, GU])
        gate = [sb(f"gate{i}", [P, GU, D]) for i in range(2)]
        keep = sb("keep", [P, NG, S], U8)
        neg, valid = sb("neg", [P, GU, S]), sb("valid", [P, GU])
        ms_ready, ms_eps, r1_raw, rr_ready = sem("ms_ready"), sem("ms_eps"), sem("r1_raw"), sem("rr_ready")
        norm_chain = Chain(sem("norm_chain"), 3)
        m_chain = Chain(sem("m_chain"), 1)
    KEYS, INPUT, QUERIES, V0, V1, LAST = range(6)
    SB = [bank[0:2], bank[2:4]]
    OB = [bank[4], bank[5]]
    FB = [bank[6], bank[7]]

    def fwait_filled(eng, t, k):
        eng.wait_ge(filled[k % 2], t * 3 + k // 2 + 1)

    def fbank(pe, t, k):
        if some(t * 3 + k // 2):
            pe.wait_ge(emptied[k % 2], t * 3 + k // 2)
        return FB[k % 2]

    def group_x(t, g):
        return x[:, bass.ds(t * (GU * D) + g * D, D)]

    def norm_dve(dve, t):
        norm_chain.begin(t)
        for g in range(GU):
            i = nc.vector.bn_stats(stats[:, g, :], group_x(t, g))
        i.then_inc(norm_chain.sem, 1)
        dve.wait_ge(norm_chain.sem, norm_chain.next())
        dve.sem_inc(passed, 1)
        for g in range(GU):
            i = nc.vector.bn_aggr(mv[:, g, :], stats[:, g, :])
        i.then_inc(norm_chain.sem, 1)
        dve.wait_ge(norm_chain.sem, norm_chain.next())
        nc.vector.tensor_scalar(ve[:], mv[:, :, 1], LN_EPS, None, ALU.add).then_inc(var_ready, 1)
        dve.wait_ge(rstd_ready, t + 1)
        if quant:
            for g in range(GU):
                i = nc.vector.tensor_scalar(xn[:, g, :], group_x(t, g), mv[:, g, 0:1], rstd[:, g:g + 1], ALU.subtract, ALU.mult)
            i.then_inc(norm_chain.sem, 1)
            dve.wait_ge(norm_chain.sem, norm_chain.next())
            nc.vector.tensor_reduce(out=sx[:], in_=xn[:], axis=AX.X, op=ALU.max, apply_absolute_value=True).then_inc(norm_chain.sem, 1)
            dve.wait_ge(norm_chain.sem, norm_chain.next())
            nc.vector.tensor_scalar(sx[:], sx[:], 1.0 / 127.0, 1e-8, ALU.mult, ALU.max).then_inc(norm_chain.sem, 1)
            dve.wait_ge(norm_chain.sem, norm_chain.next())
            nc.vector.reciprocal(rsx[:], sx[:]).then_inc(norm_chain.sem, 1)
            dve.wait_ge(norm_chain.sem, norm_chain.next())
            for g in range(GU):
                i = nc.vector.tensor_scalar(xn[:, g, :], xn[:, g, :], rsx[:, g:g + 1], MAGIC, ALU.mult, ALU.add)
            i.then_inc(norm_chain.sem, 1)
            dve.wait_ge(norm_chain.sem, norm_chain.next())
            if some((t - 1) * 3 + INPUT // 2 + 1):
                dve.wait_ge(filled[INPUT % 2], (t - 1) * 3 + INPUT // 2 + 1)
            nc.vector.tensor_scalar(qx[:], xn[:], MAGIC, None, ALU.subtract).then_inc(xn_ready, 1)
        else:
            nc.vector.tensor_tensor(out=ms[:], in0=rstd[:], in1=rstd[:], op=ALU.mult).then_inc(norm_chain.sem, 1)
            dve.wait_ge(norm_chain.sem, norm_chain.next())
            nc.vector.tensor_tensor(out=ms[:], in0=ms[:], in1=mv[:, :, 1], op=ALU.mult).then_inc(ms_ready, 1)
            dve.wait_ge(rr_ready, t + 1)
            if some((t - 1) * 3 + INPUT // 2 + 1):
                dve.wait_ge(filled[INPUT % 2], (t - 1) * 3 + INPUT // 2 + 1)
            for g in range(GU):
                i = nc.vector.tensor_scalar(xn[:, g, :], group_x(t, g), mv[:, g, 0:1], rr[:, g:g + 1], ALU.subtract, ALU.mult)
            i.then_inc(xn_ready, 1)
        norm_chain.end()

    def norm_pool(pool, t):
        pool.wait_ge(var_ready, t + 1)
        nc.gpsimd.tensor_tensor(out=rstd[:], in0=ve[:], in1=core.neghalf[:, 0:GU], op=ALU.pow).then_inc(rstd_ready, 1)
        if not quant:
            pool.wait_ge(ms_ready, t + 1)
            pool.sem_inc(passed, 1)
            nc.gpsimd.tensor_scalar(ms[:], ms[:], 1e-6, None, ALU.add).then_inc(ms_eps, 1)
            pool.wait_ge(ms_eps, t + 1)
            nc.gpsimd.tensor_tensor(out=r1[:], in0=ms[:], in1=core.neghalf[:, 0:GU], op=ALU.pow).then_inc(r1_raw, 1)
            pool.wait_ge(r1_raw, t + 1)
            nc.gpsimd.tensor_tensor(out=rr[:], in0=r1[:], in1=rstd[:], op=ALU.mult).then_inc(rr_ready, 1)

    def keys_pe(pe, t, par):
        pe.wait_ge(ctx_in[par], (t // 2 + 1) * n_ctx)
        F = fbank(pe, t, KEYS)
        for co in range(C):
            for ci in range(C):
                i = nc.tensor.matmul(F[:, co * UNIT:(co + 1) * UNIT], wkT[:, ci, co * P:(co + 1) * P], ctxT[par][:, ci, :, 0, :],
                                     start=(ci == 0), stop=(ci == C - 1))
        i.then_inc(filled[KEYS % 2], 1)

    def keys_act(act, t):
        fwait_filled(act, t, KEYS)
        if some(t):
            act.wait_ge(km_ready, t)
        for co in range(C):
            i = nc.scalar.activation(kT[:, co, :], FB[KEYS % 2][:, co * UNIT:(co + 1) * UNIT], ACT.Identity,
                                     bias=bk[:, co:co + 1] if quant else 0.0)
        i.then_inc(emptied[KEYS % 2], 1)

    def keys_pool(pool, t):
        pool.wait_ge(emptied[KEYS % 2], t * 3 + KEYS // 2 + 1)
        if some(t * GU):
            pool.wait_ge(scored, t * GU)
        for c in range(C):
            i = nc.gpsimd.tensor_tensor(out=km[:, c, :, :, :],
                                        in0=kT[:, c, :].rearrange("p (b k) -> p b k", k=S).unsqueeze(2).broadcast_to([P, BU, H8, S]),
                                        in1=hmask[:].unsqueeze(1).unsqueeze(3).broadcast_to([P, BU, H8, S]), op=ALU.mult)
        i.then_inc(km_ready, 1)

    def input_pe(pe, t):
        pe.wait_ge(xn_ready, t + 1)
        F = fbank(pe, t, INPUT)
        src, idt = (qx, core.identb) if quant else (xn, core.ident)
        F = F[:].bitcast(BF16) if quant else F
        for c in range(C):
            for g in range(GU):
                i = nc.tensor.transpose(F[:, c * UNIT + g * P:c * UNIT + (g + 1) * P], src[:, g, c * P:(c + 1) * P], idt[:])
        i.then_inc(filled[INPUT % 2], 1)

    def input_act(act, t):
        fwait_filled(act, t, INPUT)
        if some((t - 1) * 3 + QUERIES // 2 + 1):
            act.wait_ge(filled[QUERIES % 2], (t - 1) * 3 + QUERIES // 2 + 1)
        if quant:
            nc.scalar.activation(hT[:].rearrange("p c t -> p (c t)"), FB[INPUT % 2][:].bitcast(BF16)[:, 0:C * UNIT],
                                 ACT.Copy).then_inc(emptied[INPUT % 2], 1)
        else:
            if some(t * 3):
                act.wait_ge(filled[LAST % 2], t * 3)
            for c in range(C):
                i = nc.scalar.activation(hT[:, c, :], FB[INPUT % 2][:, c * UNIT:(c + 1) * UNIT], ACT.Copy, scale=norm_w[:, c:c + 1])
            i.then_inc(emptied[INPUT % 2], 1)

    def queries_pe(pe, t):
        pe.wait_ge(emptied[INPUT % 2], t * 3 + INPUT // 2 + 1)
        F = fbank(pe, t, QUERIES)
        if quant:
            for g in range(GU):
                for c in range(C):
                    i = nc.tensor.matmul(F[:, g * D:(g + 1) * D], hT[:, c, g * P:(g + 1) * P], wqT[:, c, :],
                                         start=(c == 0), stop=(c == C - 1))
        else:
            for co in range(C):
                for ci in range(C):
                    i = nc.tensor.matmul(F[:, co * UNIT:(co + 1) * UNIT], wqT[:, ci, co * P:(co + 1) * P], hT[:, ci, :],
                                         start=(ci == 0), stop=(ci == C - 1))
        i.then_inc(filled[QUERIES % 2], 1)

    def queries_dve(dve, t):
        q_chain.begin(t)
        fwait_filled(dve, t, QUERIES)
        if some(t * 3):
            dve.wait_ge(filled[LAST % 2], t * 3)
        F = FB[QUERIES % 2]
        for g in range(GU):
            i = nc.vector.scalar_tensor_tensor(out=qf[:, g, :], in0=F[:, g * D:(g + 1) * D], scalar=sx[:, g:g + 1], in1=swq[:],
                                               op0=ALU.mult, op1=ALU.mult)
        i.then_inc(q_chain.sem, 1)
        dve.wait_ge(q_chain.sem, q_chain.next())
        dve.sem_inc(emptied[QUERIES % 2], 1)
        nc.vector.tensor_tensor(out=qf[:], in0=qf[:], in1=bq[:].unsqueeze(1).broadcast_to([P, GU, D]), op=ALU.add).then_inc(qf_ready, 1)

    def queries_act(act, t, par):
        fwait_filled(act, t, QUERIES)
        if some((t - 1) * GU):
            act.wait_ge(scored, (t - 1) * GU)
        nc.scalar.activation(qT[par][:].rearrange("p c t -> p (c t)"), FB[QUERIES % 2][:], ACT.Copy).then_inc(emptied[QUERIES % 2], 1)

    def values_pe(pe, t, par, n):
        F = fbank(pe, t, V0 + n)
        for b in range(2):
            for c in range(C):
                tok = ctxT[par][:, c, 2 * n + b, :, :].rearrange("p j k -> p (j k)")
                i = nc.tensor.matmul(F[:, b * D:(b + 1) * D], tok, wvT[:, c, :],
                                     start=(c == 0), stop=(c == C - 1))
        i.then_inc(filled[(V0 + n) % 2], 1)

    def values_act(act, t, par, n):
        fwait_filled(act, t, V0 + n)
        if some((t - 1) * GU):
            act.wait_ge(o_ready, (t - 1) * GU)
        act.wait_ge(zeroed, 1)
        v = FB[(V0 + n) % 2][:].rearrange("p (b h j d) -> p b h j d", b=2, j=2, d=HD)
        for j in range(2):
            i = nc.scalar.activation(vbd[par][64 * j:64 * j + 64, 2 * n:2 * n + 2, :, j, :], v[64 * j:64 * j + 64, :, :, j, :], ACT.Copy)
        i.then_inc(emptied[(V0 + n) % 2], 1)

    def last_pe(pe, t):
        F = fbank(pe, t, LAST)
        if quant:
            pe.wait_ge(qf_ready, t + 1)
            for c in range(C):
                for g in range(GU):
                    i = nc.tensor.transpose(F[:, c * UNIT + g * P:c * UNIT + (g + 1) * P], qf[:, g, c * P:(c + 1) * P], core.ident[:])
        else:
            for g in range(GU):
                for c in range(C):
                    i = nc.tensor.matmul(F[:, g * D:(g + 1) * D], hT[:, c, g * P:(g + 1) * P], wgT[:, c, :],
                                         start=(c == 0), stop=(c == C - 1))
        i.then_inc(filled[LAST % 2], 1)

    def last_act(act, t, par):
        fwait_filled(act, t, LAST)
        if quant:
            if some((t - 1) * GU):
                act.wait_ge(scored, (t - 1) * GU)
            nc.scalar.activation(qT[par][:].rearrange("p c t -> p (c t)"), FB[LAST % 2][:], ACT.Copy).then_inc(emptied[LAST % 2], 1)
        else:
            if some((t - 1) * GU):
                act.wait_ge(y_used, (t - 1) * GU)
            nc.scalar.activation(gate[par][:].rearrange("p g d -> p (g d)"), FB[LAST % 2][:], ACT.Tanh,
                                 scale=0.5).then_inc(emptied[LAST % 2], 1)

    def scores_pe(pe, t, par, g):
        if g == 0:
            pe.wait_ge(km_ready, t + 1)
            pe.wait_ge(emptied[(LAST if quant else QUERIES) % 2], t * 3 + (LAST if quant else QUERIES) // 2 + 1)
        if some((t - 1) * GU + g + 1):
            pe.wait_ge(pTs_ready, (t - 1) * GU + g + 1)
        for c in range(C):
            for b in range(2):
                i = nc.tensor.matmul(SB[g][c][64 * b:64 * b + 64, :], qT[par][:, c, (2 * g + b) * S:(2 * g + b + 1) * S],
                                     km[:, c, 2 * g + b, :, :].rearrange("p h k -> p (h k)"), start=True, stop=True)
        i.then_inc(scored, 1)

    def softmax_dve(dve, t, par, g):
        n = t * GU + g
        soft_chain.begin(t, g)
        if not quant and g == 0:
            m_chain.begin(t)
            kp = keep[:, bass.ds(t * GU, GU), :]
            nc.vector.tensor_reduce(out=valid[:], in_=kp, axis=AX.X, op=ALU.max)
            nc.vector.tensor_scalar(neg[:], kp, 1.0, BIG, ALU.subtract, ALU.mult).then_inc(m_chain.sem, 1)
            dve.wait_ge(m_chain.sem, m_chain.next())
        dve.wait_ge(scored, n + 1)
        if quant and g == 0:
            dve.wait_ge(ctx_in[par], (t // 2 + 1) * n_ctx)
        if some(n - 1):
            dve.wait_ge(pT_ready, n - 1)
        add = mask[par][:, g, :] if quant else neg[:, g, :]
        for c in range(C):
            i = nc.vector.scalar_tensor_tensor(out=pr[g][:, c * H8:(c + 1) * H8, :], in0=SB[g][c][:].rearrange("p (h k) -> p h k", k=S),
                                               scalar=float(HD) ** -0.5, in1=add.unsqueeze(1).broadcast_to([P, H8, S]),
                                               op0=ALU.mult, op1=ALU.add)
        i.then_inc(s_read, 1)
        dve.wait_ge(s_read, n + 1)
        nc.vector.tensor_reduce(out=smax[:, g, :], in_=pr[g][:], axis=AX.X, op=ALU.max).then_inc(soft_chain.sem, 1)
        dve.wait_ge(soft_chain.sem, soft_chain.next())
        nc.vector.tensor_tensor(out=pr[g][:], in0=pr[g][:], in1=smax[:, g, :].unsqueeze(2).broadcast_to([P, NH, S]),
                                op=ALU.subtract).then_inc(shifted, 1)

    def exp_act(act, t, g):
        act.wait_ge(shifted, t * GU + g + 1)
        nc.scalar.activation(pr[g][:], pr[g][:], ACT.Exp).then_inc(e_ready, 1)

    def sums_dve(dve, t, g):
        soft_chain.begin(t, GU + 3 * g)
        dve.wait_ge(e_ready, t * GU + g + 1)
        nc.vector.tensor_reduce(out=rsum[:, g, :], in_=pr[g][:], axis=AX.X, op=ALU.add).then_inc(soft_chain.sem, 1)
        dve.wait_ge(soft_chain.sem, soft_chain.next())
        nc.vector.reciprocal(rsum[:, g, :], rsum[:, g, :]).then_inc(soft_chain.sem, 1)
        dve.wait_ge(soft_chain.sem, soft_chain.next())
        if not quant:
            nc.vector.tensor_scalar(rsum[:, g, :], rsum[:, g, :], valid[:, g:g + 1], None, ALU.mult).then_inc(soft_chain.sem, 1)
            dve.wait_ge(soft_chain.sem, soft_chain.next())
        else:
            soft_chain.k += 1
            dve.sem_inc(soft_chain.sem, 1)

    def transpose_pe(pe, t, g):
        n = t * GU + g
        pe.wait_ge(e_ready, n + 1)
        pe.wait_ge(s_read, n + 1)
        for p in range(NH // 2):
            i = nc.tensor.transpose(SB[g][p // 4][:, (p % 4) * P:(p % 4 + 1) * P],
                                    pr[g][:, 2 * p:2 * p + 2, :].rearrange("p h k -> p (h k)"), core.ident[:])
        i.then_inc(pT_ready, 1)

    def transposed_act(act, t, g):
        n = t * GU + g
        act.wait_ge(pT_ready, n + 1)
        if some(n):
            act.wait_ge(o_ready, n)
        for c in range(C):
            i = nc.scalar.activation(pT[:, 4 * c:4 * c + 4, :], SB[g][c][:].rearrange("p (h q) -> p h q", q=P), ACT.Copy)
        i.then_inc(pTs_ready, 1)

    def apply_pe(pe, t, par, g):
        n = t * GU + g
        pe.wait_ge(pTs_ready, n + 1)
        if some(n - 1):
            pe.wait_ge(y_used, n - 1)
        pe.wait_ge(emptied[V1 % 2], t * 3 + V1 // 2 + 1)
        pe.wait_ge(emptied[V0 % 2], t * 3 + V0 // 2 + 1)
        for p in range(NH // 2):
            for b in range(2):
                i = nc.tensor.matmul(OB[g][64 * b:64 * b + 64, p * 2 * HD:(p + 1) * 2 * HD], pT[:, p, 64 * b:64 * b + 64],
                                     vbd[par][:, 2 * g + b, p, :, :].rearrange("p j d -> p (j d)"), start=True, stop=True)
        i.then_inc(o_ready, 1)

    def result_dve(dve, t, g):
        n = t * GU + g
        out_chain.begin(t, g * out_chain.per_tile // GU)
        dve.wait_ge(o_ready, n + 1)
        if some(n):
            dve.wait_ge(oT_filled, n)
        i = nc.vector.tensor_tensor(out=o[:].rearrange("p (h d) -> p h d", d=HD),
                                    in0=OB[g][:, 0:D].rearrange("p (h d) -> p h d", d=HD),
                                    in1=rsum[:, g, :].unsqueeze(2).broadcast_to([P, NH, HD]), op=ALU.mult)
        if not quant:
            i.then_inc(on_ready, 1)
            return
        i.then_inc(out_chain.sem, 1)
        dve.wait_ge(out_chain.sem, out_chain.next())
        nc.vector.tensor_tensor(out=o[:], in0=o[:], in1=bv[:], op=ALU.add).then_inc(out_chain.sem, 1)
        dve.wait_ge(out_chain.sem, out_chain.next())
        nc.vector.tensor_reduce(out=so[:], in_=o[:], axis=AX.X, op=ALU.max, apply_absolute_value=True).then_inc(out_chain.sem, 1)
        dve.wait_ge(out_chain.sem, out_chain.next())
        nc.vector.tensor_scalar(so[:], so[:], 1.0 / 127.0, 1e-8, ALU.mult, ALU.max).then_inc(out_chain.sem, 1)
        dve.wait_ge(out_chain.sem, out_chain.next())
        nc.vector.reciprocal(rso[:], so[:]).then_inc(out_chain.sem, 1)
        dve.wait_ge(out_chain.sem, out_chain.next())
        nc.vector.tensor_scalar(o[:], o[:], rso[:], MAGIC, ALU.mult, ALU.add).then_inc(out_chain.sem, 1)
        dve.wait_ge(out_chain.sem, out_chain.next())
        nc.vector.tensor_scalar(oq[:], o[:], MAGIC, None, ALU.subtract).then_inc(on_ready, 1)

    def result_pe(pe, t, g):
        n = t * GU + g
        pe.wait_ge(on_ready, n + 1)
        src, idt = (oq, core.identb) if quant else (o, core.ident)
        F = OB[g][:].bitcast(BF16) if quant else OB[g]
        for c in range(C):
            i = nc.tensor.transpose(F[:, c * P:(c + 1) * P], src[:, c * P:(c + 1) * P], idt[:])
        i.then_inc(oT_filled, 1)

    def result_act(act, t, g):
        n = t * GU + g
        act.wait_ge(oT_filled, n + 1)
        if some(n):
            act.wait_ge(y_ready, n)
        F = OB[g][:].bitcast(BF16) if quant else OB[g]
        nc.scalar.activation(oT[:].rearrange("p c t -> p (c t)"), F[:, 0:C * P], ACT.Copy).then_inc(oT_ready, 1)

    def out_pe(pe, t, g):
        pe.wait_ge(oT_ready, t * GU + g + 1)
        for c in range(C):
            i = nc.tensor.matmul(OB[g][:, D:2 * D], oT[:, c, :], woT[:, c, :], start=(c == 0), stop=(c == C - 1))
        i.then_inc(y_ready, 1)

    def residual_dve(dve, t, par, g):
        n = t * GU + g
        dve.wait_ge(y_ready, n + 1)
        Yg = OB[g][:, D:2 * D]
        if quant:
            y_chain.begin(t, 2 * g)
            nc.vector.scalar_tensor_tensor(out=y[:], in0=Yg, scalar=so[:], in1=swo[:], op0=ALU.mult, op1=ALU.mult).then_inc(y_chain.sem, 1)
            dve.wait_ge(y_chain.sem, y_chain.next())
            nc.vector.tensor_tensor(out=y[:], in0=y[:], in1=bo[:], op=ALU.add).then_inc(y_chain.sem, 1)
            dve.wait_ge(y_chain.sem, y_chain.next())
            nc.vector.tensor_tensor(out=group_x(t, g), in0=group_x(t, g), in1=y[:], op=ALU.add).then_inc(y_used, 1)
        else:
            y_chain.begin(t, g)
            nc.vector.scalar_tensor_tensor(out=y[:], in0=gate[par][:, g, :], scalar=1.0, in1=Yg, op0=ALU.add, op1=ALU.mult).then_inc(y_chain.sem, 1)
            dve.wait_ge(y_chain.sem, y_chain.next())
            nc.vector.scalar_tensor_tensor(out=group_x(t, g), in0=y[:], scalar=0.5, in1=group_x(t, g),
                                           op0=ALU.mult, op1=ALU.add).then_inc(y_used, 1)

    y_chain = Chain(sem("y_chain"), GU * (2 if quant else 1))

    loads = [(wkT[:], args["wkT" if quant else "z_wkT"].rearrange("(c p) o -> p c o", p=P)),
             (wvT[:], args["wvT" if quant else "z_wvT"].rearrange("(c p) o -> p c o", p=P)),
             (hmask[:], args["hmask"])]
    if quant:
        loads += [(bq[:], args["bq"]), (bk[:], args["bk"]), (bv[:], args["bv"]), (bo[:], args["bo"])]
    else:
        loads += [(wqT[:], args["z_wqT"].rearrange("(c p) o -> p c o", p=P)), (woT[:], args["z_woT"].rearrange("(c p) o -> p c o", p=P)),
                  (wgT[:], args["z_wgT"].rearrange("(c p) o -> p c o", p=P)), (norm_w[:], args["norm_w"]),
                  (keep[:], args["keep"].rearrange("p (g k) -> p g k", k=S))]
    n_in, n_ctx = 16 * len(loads), 16 * (2 * C + (1 if quant else 0))

    def load_ctx(sp, t, par):
        if some((t - 2) * 3 + V1 // 2 + 1):
            sp.wait_ge(emptied[V1 % 2], (t - 2) * 3 + V1 // 2 + 1)
        sp.sem_inc(passed, 1)
        if some((t - 2) * 3 + V0 // 2 + 1):
            sp.wait_ge(emptied[V0 % 2], (t - 2) * 3 + V0 // 2 + 1)
        sp.sem_inc(passed, 1)
        if quant:
            if some((t - 1) * GU):
                sp.wait_ge(s_read, (t - 1) * GU)
            sp.sem_inc(passed, 1)
        src = args["ctxT"].rearrange("(c p) n -> p c n", p=P)[:, :, bass.ds(t * UNIT, UNIT)]
        for c in range(C):
            for j in range(2):
                sp.dma_start(ctxT[par][:, c, :, j, :], src[:, c, :].rearrange("p (b k) -> p b k", k=S)).then_inc(ctx_in[par], 16)
        if quant:
            sp.dma_start(mask[par][:], args["mask"].rearrange("(g p) k -> p g k", p=P)[:, bass.ds(t * GU, GU), :]).then_inc(ctx_in[par], 16)

    def unit_pe(pe, t, par):
        nxt = 1 - par
        scores_pe(pe, t, par, 0)
        scores_pe(pe, t, par, 1)
        if not is_last(t):
            keys_pe(pe, t + 1, nxt)
            input_pe(pe, t + 1)
            queries_pe(pe, t + 1)
        transpose_pe(pe, t, 0)
        if not is_last(t):
            values_pe(pe, t + 1, nxt, 0)
        apply_pe(pe, t, par, 0)
        if not is_last(t):
            values_pe(pe, t + 1, nxt, 1)
        transpose_pe(pe, t, 1)
        if not is_last(t):
            last_pe(pe, t + 1)
        apply_pe(pe, t, par, 1)
        for g in range(GU):
            result_pe(pe, t, g)
            out_pe(pe, t, g)

    def unit_act(act, t, par):
        nxt = 1 - par
        if not is_last(t):
            keys_act(act, t + 1)
            input_act(act, t + 1)
            if not quant:
                queries_act(act, t + 1, nxt)
        exp_act(act, t, 0)
        exp_act(act, t, 1)
        transposed_act(act, t, 0)
        if not is_last(t):
            values_act(act, t + 1, nxt, 0)
            values_act(act, t + 1, nxt, 1)
        transposed_act(act, t, 1)
        if not is_last(t):
            last_act(act, t + 1, nxt)
        result_act(act, t, 0)
        result_act(act, t, 1)

    def unit_dve(dve, t, par):
        softmax_dve(dve, t, par, 0)
        if not is_last(t):
            norm_dve(dve, t + 1)
        softmax_dve(dve, t, par, 1)
        sums_dve(dve, t, 0)
        if quant and not is_last(t):
            queries_dve(dve, t + 1)
        sums_dve(dve, t, 1)
        for g in range(GU):
            result_dve(dve, t, g)
            residual_dve(dve, t, par, g)

    def unit_pool(pool, t, par):
        if not is_last(t):
            norm_pool(pool, t + 1)
            keys_pool(pool, t + 1)

    with nc.Block() as block:
        @block.sync
        def _(sp):
            for out, in_ in loads:
                sp.dma_start(out, in_).then_inc(weights_in, 16)
            load_ctx(sp, 0, 0)
            load_ctx(sp, 1, 1)
            with sp.Fori(1, NU // 2) as pair:
                load_ctx(sp, pair * 2, 0)
                load_ctx(sp, pair * 2 + 1, 1)

        @block.tensor
        def _(pe):
            pe.wait_ge(weights_in, n_in)
            keys_pe(pe, 0, 0)
            input_pe(pe, 0)
            queries_pe(pe, 0)
            values_pe(pe, 0, 0, 0)
            values_pe(pe, 0, 0, 1)
            last_pe(pe, 0)
            unit_loop(pe, unit_pe)

        @block.scalar
        def _(act):
            act.wait_ge(weights_in, n_in)
            keys_act(act, 0)
            input_act(act, 0)
            if not quant:
                queries_act(act, 0, 0)
            values_act(act, 0, 0, 0)
            values_act(act, 0, 0, 1)
            last_act(act, 0, 0)
            unit_loop(act, unit_act)

        @block.vector
        def _(dve):
            dve.wait_ge(weights_in, n_in)
            norm_dve(dve, 0)
            if quant:
                queries_dve(dve, 0)
            unit_loop(dve, unit_dve)

        @block.gpsimd
        def _(pool):
            pool.wait_ge(weights_in, n_in)
            nc.gpsimd.memset(vbd[0][:], 0.0)
            nc.gpsimd.memset(vbd[1][:], 0.0).then_inc(zeroed, 1)
            norm_pool(pool, 0)
            keys_pool(pool, 0)
            unit_loop(pool, unit_pool)
    st.close()


def linear_attention_stage(core):
    nc, args, bank, x = core.nc, core.args, core.bank, core.x
    st = Stage(core, "lin")
    sb, sem = st.sb, st.sem
    HD, H8, BU = 16, 8, UNIT // S
    W = P + H8

    wqT, wgT, woT = sb("wqT", [P, C, D]), sb("wgT", [P, C, D]), sb("woT", [P, C, D])
    wkvT = sb("wkvT", [P, C, 2 * D])
    bg, hmask, bdmask = sb("bg", [P, D]), sb("hmask", [P, H8]), sb("bdmask", [P, P])
    ctxT = [sb(f"ctxT{i}", [P, C, UNIT]) for i in range(2)]
    xn = sb("xn", [P, GU, D])
    stats, mv = sb("stats", [P, GU, 6]), sb("mv", [P, GU, 2])
    ve, rstd = sb("ve", [P, GU]), sb("rstd", [P, GU])
    hT = sb("hT", [P, C, UNIT])
    low = sb("low", [P, 2 * UNIT])
    qT = [sb(f"qT{i}", [P, C * UNIT]) for i in range(2)]
    ks = [sb(f"ks{i}", [P, GU * D]) for i in range(2)]
    vs = [sb(f"vs{i}", [P, GU, C, P + 1]) for i in range(2)]
    graw = sb("graw", [P, GU, D])
    gate = [sb(f"gate{i}", [P, GU, D]) for i in range(2)]
    kv = sb("kv", [P, BU, C, W])
    rz = sb("rz", [P, C, H8])
    o, oT = sb("o", [P, D]), sb("oT", [P, C * P])

    weights_in, passed = sem("weights_in"), st.passed()
    ctx_in = [sem(f"ctx_in{i}") for i in range(2)]
    var_ready, rstd_ready, xn_ready, ones_ready = sem("var_ready"), sem("rstd_ready"), sem("xn_ready"), sem("ones_ready")
    filled = [sem(f"filled{i}") for i in range(2)]
    emptied = [sem(f"emptied{i}") for i in range(2)]
    low_ready, low_exp, graw_ready, gate_ready = sem("low_ready"), sem("low_exp"), sem("graw_ready"), sem("gate_ready")
    kv_filled, kv_ready, o_ready, on_ready, oT_filled, oT_ready, y_ready, y_used = (
        sem(n) for n in ("kv_filled", "kv_ready", "o_ready", "on_ready", "oT_filled", "oT_ready", "y_ready", "y_used"))
    norm_chain = Chain(sem("norm_chain"), 2)
    out_chain = Chain(sem("out_chain"), GU * 3)
    KEYS, INPUT, VALUES, QUERIES, GATE = 0, 1, 2, 3, 4
    ORDER = {0: [KEYS, VALUES, GATE], 1: [INPUT, QUERIES]}
    KV = [bank[0], bank[1], bank[2], bank[3]]
    OB = [bank[4], bank[5]]
    FB = [bank[6], bank[7]]

    def use(t, k):
        own = ORDER[k % 2]
        return t * len(own) + own.index(k)

    def filled_wait(eng, t, k):
        if some(use(t, k) + 1):
            eng.wait_ge(filled[k % 2], use(t, k) + 1)

    def emptied_wait(eng, t, k):
        eng.wait_ge(emptied[k % 2], use(t, k) + 1)

    def fbank(pe, t, k):
        if some(use(t, k)):
            pe.wait_ge(emptied[k % 2], use(t, k))
        return FB[k % 2]

    def group_x(t, g):
        return x[:, bass.ds(t * (GU * D) + g * D, D)]

    def norm_dve(dve, t):
        norm_chain.begin(t)
        for g in range(GU):
            i = nc.vector.bn_stats(stats[:, g, :], group_x(t, g))
        i.then_inc(norm_chain.sem, 1)
        dve.wait_ge(norm_chain.sem, norm_chain.next())
        dve.sem_inc(passed, 1)
        for g in range(GU):
            i = nc.vector.bn_aggr(mv[:, g, :], stats[:, g, :])
        i.then_inc(norm_chain.sem, 1)
        dve.wait_ge(norm_chain.sem, norm_chain.next())
        nc.vector.tensor_scalar(ve[:], mv[:, :, 1], LN_EPS, None, ALU.add).then_inc(var_ready, 1)
        dve.wait_ge(rstd_ready, t + 1)
        if some(use(t - 1, INPUT) + 1):
            dve.wait_ge(filled[INPUT % 2], use(t - 1, INPUT) + 1)
        for g in range(GU):
            i = nc.vector.tensor_scalar(xn[:, g, :], group_x(t, g), mv[:, g, 0:1], rstd[:, g:g + 1], ALU.subtract, ALU.mult)
        i.then_inc(xn_ready, 1)
        norm_chain.end()

    def norm_pool(pool, t):
        pool.wait_ge(var_ready, t + 1)
        nc.gpsimd.tensor_tensor(out=rstd[:], in0=ve[:], in1=core.neghalf[:, 0:GU], op=ALU.pow).then_inc(rstd_ready, 1)

    def keys_pe(pe, t, par):
        pe.wait_ge(ctx_in[par], (t // 2 + 1) * 16)
        F = fbank(pe, t, KEYS)
        for g in range(GU):
            for c in range(C):
                i = nc.tensor.matmul(F[:, g * D:(g + 1) * D], ctxT[par][:, c, g * P:(g + 1) * P], wkvT[:, c, 0:D],
                                     start=(c == 0), stop=(c == C - 1))
        i.then_inc(filled[KEYS % 2], 1)

    def values_pe(pe, t, par):
        F = fbank(pe, t, VALUES)
        for g in range(GU):
            for c in range(C):
                i = nc.tensor.matmul(F[:, g * D:(g + 1) * D], ctxT[par][:, c, g * P:(g + 1) * P], wkvT[:, c, D:2 * D],
                                     start=(c == 0), stop=(c == C - 1))
        i.then_inc(filled[VALUES % 2], 1)

    def values_act(act, t, par):
        filled_wait(act, t, VALUES)
        act.wait_ge(ones_ready, 2)
        if some((t - 1) * BU):
            act.wait_ge(kv_filled, (t - 1) * BU)
        nc.scalar.activation(vs[par][:, :, :, 0:P], FB[VALUES % 2][:].rearrange("p (g c d) -> p g c d", g=GU, c=C),
                             ACT.Copy).then_inc(emptied[VALUES % 2], 1)

    def input_pe(pe, t):
        pe.wait_ge(xn_ready, t + 1)
        F = fbank(pe, t, INPUT)
        for c in range(C):
            for g in range(GU):
                i = nc.tensor.transpose(F[:, c * UNIT + g * P:c * UNIT + (g + 1) * P], xn[:, g, c * P:(c + 1) * P], core.ident[:])
        i.then_inc(filled[INPUT % 2], 1)

    def input_act(act, t):
        filled_wait(act, t, INPUT)
        filled_wait(act, t - 1, GATE)
        nc.scalar.activation(hT[:].rearrange("p c t -> p (c t)"), FB[INPUT % 2][:], ACT.Copy).then_inc(emptied[INPUT % 2], 1)

    def queries_pe(pe, t):
        emptied_wait(pe, t, INPUT)
        F = fbank(pe, t, QUERIES)
        for co in range(C):
            for ci in range(C):
                i = nc.tensor.matmul(F[:, co * UNIT:(co + 1) * UNIT], wqT[:, ci, co * P:(co + 1) * P], hT[:, ci, :],
                                     start=(ci == 0), stop=(ci == C - 1))
        i.then_inc(filled[QUERIES % 2], 1)

    def gate_pe(pe, t):
        F = fbank(pe, t, GATE)
        for g in range(GU):
            for c in range(C):
                i = nc.tensor.matmul(F[:, g * D:(g + 1) * D], hT[:, c, g * P:(g + 1) * P], wgT[:, c, :],
                                     start=(c == 0), stop=(c == C - 1))
        i.then_inc(filled[GATE % 2], 1)

    def map_dve(dve, t, k, m, out):
        n = 2 * t + m
        filled_wait(dve, t, k)
        if some(use(t, KEYS) + 1 if m else use(t - 1, QUERIES) + 1):
            dve.wait_ge(emptied[KEYS % 2 if m else QUERIES % 2], use(t, KEYS) + 1 if m else use(t - 1, QUERIES) + 1)
        nc.vector.tensor_scalar(low[:], FB[k % 2][:], 0.0, None, ALU.min).then_inc(low_ready, 1)
        dve.wait_ge(low_exp, n + 1)
        if some((t - 1) * (GU if k == QUERIES else BU)):
            dve.wait_ge(o_ready if k == QUERIES else kv_filled, (t - 1) * (GU if k == QUERIES else BU))
        nc.vector.scalar_tensor_tensor(out=out[:], in0=FB[k % 2][:], scalar=0.0, in1=low[:], op0=ALU.max,
                                       op1=ALU.add).then_inc(emptied[k % 2], 1)

    def map_act(act, t, m):
        act.wait_ge(low_ready, 2 * t + m + 1)
        nc.scalar.activation(low[:], low[:], ACT.Exp).then_inc(low_exp, 1)

    def gate_dve(dve, t):
        filled_wait(dve, t, GATE)
        if some(t):
            dve.wait_ge(gate_ready, t)
        nc.vector.tensor_tensor(out=graw[:], in0=FB[GATE % 2][:].rearrange("p (g d) -> p g d", d=D),
                                in1=bg[:].unsqueeze(1).broadcast_to([P, GU, D]), op=ALU.add).then_inc(emptied[GATE % 2], 1)

    def gate_act(act, t, par):
        emptied_wait(act, t, GATE)
        if some((t - 1) * GU):
            act.wait_ge(on_ready, (t - 1) * GU)
        nc.scalar.activation(gate[par][:], graw[:], ACT.Tanh, scale=0.5).then_inc(gate_ready, 1)

    def summary_pe(pe, t, par):
        emptied_wait(pe, t, KEYS)
        emptied_wait(pe, t, VALUES)
        for b in range(BU):
            g, half = b // 2, slice(64 * (b % 2), 64 * (b % 2) + 64)
            if some((t - 1) * BU + b + 1):
                pe.wait_ge(kv_ready, (t - 1) * BU + b + 1)
            for c in range(C):
                i = nc.tensor.matmul(KV[b][:, c * (P + 1):(c + 1) * (P + 1)], ks[par][half, g * D + c * P:g * D + (c + 1) * P],
                                     vs[par][half, g, c, :], start=True, stop=True)
            i.then_inc(kv_filled, 1)

    def summary_dve(dve, t):
        if some(t * GU):
            dve.wait_ge(o_ready, t * GU)
        for b in range(BU):
            dve.wait_ge(kv_filled, t * BU + b + 1)
            prod = KV[b][:, 0:C * (P + 1)].rearrange("p (c w) -> p c w", w=P + 1)
            nc.vector.tensor_tensor(out=kv[:, b, :, 0:P], in0=prod[:, :, 0:P], in1=bdmask[:].unsqueeze(1).broadcast_to([P, C, P]), op=ALU.mult)
            nc.vector.tensor_tensor(out=kv[:, b, :, P:W], in0=prod[:, :, P:P + 1].broadcast_to([P, C, H8]),
                                    in1=hmask[:].unsqueeze(1).broadcast_to([P, C, H8]), op=ALU.mult).then_inc(kv_ready, 1)

    def apply_pe(pe, t, par, g):
        n = t * GU + g
        pe.wait_ge(kv_ready, t * BU + 2 * g + 2)
        if some(n - 1):
            pe.wait_ge(y_used, n - 1)
        for b in (2 * g, 2 * g + 1):
            for c in range(C):
                i = nc.tensor.matmul(OB[g][64 * (b % 2):64 * (b % 2) + 64, c * W:(c + 1) * W],
                                     qT[par][:, c * UNIT + b * S:c * UNIT + (b + 1) * S], kv[:, b, c, :], start=True, stop=True)
        i.then_inc(o_ready, 1)

    def result_dve(dve, t, par, g):
        n = t * GU + g
        out_chain.begin(t, 3 * g)
        dve.wait_ge(o_ready, n + 1)
        res = OB[g][:, 0:C * W].rearrange("p (c w) -> p c w", w=W)
        nc.vector.tensor_scalar(rz[:], res[:, :, P:W], 1e-6, None, ALU.add).then_inc(out_chain.sem, 1)
        dve.wait_ge(out_chain.sem, out_chain.next())
        nc.vector.reciprocal(rz[:], rz[:]).then_inc(out_chain.sem, 1)
        dve.wait_ge(out_chain.sem, out_chain.next())
        if some(n):
            dve.wait_ge(oT_filled, n)
        o4 = o[:].rearrange("p (c h d) -> p c h d", c=C, d=HD)
        nc.vector.tensor_tensor(out=o4, in0=res[:, :, 0:P].rearrange("p c (h d) -> p c h d", d=HD),
                                in1=rz[:].unsqueeze(3).broadcast_to([P, C, H8, HD]), op=ALU.mult).then_inc(out_chain.sem, 1)
        dve.wait_ge(out_chain.sem, out_chain.next())
        dve.wait_ge(gate_ready, t + 1)
        nc.vector.scalar_tensor_tensor(out=o[:], in0=gate[par][:, g, :], scalar=1.0, in1=o[:], op0=ALU.add,
                                       op1=ALU.mult).then_inc(on_ready, 1)

    def result_pe(pe, t, g):
        pe.wait_ge(on_ready, t * GU + g + 1)
        for c in range(C):
            i = nc.tensor.transpose(OB[g][:, c * P:(c + 1) * P], o[:, c * P:(c + 1) * P], core.ident[:])
        i.then_inc(oT_filled, 1)

    def result_act(act, t, g):
        act.wait_ge(oT_filled, t * GU + g + 1)
        if some(t * GU + g):
            act.wait_ge(y_ready, t * GU + g)
        nc.scalar.activation(oT[:], OB[g][:, 0:C * P], ACT.Copy).then_inc(oT_ready, 1)

    def out_pe(pe, t, g):
        pe.wait_ge(oT_ready, t * GU + g + 1)
        for c in range(C):
            i = nc.tensor.matmul(OB[g][:, D:2 * D], oT[:, c * P:(c + 1) * P], woT[:, c, :], start=(c == 0), stop=(c == C - 1))
        i.then_inc(y_ready, 1)

    def residual_dve(dve, t, g):
        dve.wait_ge(y_ready, t * GU + g + 1)
        nc.vector.scalar_tensor_tensor(out=group_x(t, g), in0=OB[g][:, D:2 * D], scalar=0.5, in1=group_x(t, g),
                                       op0=ALU.mult, op1=ALU.add).then_inc(y_used, 1)

    loads = [(w[:], args[n].rearrange("(c p) o -> p c o", p=P)) for w, n in ((wqT, "l_wqT"), (wgT, "l_wgT"), (woT, "l_woT"), (wkvT, "l_wkvT"))]
    loads += [(bg[:], args["bg"]), (hmask[:], args["hmask"]), (bdmask[:], args["bdmask"])]
    n_in = 16 * len(loads)

    def load_ctx(sp, t, par):
        if some(use(t - 2, VALUES) + 1):
            sp.wait_ge(emptied[VALUES % 2], use(t - 2, VALUES) + 1)
        sp.sem_inc(passed, 1)
        sp.dma_start(ctxT[par][:], args["ctxT"].rearrange("(c p) n -> p c n", p=P)[:, :, bass.ds(t * UNIT, UNIT)]).then_inc(ctx_in[par], 16)

    def unit_pe(pe, t, par):
        nxt = 1 - par
        summary_pe(pe, t, par)
        if not is_last(t):
            keys_pe(pe, t + 1, nxt)
            input_pe(pe, t + 1)
            values_pe(pe, t + 1, nxt)
        apply_pe(pe, t, par, 0)
        apply_pe(pe, t, par, 1)
        if not is_last(t):
            queries_pe(pe, t + 1)
            gate_pe(pe, t + 1)
        for g in range(GU):
            result_pe(pe, t, g)
            out_pe(pe, t, g)

    def unit_act(act, t, par):
        nxt = 1 - par
        if not is_last(t):
            map_act(act, t + 1, 0)
            input_act(act, t + 1)
            values_act(act, t + 1, nxt)
            map_act(act, t + 1, 1)
            gate_act(act, t + 1, nxt)
        result_act(act, t, 0)
        result_act(act, t, 1)

    def unit_dve(dve, t, par):
        nxt = 1 - par
        if not is_last(t):
            norm_dve(dve, t + 1)
        summary_dve(dve, t)
        if not is_last(t):
            map_dve(dve, t + 1, KEYS, 0, ks[nxt])
            map_dve(dve, t + 1, QUERIES, 1, qT[nxt])
            gate_dve(dve, t + 1)
        for g in range(GU):
            result_dve(dve, t, par, g)
        for g in range(GU):
            residual_dve(dve, t, g)

    def unit_pool(pool, t, par):
        if not is_last(t):
            norm_pool(pool, t + 1)

    with nc.Block() as block:
        @block.sync
        def _(sp):
            for out, in_ in loads:
                sp.dma_start(out, in_).then_inc(weights_in, 16)
            load_ctx(sp, 0, 0)
            load_ctx(sp, 1, 1)
            with sp.Fori(1, NU // 2) as pair:
                load_ctx(sp, pair * 2, 0)
                load_ctx(sp, pair * 2 + 1, 1)

        @block.tensor
        def _(pe):
            pe.wait_ge(weights_in, n_in)
            keys_pe(pe, 0, 0)
            input_pe(pe, 0)
            values_pe(pe, 0, 0)
            queries_pe(pe, 0)
            gate_pe(pe, 0)
            unit_loop(pe, unit_pe)

        @block.scalar
        def _(act):
            act.wait_ge(weights_in, n_in)
            map_act(act, 0, 0)
            input_act(act, 0)
            values_act(act, 0, 0)
            map_act(act, 0, 1)
            gate_act(act, 0, 0)
            unit_loop(act, unit_act)

        @block.vector
        def _(dve):
            dve.wait_ge(weights_in, n_in)
            norm_dve(dve, 0)
            map_dve(dve, 0, KEYS, 0, ks[0])
            map_dve(dve, 0, QUERIES, 1, qT[0])
            gate_dve(dve, 0)
            unit_loop(dve, unit_dve)

        @block.gpsimd
        def _(pool):
            for i in range(2):
                nc.gpsimd.memset(vs[i][:], 1.0).then_inc(ones_ready, 1)
            norm_pool(pool, 0)
            unit_loop(pool, unit_pool)
    st.close()


def memory_attention_stage(core):
    nc, args, bank, x = core.nc, core.args, core.bank, core.x
    st = Stage(core, "mem")
    sb, sem = st.sb, st.sem
    ctxT = [sb(f"ctxT{i}", [P, C, UNIT]) for i in range(2)]
    ctx = [sb(f"ctx{i}", [P, GU, D]) for i in range(2)]
    keep = sb("keep", [P, NG, S], U8)
    neg, valid = sb("neg", [P, GU, S]), sb("valid", [P, GU])
    xn = sb("xn", [P, GU, D])
    stats, mv = sb("stats", [P, GU, 6]), sb("mv", [P, GU, 2])
    ve, rstd = sb("ve", [P, GU]), sb("rstd", [P, GU])
    hT = sb("hT", [P, C, UNIT])
    pr = sb("pr", [P, GU, S])
    smax, rsum = sb("smax", [P, GU]), sb("rsum", [P, GU])
    pbd = sb("pbd", [P, GU, P])
    pT = sb("pT", [P, UNIT])

    weights_in, passed = sem("weights_in"), st.passed()
    ctx_in = [sem(f"ctx_in{i}") for i in range(2)]
    var_ready, rstd_ready, xn_ready, zeroed = sem("var_ready"), sem("rstd_ready"), sem("xn_ready"), sem("zeroed")
    hT_filled, hT_ready, scored, s_read, shifted, e_ready = (sem(n) for n in ("hT_filled", "hT_ready", "scored", "s_read", "shifted", "e_ready"))
    p_ready, pT_filled, pT_ready, y_ready, y_used = (sem(n) for n in ("p_ready", "pT_filled", "pT_ready", "y_ready", "y_used"))
    norm_chain, soft_chain = Chain(sem("norm_chain"), 2), Chain(sem("soft_chain"), 5)
    FB, SB, TB, YB = bank[0], bank[1], bank[2], bank[3]

    def group_x(t, g):
        return x[:, bass.ds(t * (GU * D) + g * D, D)]

    def norm_dve(dve, t):
        norm_chain.begin(t)
        for g in range(GU):
            i = nc.vector.bn_stats(stats[:, g, :], group_x(t, g))
        i.then_inc(norm_chain.sem, 1)
        dve.wait_ge(norm_chain.sem, norm_chain.next())
        dve.sem_inc(passed, 1)
        for g in range(GU):
            i = nc.vector.bn_aggr(mv[:, g, :], stats[:, g, :])
        i.then_inc(norm_chain.sem, 1)
        dve.wait_ge(norm_chain.sem, norm_chain.next())
        nc.vector.tensor_scalar(ve[:], mv[:, :, 1], LN_EPS, None, ALU.add).then_inc(var_ready, 1)
        dve.wait_ge(rstd_ready, t + 1)
        if some(t):
            dve.wait_ge(hT_filled, t)
        for g in range(GU):
            i = nc.vector.tensor_scalar(xn[:, g, :], group_x(t, g), mv[:, g, 0:1], rstd[:, g:g + 1], ALU.subtract, ALU.mult)
        i.then_inc(xn_ready, 1)
        norm_chain.end()

    def norm_pool(pool, t):
        pool.wait_ge(var_ready, t + 1)
        nc.gpsimd.tensor_tensor(out=rstd[:], in0=ve[:], in1=core.neghalf[:, 0:GU], op=ALU.pow).then_inc(rstd_ready, 1)

    def input_pe(pe, t):
        pe.wait_ge(xn_ready, t + 1)
        if some(t):
            pe.wait_ge(hT_ready, t)
        for c in range(C):
            for g in range(GU):
                i = nc.tensor.transpose(FB[:, c * UNIT + g * P:c * UNIT + (g + 1) * P], xn[:, g, c * P:(c + 1) * P], core.ident[:])
        i.then_inc(hT_filled, 1)

    def input_act(act, t):
        act.wait_ge(hT_filled, t + 1)
        if some(t):
            act.wait_ge(scored, t)
        nc.scalar.activation(hT[:].rearrange("p c t -> p (c t)"), FB[:], ACT.Copy).then_inc(hT_ready, 1)

    def scores_pe(pe, t, par):
        pe.wait_ge(hT_ready, t + 1)
        pe.wait_ge(ctx_in[par], (t // 2 + 1) * 32)
        if some(t):
            pe.wait_ge(s_read, t)
        for b in range(2 * GU):
            for c in range(C):
                i = nc.tensor.matmul(SB[64 * (b % 2):64 * (b % 2) + 64, (b // 2) * S:(b // 2 + 1) * S], hT[:, c, b * S:(b + 1) * S],
                                     ctxT[par][:, c, b * S:(b + 1) * S], start=(c == 0), stop=(c == C - 1))
        i.then_inc(scored, 1)

    def softmax_dve(dve, t):
        soft_chain.begin(t)
        kp, wide = keep[:, bass.ds(t * GU, GU), :], [P, GU, S]
        nc.vector.tensor_reduce(out=valid[:], in_=kp, axis=AX.X, op=ALU.max)
        nc.vector.tensor_scalar(neg[:], kp, 1.0, BIG, ALU.subtract, ALU.mult).then_inc(soft_chain.sem, 1)
        dve.wait_ge(soft_chain.sem, soft_chain.next())
        dve.wait_ge(scored, t + 1)
        nc.vector.scalar_tensor_tensor(out=pr[:], in0=SB[:, 0:GU * S].rearrange("p (g k) -> p g k", k=S), scalar=float(D) ** -0.5,
                                       in1=neg[:], op0=ALU.mult, op1=ALU.add).then_inc(s_read, 1)
        dve.wait_ge(s_read, t + 1)
        nc.vector.tensor_reduce(out=smax[:], in_=pr[:], axis=AX.X, op=ALU.max).then_inc(soft_chain.sem, 1)
        dve.wait_ge(soft_chain.sem, soft_chain.next())
        nc.vector.tensor_tensor(out=pr[:], in0=pr[:], in1=smax[:].unsqueeze(2).broadcast_to(wide), op=ALU.subtract).then_inc(shifted, 1)

    def exp_act(act, t):
        act.wait_ge(shifted, t + 1)
        nc.scalar.activation(pr[:], pr[:], ACT.Exp).then_inc(e_ready, 1)

    def normalize_dve(dve, t):
        soft_chain.begin(t, 2)
        dve.wait_ge(e_ready, t + 1)
        nc.vector.tensor_reduce(out=rsum[:], in_=pr[:], axis=AX.X, op=ALU.add).then_inc(soft_chain.sem, 1)
        dve.wait_ge(soft_chain.sem, soft_chain.next())
        nc.vector.reciprocal(rsum[:], rsum[:]).then_inc(soft_chain.sem, 1)
        dve.wait_ge(soft_chain.sem, soft_chain.next())
        nc.vector.tensor_tensor(out=rsum[:], in0=rsum[:], in1=valid[:], op=ALU.mult).then_inc(soft_chain.sem, 1)
        dve.wait_ge(soft_chain.sem, soft_chain.next())
        if some(t):
            dve.wait_ge(pT_filled, t)
        dve.wait_ge(zeroed, 1)
        for b in range(2):
            half = slice(64 * b, 64 * b + 64)
            i = nc.vector.tensor_tensor(out=pbd[half, :, 64 * b:64 * b + 64], in0=pr[half, :, :],
                                        in1=rsum[half, :].unsqueeze(2).broadcast_to([64, GU, S]), op=ALU.mult)
        i.then_inc(p_ready, 1)

    def transpose_pe(pe, t):
        pe.wait_ge(p_ready, t + 1)
        if some(t):
            pe.wait_ge(pT_ready, t)
        for g in range(GU):
            i = nc.tensor.transpose(TB[:, g * P:(g + 1) * P], pbd[:, g, :], core.ident[:])
        i.then_inc(pT_filled, 1)

    def transposed_act(act, t):
        act.wait_ge(pT_filled, t + 1)
        if some(t):
            act.wait_ge(y_ready, t)
        nc.scalar.activation(pT[:], TB[:, 0:UNIT], ACT.Copy).then_inc(pT_ready, 1)

    def readout_pe(pe, t, par):
        pe.wait_ge(pT_ready, t + 1)
        if some(t):
            pe.wait_ge(y_used, t)
        for g in range(GU):
            i = nc.tensor.matmul(YB[:, g * D:(g + 1) * D], pT[:, g * P:(g + 1) * P], ctx[par][:, g, :], start=True, stop=True)
        i.then_inc(y_ready, 1)

    def residual_dve(dve, t):
        dve.wait_ge(y_ready, t + 1)
        xt = x[:, bass.ds(t * (GU * D), GU * D)]
        nc.vector.tensor_tensor(out=xt, in0=YB[:], in1=xt, op=ALU.add).then_inc(y_used, 1)

    def load_ctx(sp, t, par):
        if some(t - 1):
            sp.wait_ge(y_ready, t - 1)
        sp.sem_inc(passed, 1)
        sp.dma_start(ctxT[par][:], args["ctxT"].rearrange("(c p) n -> p c n", p=P)[:, :, bass.ds(t * UNIT, UNIT)]).then_inc(ctx_in[par], 16)
        sp.dma_start(ctx[par][:], args["ctx"].rearrange("(g p) d -> p g d", p=P)[:, bass.ds(t * GU, GU), :]).then_inc(ctx_in[par], 16)

    def unit_pe(pe, t, par):
        scores_pe(pe, t, par)
        if not is_last(t):
            input_pe(pe, t + 1)
        transpose_pe(pe, t)
        readout_pe(pe, t, par)

    def unit_act(act, t, par):
        exp_act(act, t)
        if not is_last(t):
            input_act(act, t + 1)
        transposed_act(act, t)

    def unit_dve(dve, t, par):
        if not is_last(t):
            norm_dve(dve, t + 1)
        softmax_dve(dve, t)
        normalize_dve(dve, t)
        residual_dve(dve, t)

    def unit_pool(pool, t, par):
        if not is_last(t):
            norm_pool(pool, t + 1)

    with nc.Block() as block:
        @block.sync
        def _(sp):
            sp.dma_start(keep[:], args["keep"].rearrange("p (g k) -> p g k", k=S)).then_inc(weights_in, 16)
            load_ctx(sp, 0, 0)
            load_ctx(sp, 1, 1)
            with sp.Fori(1, NU // 2) as pair:
                load_ctx(sp, pair * 2, 0)
                load_ctx(sp, pair * 2 + 1, 1)

        @block.tensor
        def _(pe):
            input_pe(pe, 0)
            unit_loop(pe, unit_pe)

        @block.scalar
        def _(act):
            input_act(act, 0)
            unit_loop(act, unit_act)

        @block.vector
        def _(dve):
            dve.wait_ge(weights_in, 16)
            norm_dve(dve, 0)
            unit_loop(dve, unit_dve)

        @block.gpsimd
        def _(pool):
            nc.gpsimd.memset(pbd[:], 0.0).then_inc(zeroed, 1)
            norm_pool(pool, 0)
            unit_loop(pool, unit_pool)
    st.close()


def build_program(nc, args, stages):
    ctx = ExitStack()
    with ctx:
        core = Core(nc, ctx, args)
        load_block(core)
        if 0 in stages:
            head_attention_stage(core, "att8", quant=True)
        if 1 in stages:
            ffn_stage(core, "peer", "peer", "ln", blocks=16)
        if 2 in stages:
            linear_attention_stage(core)
        if 3 in stages:
            ffn_stage(core, "ffn4", "relu", "ln", blocks=8)
        if 4 in stages:
            memory_attention_stage(core)
        if 5 in stages:
            self_attention_stage(core)
            ffn_stage(core, "moe2a", "gated", "scratch", blocks=13, top_k=6)
            ffn_stage(core, "moe2b", "gated", "scratch", blocks=12, top_k=6, first=13)
        if 6 in stages:
            head_attention_stage(core, "att32", quant=False)
        if 7 in stages:
            ffn_stage(core, "moe3", "gated", "ln", blocks=16, top_k=2)
        store_block(core)


def lay_out(i):
    import numpy as np
    i = {k: np.asarray(v) for k, v in i.items()}
    c = np.ascontiguousarray
    a = {"x": i["x"].reshape(T, D)}
    a["ctx"] = i["ctx_2048"].reshape(T, D)
    for w in ("Wq", "Wg", "Wo", "Wkv"):
        a["l_" + w.lower() + "T"] = c(i["L1_xattn_" + w].T)
    a["bg"] = c(np.broadcast_to(i["L1_xattn_bg"], (P, D)))
    a["bdmask"] = (np.arange(P)[:, None] // 16 == np.arange(P)[None, :] // 16).astype(np.float32)
    a["ctxT"] = c(i["ctx_2048"].reshape(T, D).T)
    a["mask"] = i["mask_BxSxS2_ff0"].reshape(T, S)
    a["keep"] = c(np.repeat(i["mask_BxS2_bk0"], S, axis=0).reshape(NG, P, S).transpose(1, 0, 2).reshape(P, NG * S))
    a["hmask"] = (np.arange(P)[:, None] // 16 == np.arange(8)[None, :]).astype(np.float32)
    a["wq"], a["wo"] = i["L0_xattn_wq"], i["L0_xattn_wo"]
    a["wkT"], a["wvT"] = c(i["L0_xattn_wk"].T), c(i["L0_xattn_wv"].T)
    a["bk"] = c(i["L0_xattn_bk"].reshape(C, P).T)
    for w in ("bq", "bv", "bo"):
        a[w] = c(np.broadcast_to(i["L0_xattn_" + w], (P, D)))
    for w in ("wq", "wk", "wv", "wo", "wg"):
        a["z_" + w + "T"] = c(i["L3_xattn_" + w].T)
    a["norm_w"] = c(i["L3_xattn_norm_w"].reshape(C, P).T)
    a["p_wq"] = i["L0_ffn_Wq"]
    a["p_keys"] = c(i["L0_ffn_keys"].transpose(2, 3, 0, 1).reshape(P, 4, P))
    a["e_downT"] = c(i["L0_ffn_e_down"].T)
    a["e_up"] = i["L0_ffn_e_up"]
    a["up_q"] = c(i["L1_ffn_w_up_q"].T)
    a["up_s"] = c(np.repeat(i["L1_ffn_w_up_scale"].T, 64, axis=0))
    a["down_q"] = c(i["L1_ffn_w_down_q"].T)
    a["down_s"] = c(np.repeat(i["L1_ffn_w_down_scale"].T, 64, axis=0))
    a["up_aT"] = c(i["L1_ffn_w_up_lora_a"].T)
    a["up_b"] = i["L1_ffn_w_up_lora_b"]
    a["down_aT"] = c(i["L1_ffn_w_down_lora_a"].T)
    a["down_b"] = i["L1_ffn_w_down_lora_b"]
    a["bup"] = c(i["L1_ffn_b_up"].reshape(-1, P).T)
    a["bdn"] = c(np.broadcast_to(i["L1_ffn_b_down"], (P, D)))

    def selection(rows, per):
        s = np.zeros((32, rows), np.float32)
        s[np.minimum(np.arange(rows) // per, 16), np.arange(rows)] = 1.0
        return s

    for w in ("q", "k", "v", "o"):
        a["a_w" + w] = i["L2_ffn_w" + w]
    a["ln1"] = c(i["L2_ffn_ln1_w"].reshape(C, P).T)
    a["ln2"] = c(i["L2_ffn_ln2_w"].reshape(C, P).T)
    q = np.arange(P)
    a["causal"] = np.where((q[:, None] // S == q[None, :] // S) & (q[:, None] >= q[None, :]), 0.0, -1e9).astype(np.float32)
    rows = 25 * P

    def padded(v):
        out = np.zeros((rows, D), np.float32)
        out[:len(v)] = v
        return out

    a["moe2_wg"] = c(padded(np.concatenate([i["L2_ffn_eg_w"].reshape(-1, D), i["L2_ffn_sg_w"]])).T)
    a["moe2_wu"] = c(padded(np.concatenate([i["L2_ffn_eu_w"].reshape(-1, D), i["L2_ffn_su_w"]])).T)
    a["moe2_wd"] = padded(np.concatenate([i["L2_ffn_ed_w"].transpose(0, 2, 1).reshape(-1, D), i["L2_ffn_sd_w"].T]))
    a["moe2_gate"] = c(i["L2_ffn_gate_w"].T)
    a["moe2_sel"] = selection(rows, 176)
    a["moe3_wg"] = c(i["L3_ffn_wg"].transpose(1, 0, 2).reshape(D, -1))
    a["moe3_wu"] = c(i["L3_ffn_wu"].transpose(1, 0, 2).reshape(D, -1))
    a["moe3_wd"] = c(i["L3_ffn_wd"].reshape(-1, D))
    a["moe3_gate"] = c(i["L3_ffn_gate_w"].T)
    a["moe3_sel"] = selection(2048, 128)
    return a


def build(nc, inputs, stages=tuple(range(8))):
    arrays, args = {}, {}
    for name, v in lay_out(inputs).items():
        arrays[f"in_{name}_dram"] = v
        args[name] = nc.dram_tensor(f"in_{name}_dram", v.shape, mybir.dt.from_np(v.dtype), kind="ExternalInput").ap()
    args["t_scratch"] = nc.dram_tensor("t_scratch", (D, T), FP32, kind="Internal").ap()
    args["out"] = nc.dram_tensor("out_0_dram", (T, D), FP32, kind="ExternalOutput").ap()
    build_program(nc, args, stages)
    return arrays


def kernel(**inputs):
    import concourse.bacc as _bacc
    from concourse.bass_utils import run_bass_kernel_spmd as _run
    nc = _bacc.Bacc("TRN2", target_bir_lowering=False, num_devices=1)
    arrays = build(nc, inputs)
    r = _run(nc, [arrays], core_ids=[0])
    return r.results[0]["out_0_dram"].reshape(B, S, D)
```

```python
import concourse.bass as bass
from concourse import mybir
from contextlib import ExitStack

FP32 = mybir.dt.float32
FP32R = mybir.dt.float32r
BF16 = mybir.dt.bfloat16
U8 = mybir.dt.uint8
U32 = mybir.dt.uint32
I32 = mybir.dt.int32
ALU = mybir.AluOpType
ACT = mybir.ActivationFunctionType
AX = mybir.AxisListType

P = 128
B, S, D = 64, 64, 256
T = B * S
NG = T // P
C = D // P
TILE = 512
NT = T // TILE
GT = TILE // P
LN_EPS = 1e-5
MAGIC = 1.5 * 2.0 ** 23
BIG = 1e30


def some(n):
    return not isinstance(n, int) or n > 0


class Chain:

    def __init__(self, sem, per_tile):
        self.sem, self.per_tile, self.k = sem, per_tile, 0

    def begin(self, t, k=0):
        self.t, self.k = t, k

    def next(self):
        self.k += 1
        return self.t * self.per_tile + self.k

    def end(self):
        assert self.k == self.per_tile, (self.k, self.per_tile)


class Core:

    def __init__(self, nc, ctx, args):
        self.nc, self.args = nc, args
        self.x = ctx.enter_context(nc.sbuf_tensor("x", [P, NG * D], FP32))
        self.ident = ctx.enter_context(nc.sbuf_tensor("ident", [P, P], FP32))
        self.identb = ctx.enter_context(nc.sbuf_tensor("identb", [P, P], BF16))
        self.neghalf = ctx.enter_context(nc.sbuf_tensor("neghalf", [P, 16], FP32))
        self.x_in = ctx.enter_context(nc.semaphore("x_in"))
        self.bank = [ctx.enter_context(nc.psum_tensor(f"bank{i}", [P, 512], FP32)) for i in range(8)]


class Stage:

    def __init__(self, core, name):
        self.core, self.nc, self.name = core, core.nc, name
        self.ctx, self.sems = ExitStack(), []

    def sb(self, name, shape, dt=FP32):
        return self.ctx.enter_context(self.nc.sbuf_tensor(f"{self.name}_{name}", shape, dt))

    def passed(self):
        return self.sem("passed")

    def sem(self, name):
        s = self.ctx.enter_context(self.nc.semaphore(f"{self.name}_{name}"))
        self.sems.append(s)
        return s

    def close(self):
        with self.nc.Block() as block:
            @block.gpsimd
            def _(pool):
                for s in self.sems:
                    pool.sem_clear(s)
        self.ctx.close()


def load_block(core):
    nc = core.nc
    st = Stage(core, "init")
    zeroed, made = st.sem("zeroed"), st.sem("made")
    with nc.Block() as block:
        @block.sync
        def _(sp):
            for q in range(4):
                n = NG // 4
                sp.dma_start(core.x[:, q * n * D:(q + 1) * n * D].rearrange("p (g d) -> p g d", d=D),
                             core.args["x"][q * n * P:(q + 1) * n * P, :].rearrange("(g p) d -> p g d", p=P)).then_inc(core.x_in, 16)

        @block.gpsimd
        def _(pool):
            nc.gpsimd.memset(core.neghalf[:], -0.5).then_inc(zeroed, 1)
            nc.gpsimd.memset(core.ident[:], 0.0).then_inc(zeroed, 1)
            pool.wait_ge(zeroed, 2)
            nc.gpsimd.affine_select(out=core.ident[:], in_=core.ident[:], compare_op=ALU.not_equal, fill=1.0,
                                    base=0, pattern=[[-1, P]], channel_multiplier=1).then_inc(made, 1)
            pool.wait_ge(made, 1)
            nc.gpsimd.tensor_copy(core.identb[:], core.ident[:]).then_inc(made, 1)
    st.close()


def dequant_block(core, st, wgs, wds, bup, bdn, NB):
    nc, args, bank = core.nc, core.args, core.bank
    H = NB * P
    tmp = Stage(core, st.name + "_dq")
    gq, gs = tmp.sb("gq", [P, C, H], I32), tmp.sb("gs", [P, C, H])
    dq, ds = tmp.sb("dq", [P, NB, D], I32), tmp.sb("ds", [P, NB, D])
    ua, ub = tmp.sb("ua", [16, D]), tmp.sb("ub", [16, H])
    da, db = tmp.sb("da", [16, H]), tmp.sb("db", [16, D])
    wg, wd = tmp.sb("wg", [P, C, H]), tmp.sb("wd", [P, NB, D])
    hi_made = tmp.sem("hi_made")
    q_in, scaled, lora, added = tmp.sem("q_in"), tmp.sem("scaled"), tmp.sem("lora"), tmp.sem("added")
    loads = [(gq[:], args["up_q"].rearrange("(c p) h -> p c h", p=P)),
             (gs[:], args["up_s"].rearrange("(c p) h -> p c h", p=P)),
             (dq[:], args["down_q"].rearrange("(n p) d -> p n d", p=P)),
             (ds[:], args["down_s"].rearrange("(n p) d -> p n d", p=P)),
             (ua[:], args["up_aT"]), (ub[:], args["up_b"]), (da[:], args["down_aT"]), (db[:], args["down_b"]),
             (bup[:], args["bup"]), (bdn[:], args["bdn"])]
    parts = [(ua[:, c * P:(c + 1) * P], ub[:, n * 512:(n + 1) * 512], wg[:, c, n * 512:(n + 1) * 512])
             for c in range(C) for n in range(H // 512)]
    parts += [(da[:, n * P:(n + 1) * P], db[:], wd[:, n, :]) for n in range(NB)]
    with nc.Block() as block:
        @block.sync
        def _(sp):
            for out, in_ in loads:
                sp.dma_start(out, in_).then_inc(q_in, 16)

        @block.tensor
        def _(pe):
            pe.wait_ge(q_in, 16 * len(loads))
            for n, (rows, cols, target) in enumerate(parts):
                if n >= 4:
                    pe.wait_ge(added, n - 3)
                width = cols.shape[-1]
                nc.tensor.matmul(bank[n % 4][:, 0:width], rows, cols, start=True, stop=True).then_inc(lora, 1)

        @block.vector
        def _(dve):
            dve.wait_ge(q_in, 16 * len(loads))
            nc.vector.scalar_tensor_tensor(out=wg[:], in0=gq[:], scalar=7.5, in1=gs[:], op0=ALU.subtract, op1=ALU.mult)
            nc.vector.scalar_tensor_tensor(out=wd[:], in0=dq[:], scalar=7.5, in1=ds[:], op0=ALU.subtract,
                                           op1=ALU.mult).then_inc(scaled, 1)
            dve.wait_ge(scaled, 1)
            for n, (rows, cols, target) in enumerate(parts):
                dve.wait_ge(lora, n + 1)
                width = cols.shape[-1]
                nc.vector.tensor_tensor(out=target, in0=bank[n % 4][:, 0:width], in1=target, op=ALU.add).then_inc(added, 1)
            for n, (w, parts_) in enumerate(((wg, wgs), (wd, wds))):
                dve.wait_ge(hi_made, n + 1)
                nc.vector.tensor_tensor(out=parts_[1][:], in0=w[:], in1=parts_[0][:], op=ALU.subtract)

        @block.scalar
        def _(act):
            act.wait_ge(added, len(parts))
            nc.scalar.activation(wgs[0][:], wg[:], ACT.Copy).then_inc(hi_made, 1)
            nc.scalar.activation(wds[0][:], wd[:], ACT.Copy).then_inc(hi_made, 1)
    tmp.close()


def ffn_stage(core, name, kind, front_kind, blocks, top_k=0, first=0, store=False):
    nc, args, bank, x = core.nc, core.args, core.bank, core.x
    st = Stage(core, name)
    sb, sem = st.sb, st.sem
    NB = blocks
    H = NB * P
    E = 16
    gated, peer, relu = kind == "gated", kind == "peer", kind == "relu"
    ln = front_kind == "ln"

    split = gated or relu
    if split:
        wgs = [sb(n, [P, C, H], FP32R) for n in ("wg_hi", "wg_lo")]
        wus = [sb(n, [P, C, H], FP32R) for n in ("wu_hi", "wu_lo")] if gated else None
        wds = [sb(n, [P, NB, D], FP32R) for n in ("wd_hi", "wd_lo")]
        hTs = [sb(n, [P, 2, C, TILE], FP32R) for n in ("hT_hi", "hT_lo")]
        hhs = [sb(n, [P, 2, TILE], FP32R) for n in ("hh_hi", "hh_lo")]
        PARTS = ((0, 0), (0, 1), (1, 0))
        hi_ready, lo_ready, hT_hi_ready = sem("hi_ready"), sem("lo_ready"), sem("hT_hi_ready")
    else:
        wg = sb("wg", [P, C, H])
        wd = sb("wd", [P, NB, D])
        hT = sb("hT", [P, C, TILE])
    hTf2 = [sb(f"hTf{n}", [P, C, TILE]) for n in range(2 if peer else 1)]
    hh = sb("hh", [P, 2, TILE])
    a = sb("a", [P, 2, TILE])
    b = sb("b", [P, 2, TILE]) if gated else None
    G, U, CW, Y, F = bank[0:2], bank[2:4], bank[4], bank[5:7], bank[7]
    RING = [U[0], U[1], F] if peer else [F]
    R = len(RING)

    weights_in, out_done = sem("weights_in"), sem("out_done")
    g_ready, u_ready, cw_ready = sem("g_ready"), sem("u_ready"), sem("cw_ready")
    a_ready, b_ready, hh_ready, hh_used = sem("a_ready"), sem("b_ready"), sem("hh_ready"), sem("hh_used")
    passed = st.passed()
    y_used, hT_ready, hTf_ready = sem("y_used"), sem("hT_ready"), sem("hTf_ready")
    f_filled, f_emptied = sem("f_filled"), sem("f_emptied")
    if ln:
        xn = sb("xn", [P, GT, D])
        stats, mv = sb("stats", [P, GT, 6]), sb("mv", [P, GT, 2])
        ve, rstd = sb("ve", [P, GT]), sb("rstd", [P, GT])
        var_ready, rstd_ready, xn_ready = sem("var_ready"), sem("rstd_ready"), sem("xn_ready")
        ln_chain = Chain(sem("ln_chain"), 2)
    else:
        hTf_in = sem("hTf_in")
    NTR = C if ln else 0
    if gated:
        sel, gw = sb("sel", [64, H], FP32R), sb("gw", [P, C, E])
        shifted, pr, pm, cw = sb("shifted", [P, GT, E]), sb("pr", [P, GT, E]), sb("pm", [P, GT, E]), sb("cw", [P, GT, P])
        rmax, rsum, m8 = sb("rmax", [P, GT]), sb("rsum", [P, GT]), sb("m8", [P, GT, 8])
        cwTf, cwT_hi, cwT = sb("cwTf", [64, TILE]), sb("cwT_hi", [64, TILE], FP32R), sb("cwT", [64, 2, TILE], FP32R)
        e_ready, cw_done, cw_zeroed, cw_init, cwTf_ready = sem("e_ready"), sem("cw_done"), sem("cw_zeroed"), sem("cw_init"), sem("cwTf_ready")
        router_chain = Chain(sem("router_chain"), 9)
        NF = NTR + 2
    if relu:
        bup, bdn = sb("bup", [P, NB]), sb("bdn", [P, D])
        y_sum = sem("y_sum")
        NF = NTR
        dequant_block(core, st, wgs, wds, bup, bdn, NB)
    if peer:
        NH = 4
        wq, bdk, qTs = sb("wq", [P, C, NH * P]), sb("bdk", [P, NH, 256]), sb("qTs", [P, NH, TILE])
        sims = sb("sims", [P, 2, NH, 256])
        s8, f8, th = sb("s8", [P, NH, 2, 8]), sb("f8", [P, NH, 8]), sb("th", [P, NH])
        cand, wc, i1, past = sb("cand", [P, NH, 64]), sb("wc", [P, NH, 64]), sb("i1", [P, NH, 8], U32), sb("past", [P, NH, 8])
        rest = sb("rest", [P, 1])
        sums, wtab = sb("sums", [P, 2, H]), sb("wtab", [P, H])
        cwT_all = sb("cwT_all", [P, 2, NB, TILE])
        
        sum_ready, sum_used = sem("sum_ready"), sem("sum_used")
        w_ready, cwT_ready, bdk_zero = sem("w_ready"), sem("cwT_ready"), sem("bdk_zero")
        peer_chain = Chain(sem("peer_chain"), GT * (7 + 1 + 6))
        NS, NW = 2, H // 512
        NF = GT * (NS + NW)
        assert NF % R == 0

    if peer:
        IN_RING, in_filled, in_emptied, NIN = [CW], sem("in_filled"), sem("in_emptied"), NTR + NH
    else:
        IN_RING, in_filled, in_emptied, NIN = RING, f_filled, f_emptied, NF

    def is_last_tile(t):
        return isinstance(t, int) and t == NT - 1

    def group_x(t, g):
        return x[:, bass.ds(t * (GT * D) + g * D, D)]

    hTf = hTf2[0]

    def norm_dve(dve, t):
        ln_chain.begin(t)
        for g in range(GT):
            i = nc.vector.bn_stats(stats[:, g, :], group_x(t, g))
        i.then_inc(ln_chain.sem, 1)
        dve.wait_ge(ln_chain.sem, ln_chain.next())
        dve.sem_inc(passed, 1)
        for g in range(GT):
            i = nc.vector.bn_aggr(mv[:, g, :], stats[:, g, :])
        i.then_inc(ln_chain.sem, 1)
        dve.wait_ge(ln_chain.sem, ln_chain.next())
        nc.vector.tensor_scalar(ve[:], mv[:, :, 1], LN_EPS, None, ALU.add).then_inc(var_ready, 1)
        if some((t - 1) * NIN + NTR):
            dve.wait_ge(in_filled, (t - 1) * NIN + NTR)
        dve.wait_ge(rstd_ready, t + 1)
        for g in range(GT):
            i = nc.vector.tensor_scalar(xn[:, g, :], group_x(t, g), mv[:, g, 0:1], rstd[:, g:g + 1],
                                        ALU.subtract, ALU.mult)
        i.then_inc(xn_ready, 1)
        ln_chain.end()

    def norm_pool(pool, t):
        pool.wait_ge(var_ready, t + 1)
        nc.gpsimd.tensor_tensor(out=rstd[:], in0=ve[:], in1=core.neghalf[:, 0:GT], op=ALU.pow).then_inc(rstd_ready, 1)

    def input_bank(pe, t, k):
        if not peer:
            return front_bank(pe, t, k)
        if some(t * NIN + k):
            pe.wait_ge(in_emptied, t * NIN + k)
        return CW

    def front_bank(pe, t, k):
        if some(t * NF + k + 1 - R):
            pe.wait_ge(f_emptied, t * NF + k + 1 - R)
        return RING[k % R]

    def transposes_pe(pe, t):
        pe.wait_ge(xn_ready, t + 1)
        for c in range(C):
            F_ = input_bank(pe, t, c)
            for g in range(GT):
                i = nc.tensor.transpose(F_[:, g * P:(g + 1) * P], xn[:, g, c * P:(c + 1) * P], core.ident[:])
            i.then_inc(in_filled, 1)

    def transposes_act(act, t, par):
        hTf = hTf2[par if peer else 0]
        if some(t - 1 if peer else t):
            act.wait_ge(hT_ready, t - 1 if peer else t)
        for c in range(C):
            act.wait_ge(in_filled, t * NIN + c + 1)
            if split:
                nc.scalar.activation(hTs[0][:, par, c, :], IN_RING[c % len(IN_RING)][:], ACT.Copy)
            nc.scalar.activation(hTf[:, c, :], IN_RING[c % len(IN_RING)][:], ACT.Copy).then_inc(in_emptied, 1)

    def loaded_act(act, t, par):
        act.wait_ge(hTf_in, (t + 1) * 16)
        nc.scalar.activation(hTs[0][:, par, :, :], hTf[:], ACT.Copy).then_inc(hT_hi_ready, 1)

    def load_front_sp(sp, t):
        if some(t):
            sp.wait_ge(hT_ready, t)
        sp.dma_start(hTf[:], args["t_scratch"].rearrange("(c p) n -> p c n", p=P)[:, :, bass.ds(t * TILE, TILE)]).then_inc(hTf_in, 16)

    def hTf_wait(eng, t):
        if ln:
            eng.wait_ge(in_emptied, t * NIN + NTR)
        else:
            eng.wait_ge(hTf_in, (t + 1) * 16)

    def logits_pe(pe, t):
        hTf_wait(pe, t)
        F_ = front_bank(pe, t, NTR)
        for g in range(GT):
            for c in range(C):
                i = nc.tensor.matmul(F_[:, g * E:(g + 1) * E], hTf[:, c, g * P:(g + 1) * P], gw[:, c, :],
                                     start=(c == 0), stop=(c == C - 1))
        i.then_inc(f_filled, 1)

    def router_dve(dve, t):
        router_chain.begin(t)
        dve.wait_ge(f_filled, t * NF + NTR + 1)
        logits = F[:, 0:GT * E].rearrange("p (g e) -> p g e", e=E)
        wide = [P, GT, E]
        nc.vector.tensor_reduce(out=rmax[:], in_=logits, axis=AX.X, op=ALU.max).then_inc(router_chain.sem, 1)
        dve.wait_ge(router_chain.sem, router_chain.next())
        nc.vector.tensor_tensor(out=shifted[:], in0=logits, in1=rmax[:].unsqueeze(2).broadcast_to(wide),
                                op=ALU.subtract).then_inc(f_emptied, 1)
        dve.wait_ge(e_ready, t + 1)
        nc.vector.tensor_reduce(out=rsum[:], in_=pr[:], axis=AX.X, op=ALU.add).then_inc(router_chain.sem, 1)
        dve.wait_ge(router_chain.sem, router_chain.next())
        nc.vector.reciprocal(rmax[:], rsum[:]).then_inc(router_chain.sem, 1)
        dve.wait_ge(router_chain.sem, router_chain.next())
        nc.vector.tensor_tensor(out=pr[:], in0=pr[:], in1=rmax[:].unsqueeze(2).broadcast_to(wide), op=ALU.mult).then_inc(router_chain.sem, 1)
        dve.wait_ge(router_chain.sem, router_chain.next())
        dve.sem_inc(passed, 1)
        for g in range(GT):
            i = nc.vector.max(m8[:, g, :], pr[:, g, :])
        i.then_inc(router_chain.sem, 1)
        dve.wait_ge(router_chain.sem, router_chain.next())
        nc.vector.tensor_tensor(out=pm[:], in0=pr[:], in1=m8[:, :, top_k - 1:top_k].broadcast_to(wide), op=ALU.is_ge).then_inc(router_chain.sem, 1)
        dve.wait_ge(router_chain.sem, router_chain.next())
        nc.vector.tensor_tensor(out=pm[:], in0=pm[:], in1=pr[:], op=ALU.mult).then_inc(router_chain.sem, 1)
        dve.wait_ge(router_chain.sem, router_chain.next())
        nc.vector.tensor_reduce(out=rsum[:], in_=pm[:], axis=AX.X, op=ALU.add).then_inc(router_chain.sem, 1)
        dve.wait_ge(router_chain.sem, router_chain.next())
        nc.vector.reciprocal(rmax[:], rsum[:]).then_inc(router_chain.sem, 1)
        dve.wait_ge(router_chain.sem, router_chain.next())
        dve.wait_ge(cw_init, 2)
        if some((t - 1) * NF + NF):
            dve.wait_ge(f_filled, (t - 1) * NF + NF)
        nc.vector.tensor_tensor(out=cw[:, :, 32:32 + E], in0=pm[:], in1=rmax[:].unsqueeze(2).broadcast_to(wide), op=ALU.mult)
        nc.vector.tensor_tensor(out=cw[:, :, 0:E], in0=pm[:], in1=rmax[:].unsqueeze(2).broadcast_to(wide),
                                op=ALU.mult).then_inc(cw_done, 1)
        router_chain.end()

    def router_act(act, t):
        act.wait_ge(f_emptied, t * NF + NTR + 1)
        nc.scalar.activation(pr[:], shifted[:], ACT.Exp).then_inc(e_ready, 1)

    def cwT_pe(pe, t):
        pe.wait_ge(cw_done, t + 1)
        F_ = front_bank(pe, t, NF - 1)
        for g in range(GT):
            i = nc.tensor.transpose(F_[:, g * P:(g + 1) * P], cw[:, g, :], core.ident[:])
        i.then_inc(f_filled, 1)

    def cwT_act(act, t, par):
        act.wait_ge(f_filled, (t + 1) * NF)
        if some(t):
            act.wait_ge(hT_ready, t)
        nc.scalar.activation(cwT[0:32, par, :], F[0:32, :], ACT.Copy)
        nc.scalar.activation(cwT_hi[32:64, :], F[32:64, :], ACT.Copy)
        nc.scalar.activation(cwTf[32:64, :], F[32:64, :], ACT.Copy).then_inc(f_emptied, 1)

    def queries_pe(pe, t, par, heads):
        hTf = hTf2[par]
        hTf_wait(pe, t)
        for h in heads:
            F_ = input_bank(pe, t, NTR + h)
            for c in range(C):
                i = nc.tensor.matmul(F_[:], wq[:, c, h * P:(h + 1) * P], hTf[:, c, :], start=(c == 0), stop=(c == C - 1))
            i.then_inc(in_filled, 1)

    def queries_act(act, t, heads):
        for h in heads:
            act.wait_ge(in_filled, t * NIN + NTR + h + 1)
            nc.scalar.activation(qTs[:, h, :], CW[:], ACT.Copy).then_inc(in_emptied, 1)

    def first_of_group(g):
        return g * (NS + NW) - (NW if g else 0)

    def first_of_table(g):
        return (g + 1) * NS + g * NW + (NS if g < GT - 1 else 0)

    def scores_pe(pe, t, g):
        for n in range(NS):
            k = first_of_group(g) + n
            F_ = front_bank(pe, t, k)
            pe.wait_ge(in_emptied, (t + 1) * NIN)
            for h in (2 * n, 2 * n + 1):
                i = nc.tensor.matmul(F_[:, (h % 2) * 256:(h % 2 + 1) * 256], qTs[:, h, g * P:(g + 1) * P], bdk[:, h, :],
                                     start=True, stop=True)
            i.then_inc(f_filled, 1)

    def scores_act(act, t, g):
        n = t * GT + g - 1
        if some(n * NH):
            act.wait_ge(sum_ready, n * NH)
            act.wait_ge(w_ready, n)
        for n in range(NS):
            k = first_of_group(g) + n
            act.wait_ge(f_filled, t * NF + k + 1)
            nc.scalar.activation(sims[:, g % 2, 2 * n:2 * n + 2, :], RING[k % R][:].rearrange("p (h k) -> p h k", h=2),
                                 ACT.Copy).then_inc(f_emptied, 1)

    def pick_dve(dve, t, g):
        dve.wait_ge(f_emptied, t * NF + first_of_group(g) + NS)
        dve.sem_inc(passed, 1)
        for h in range(NH):
            for s in range(2):
                i = nc.vector.max(s8[:, h, s, :], sims[:, g % 2, h, s * P:(s + 1) * P])
        i.then_inc(peer_chain.sem, 1)
        dve.wait_ge(peer_chain.sem, peer_chain.next())
        dve.sem_inc(passed, 1)
        for h in range(NH):
            nc.vector.max_index(i1[:, h, :], s8[:, h, 0, :], sims[:, g % 2, h, 0:P])
        nc.vector.tensor_tensor(out=cand[:].rearrange("p h (i j) -> p h i j", j=8),
                                in0=s8[:, :, 0, :].unsqueeze(3).broadcast_to([P, NH, 8, 8]),
                                in1=s8[:, :, 1, :].unsqueeze(2).broadcast_to([P, NH, 8, 8]), op=ALU.add).then_inc(peer_chain.sem, 1)
        dve.wait_ge(peer_chain.sem, peer_chain.next())
        nc.vector.tensor_scalar(past[:], i1[:], float(H // P), None, ALU.is_ge)
        for h in range(NH):
            i = nc.vector.max(f8[:, h, :], cand[:, h, :])
        i.then_inc(peer_chain.sem, 1)
        dve.wait_ge(peer_chain.sem, peer_chain.next())
        nc.vector.tensor_scalar(th[:], f8[:, :, 7], 0.0, None, ALU.max).then_inc(peer_chain.sem, 1)
        dve.wait_ge(peer_chain.sem, peer_chain.next())
        for h in range(NH):
            i = nc.vector.scalar_tensor_tensor(out=wc[:, h, :], in0=cand[:, h, :], scalar=th[:, h:h + 1], in1=cand[:, h, :],
                                               op0=ALU.is_ge, op1=ALU.mult)
        i.then_inc(peer_chain.sem, 1)
        dve.wait_ge(peer_chain.sem, peer_chain.next())
        nc.vector.tensor_tensor(out=wc[:].rearrange("p h (i j) -> p h i j", j=8),
                                in0=wc[:].rearrange("p h (i j) -> p h i j", j=8),
                                in1=past[:].unsqueeze(3).broadcast_to([P, NH, 8, 8]), op=ALU.mult).then_inc(peer_chain.sem, 1)
        dve.wait_ge(peer_chain.sem, peer_chain.next())
        nc.vector.tensor_reduce(out=rest[:], in_=wc[:].rearrange("p h k -> p (h k)"), axis=AX.X, op=ALU.add).then_inc(peer_chain.sem, 1)
        dve.wait_ge(peer_chain.sem, peer_chain.next())

    def sum_pool(pool, t, g, h):
        n = (t * GT + g) * NH + h
        pool.wait_ge(f_emptied, t * NF + first_of_group(g) + NS)
        if some(n + 1 - 2):
            pool.wait_ge(sum_used, n + 1 - 2)
        nc.gpsimd.tensor_tensor(out=sums[:, h % 2, :].rearrange("p (a b) -> p a b", b=P),
                                in0=sims[:, g % 2, h, P:2 * P].unsqueeze(1).broadcast_to([P, NB, P]),
                                in1=sims[:, g % 2, h, 0:NB].unsqueeze(2).broadcast_to([P, NB, P]), op=ALU.add).then_inc(sum_ready, 1)

    def table_dve(dve, t, g, h):
        n = (t * GT + g) * NH + h
        dve.wait_ge(sum_ready, n + 1)
        if h == 0:
            if some(t * NF + first_of_table(g - 1) + NW if g else (t - 1) * NF + NF):
                dve.wait_ge(f_filled, t * NF + first_of_table(g - 1) + NW if g else (t - 1) * NF + NF)
        picked = sums[:, h % 2, :]
        nc.vector.scalar_tensor_tensor(out=wtab[:] if h == 0 else picked, in0=picked, scalar=th[:, h:h + 1], in1=picked,
                                       op0=ALU.is_ge, op1=ALU.mult).then_inc(peer_chain.sem, 1)
        dve.wait_ge(peer_chain.sem, peer_chain.next())
        if h:
            nc.vector.tensor_tensor(out=wtab[:], in0=wtab[:], in1=picked, op=ALU.add).then_inc(peer_chain.sem, 1)
            dve.wait_ge(peer_chain.sem, peer_chain.next())
        nc.vector.sem_inc(sum_used, 1)
        if h == NH - 1:
            nc.vector.tensor_tensor(out=wtab[:, H - 1:H], in0=wtab[:, H - 1:H], in1=rest[:], op=ALU.add).then_inc(w_ready, 1)

    def table_pe(pe, t, g):
        pe.wait_ge(w_ready, t * GT + g + 1)
        for n in range(NW):
            F_ = front_bank(pe, t, first_of_table(g) + n)
            for j in range(4):
                blk = 4 * n + j
                i = nc.tensor.transpose(F_[:, j * P:(j + 1) * P], wtab[:, blk * P:(blk + 1) * P], core.ident[:])
            i.then_inc(f_filled, 1)

    def table_act(act, t, par, g):
        for n in range(NW):
            k = first_of_table(g) + n
            act.wait_ge(f_filled, t * NF + k + 1)
            dst = cwT_all[:, par, 4 * n:4 * n + 4, g * P:(g + 1) * P]
            nc.scalar.activation(dst, RING[k % R][:].rearrange("p (b t) -> p b t", t=P), ACT.Copy).then_inc(f_emptied, 1)

    def same_buffer(j):
        return 1 if NB % 2 and j == 0 else 2

    def projected(out, ws, par, j):
        for n, (pw, ph) in enumerate(PARTS):
            for c in range(C):
                i = nc.tensor.matmul(out, ws[pw][:, c, j * P:(j + 1) * P], hTs[ph][:, par, c, :],
                                     start=(n == 0 and c == 0), stop=(n == len(PARTS) - 1 and c == C - 1))
        return i

    def down_pe(pe, t, j):
        pe.wait_ge(lo_ready if split else hh_ready, t * NB + j + 1)
        if j == 0:
            if some(t):
                pe.wait_ge(y_used, t)
        for g in range(GT):
            if split:
                for n, (ph, pw) in enumerate(PARTS):
                    i = nc.tensor.matmul(Y[g // 2][:, (g % 2) * D:(g % 2 + 1) * D], hhs[ph][:, j % 2, g * P:(g + 1) * P],
                                         wds[pw][:, j, :], start=(j == 0 and g % 2 == 0 and n == 0),
                                         stop=(j == NB - 1 and n == len(PARTS) - 1), skip_group_check=True)
            else:
                i = nc.tensor.matmul(Y[g // 2][:, (g % 2) * D:(g % 2 + 1) * D], hh[:, j % 2, g * P:(g + 1) * P], wd[:, j, :],
                                     start=(j == 0 and g % 2 == 0), stop=(j == NB - 1), skip_group_check=True)
        i.then_inc(hh_used, 1)

    def block_pe(pe, t, par, j, before):
        n = t * NB + j + 1
        if peer and is_first(t) and j == 0:
            pe.wait_ge(tables_in, 32)
        if gated and is_first(t) and j % QB == 0:
            pe.wait_ge(w_lo_made, (j // QB + 1) * (len(raws) - 1))
            pe.wait_ge(w_hi_made, (j // QB + 1) * len(raws))
        if j == 0:
            pe.wait_ge(hT_ready, t + 1)
        if some(n - same_buffer(j)):
            pe.wait_ge(hh_ready if relu else a_ready, n - same_buffer(j))
        if split:
            projected(G[j % 2][:], wgs, par, j).then_inc(g_ready, 1)
        else:
            for c in range(C):
                i = nc.tensor.matmul(G[j % 2][:], wg[:, c, j * P:(j + 1) * P], hT[:, c, :], start=(c == 0), stop=(c == C - 1))
            i.then_inc(g_ready, 1)
        if gated:
            if some(n - same_buffer(j)):
                pe.wait_ge(b_ready, n - same_buffer(j))
            projected(U[j % 2][:], wus, par, j).then_inc(u_ready, 1)
            if some(n - 1):
                pe.wait_ge(hh_ready, n - 1)
            nc.tensor.matmul(CW[:], sel[:, j * P:(j + 1) * P], cwT[:, par, :], start=True, stop=True).then_inc(cw_ready, 1)
        if before is not None:
            down_pe(pe, *before)

    def block_act(act, t, j):
        n = t * NB + j + 1
        act.wait_ge(g_ready, n)
        if relu:
            if some(n - same_buffer(j)):
                act.wait_ge(hh_used, n - same_buffer(j))
            nc.scalar.activation(hhs[0][:, j % 2, :], G[j % 2][:], ACT.Relu, bias=bup[:, j:j + 1]).then_inc(hi_ready, 1)
            if some(n - same_buffer(j)):
                act.wait_ge(lo_ready, n - same_buffer(j))
            nc.scalar.activation(hh[:, j % 2, :], G[j % 2][:], ACT.Relu, bias=bup[:, j:j + 1]).then_inc(hh_ready, 1)
        else:
            if some(n - same_buffer(j)):
                act.wait_ge(b_ready if gated else hh_ready, n - same_buffer(j))
            nc.scalar.activation(a[:, j % 2, :], G[j % 2][:], ACT.Silu).then_inc(a_ready, 1)
        if gated:
            act.wait_ge(hh_ready, n)
            if some(n - same_buffer(j)):
                act.wait_ge(hh_used, n - same_buffer(j))
            nc.scalar.activation(hhs[0][:, j % 2, :], hh[:, j % 2, :], ACT.Copy).then_inc(hi_ready, 1)

    def block_pool(pool, t, j):
        n = t * NB + j + 1
        pool.wait_ge(hh_ready, n)
        pool.wait_ge(hi_ready, n)
        if some(n - same_buffer(j)):
            pool.wait_ge(hh_used, n - same_buffer(j))
        nc.gpsimd.tensor_tensor(out=hhs[1][:, j % 2, :], in0=hh[:, j % 2, :], in1=hhs[0][:, j % 2, :],
                                op=ALU.subtract).then_inc(lo_ready, 1)

    def block_dve(dve, t, par, j):
        n = t * NB + j + 1
        if peer and j == NB - 1 and not (isinstance(t, int) and t == NT - 1):
            hand_over_dve(dve, t + 1, 1 - par)
        if gated:
            dve.wait_ge(a_ready, n)
            dve.wait_ge(u_ready, n)
            if some(n - same_buffer(j)):
                dve.wait_ge(hh_ready, n - same_buffer(j))
            nc.vector.tensor_tensor(out=b[:, j % 2, :], in0=a[:, j % 2, :], in1=U[j % 2][:], op=ALU.mult).then_inc(b_ready, 1)
            dve.wait_ge(b_ready, n)
            dve.wait_ge(cw_ready, n)
            if some(n - same_buffer(j)):
                dve.wait_ge(lo_ready, n - same_buffer(j))
            nc.vector.tensor_tensor(out=hh[:, j % 2, :], in0=b[:, j % 2, :], in1=CW[:], op=ALU.mult).then_inc(hh_ready, 1)
        if peer:
            if j == 0:
                dve.wait_ge(f_emptied, (t + 1) * NF)
            dve.wait_ge(a_ready, n)
            if some(n - same_buffer(j)):
                dve.wait_ge(hh_used, n - same_buffer(j))
            nc.vector.tensor_tensor(out=hh[:, j % 2, :], in0=a[:, j % 2, :], in1=cwT_all[:, par, j, :], op=ALU.mult).then_inc(hh_ready, 1)

    def hand_over_dve(dve, t, par):
        hTf_wait(dve, t)
        if some(t * NB):
            dve.wait_ge(g_ready, t * NB)
        nc.vector.tensor_copy(hT[:], hTf2[par][:]).then_inc(hT_ready, 1)

    def low_dve(dve, t, par):
        if not ln:
            dve.wait_ge(hT_hi_ready, t + 1)
        if NF:
            dve.wait_ge(f_emptied, (t + 1) * NF)
        if gated:
            nc.vector.tensor_tensor(out=cwT[32:64, par, :], in0=cwTf[32:64, :], in1=cwT_hi[32:64, :], op=ALU.subtract)
        nc.vector.tensor_tensor(out=hTs[1][:, par, :, :], in0=hTf[:], in1=hTs[0][:, par, :, :],
                                op=ALU.subtract).then_inc(hT_ready, 1)

    def residual_dve(dve, t):
        dve.wait_ge(hh_used, (t + 1) * NB)
        xt = x[:, bass.ds(t * (GT * D), GT * D)]
        half = GT * D // 2
        for n in range(2):
            xt = x[:, bass.ds(t * (GT * D) + n * half, half)]
            i = nc.vector.tensor_tensor(out=xt, in0=Y[n][:], in1=xt, op=ALU.add)
        if relu:
            i.then_inc(y_sum, 1)
            dve.wait_ge(y_sum, t + 1)
            xt = x[:, bass.ds(t * (GT * D), GT * D)].rearrange("p (g d) -> p g d", d=D)
            i = nc.vector.tensor_tensor(out=xt, in0=xt, in1=bdn[:].unsqueeze(1).broadcast_to([P, GT, D]), op=ALU.add)
        i.then_inc(y_used, 1)

    NORM, TRANS, LOGITS, ROUTER, WEIGHTS, LOW = 0, 3, 4, 5, 8, 9 if gated else 4
    PRE_NORM, PRE_TRANS, PRE_QUERIES, PRE_SCORES = 4, 6, {10: (0, 1), 12: (2, 3)}, 15
    SCORES = {2: 1, 6: 2, 9: 3}
    PICK = {0: 0, 4: 1, 8: 2, 11: 3}
    TABLE = {0: [(0, 0)], 1: [(0, 1)], 2: [(0, 2)], 3: [(0, 3)], 4: [(1, 0)], 5: [(1, 1)], 6: [(1, 2)],
             7: [(1, 3)], 8: [(2, 0)], 9: [(2, 1)], 10: [(2, 2), (2, 3)], 11: [(3, 0)], 12: [(3, 1)],
             13: [(3, 2)], 14: [(3, 3)]}
    TURN = {4: 0, 8: 1, 11: 2, 15: 3}

    def front_pe(pe, t, j):
        if ln and not peer and j == TRANS:
            transposes_pe(pe, t)
        if gated and j == LOGITS:
            logits_pe(pe, t)
        if gated and j == WEIGHTS:
            cwT_pe(pe, t)
        if peer and j in SCORES:
            scores_pe(pe, t, SCORES[j])
        if peer and j in TURN:
            table_pe(pe, t, TURN[j])

    def pre_pe(pe, t, par, j):
        if j == PRE_TRANS:
            transposes_pe(pe, t)
        if j in PRE_QUERIES:
            queries_pe(pe, t, par, PRE_QUERIES[j])
        if j == PRE_SCORES:
            scores_pe(pe, t, 0)

    def front_act(act, t, par, j):
        if not peer and j == TRANS:
            if ln:
                transposes_act(act, t, par)
            else:
                loaded_act(act, t, par)
        if gated and j == ROUTER:
            router_act(act, t)
        if gated and j == WEIGHTS:
            cwT_act(act, t, par)
        if peer and j in SCORES:
            scores_act(act, t, SCORES[j])
        if peer and j in TURN:
            table_act(act, t, par, TURN[j])

    def pre_act(act, t, par, j):
        if j == PRE_TRANS:
            transposes_act(act, t, par)
        if j in PRE_QUERIES:
            queries_act(act, t, PRE_QUERIES[j])
        if j == PRE_SCORES:
            scores_act(act, t, 0)

    def front_dve(dve, t, par, j):
        if ln and not peer and j == NORM:
            norm_dve(dve, t)
        if gated and j == ROUTER:
            router_dve(dve, t)
        if split and j == LOW:
            low_dve(dve, t, par)
        if peer and j in PICK:
            if PICK[j] == 0:
                peer_chain.begin(t)
            pick_dve(dve, t, PICK[j])
        if peer:
            for g, h in TABLE.get(j, []):
                table_dve(dve, t, g, h)
                if (g, h) == (GT - 1, NH - 1):
                    peer_chain.end()

    def pre_dve(dve, t, par, j):
        if j == PRE_NORM:
            norm_dve(dve, t)

    def front_pool(pool, t, j):
        if ln and not peer and j == NORM:
            norm_pool(pool, t)
        if peer:
            for g, h in TABLE.get(j, []):
                sum_pool(pool, t, g, h)

    def pre_pool(pool, t, j):
        if j == PRE_NORM:
            norm_pool(pool, t)

    loads = []
    if peer:
        tables_in = sem("tables_in")
        loads = [(wq[:], args["p_wq"].rearrange("(c p) h -> p c h", p=P))]
    QB = 4
    QUADS = -(-NB // QB)
    if gated:
        loads = [(gw[:], args[name[:4] + "_gate"].rearrange("(c p) e -> p c e", p=P))]
        raws = [sb(f"raw{n}", [P, QB * P]) for n in range(2 * C)] + [sb("raw_wd", [P, QB, D]), sb("raw_sel", [64, QB * P])]
        raw_in = [sem(f"raw_in{n}") for n in range(len(raws))]
        w_hi_made, w_lo_made = sem("w_hi_made"), sem("w_lo_made")

    def quad_parts(quad):
        n0, n1 = quad * QB, min(quad * QB + QB, NB)
        cols, src_cols = slice(n0 * P, n1 * P), slice((first + n0) * P, (first + n1) * P)
        parts = [(args[f"{name[:4]}_{n}"][c * P:(c + 1) * P, src_cols], raws[k * C + c][:, 0:(n1 - n0) * P],
                  w[0][:, c, cols], w[1][:, c, cols]) for k, (n, w) in enumerate((("wg", wgs), ("wu", wus))) for c in range(C)]
        parts.append((args[name[:4] + "_wd"][src_cols, :].rearrange("(n p) d -> p n d", p=P), raws[2 * C][:, 0:n1 - n0, :],
                      wds[0][:, n0:n1, :], wds[1][:, n0:n1, :]))
        parts.append((args[name[:4] + "_sel"][:, src_cols], raws[2 * C + 1][:, 0:(n1 - n0) * P], sel[:, cols], None))
        return parts

    def load_quad_sp(sp, quad):
        for n, (src, raw, hi, lo) in enumerate(quad_parts(quad)):
            if quad:
                if lo is None:
                    sp.wait_ge(w_hi_made, quad * len(raws))
                else:
                    sp.wait_ge(w_lo_made, (quad - 1) * (len(raws) - 1) + n + 1)
            sp.dma_start(raw, src).then_inc(raw_in[n], 16)

    def split_act(act, quad):
        for n, (src, raw, hi, lo) in enumerate(quad_parts(quad)):
            act.wait_ge(raw_in[n], 16 * (quad + 1))
            nc.scalar.activation(hi, raw, ACT.Copy).then_inc(w_hi_made, 1)

    def split_dve(dve, quad):
        for n, (src, raw, hi, lo) in enumerate(quad_parts(quad)):
            if lo is not None:
                dve.wait_ge(w_hi_made, quad * len(raws) + n + 1)
                nc.vector.tensor_tensor(out=lo, in0=raw, in1=hi, op=ALU.subtract).then_inc(w_lo_made, 1)

    def next_quad(t, j):
        quad = j // QB + 1
        return quad if gated and is_first(t) and j % QB == 0 and quad < QUADS else None

    with nc.Block() as block:
        @block.sync
        def _(sp):
            for out, in_ in loads:
                sp.dma_start(out, in_).then_inc(weights_in, 16)
            if peer:
                sp.wait_ge(bdk_zero, 1)
                for s in range(2):
                    sp.dma_start(bdk[64 * s:64 * s + 64, :, P * s:P * (s + 1)],
                                 args["p_keys"][64 * s:64 * s + 64, :, :]).then_inc(weights_in, 16)
                sp.dma_start(wg[:], args["e_downT"].rearrange("(c p) h -> p c h", p=P)).then_inc(tables_in, 16)
                sp.dma_start(wd[:], args["e_up"].rearrange("(n p) d -> p n d", p=P)).then_inc(tables_in, 16)
            if not ln:
                load_front_sp(sp, 0)
            if gated:
                load_quad_sp(sp, 0)
                load_quad_sp(sp, 1)
            if not ln:
                load_front_sp(sp, 1)
            if gated:
                for quad in range(2, QUADS):
                    load_quad_sp(sp, quad)
            if not ln:
                with sp.Fori(2, NT) as t:
                    load_front_sp(sp, t)
            if store:
                with sp.Fori(0, NT) as t:
                    sp.wait_ge(y_used, t + 1)
                    sp.dma_start(args["out"].rearrange("(g p) d -> p g d", p=P)[:, bass.ds(t * GT, GT), :],
                                 x[:, bass.ds(t * (GT * D), GT * D)].rearrange("p (g d) -> p g d", d=D)).then_inc(out_done, 16)
                sp.wait_ge(out_done, 16 * NT)

        n_in = 16 * (len(loads) + (2 if peer else 0))

        def all_tiles(eng, tile):
            tile(0, 0)
            with eng.Fori(0, (NT - 4) // 2) as pair:
                tile(pair * 2 + 1, 1)
                tile(pair * 2 + 2, 0)
            for t in range(NT - 3, NT):
                tile(t, t % 2)

        def has_pre(t):
            return peer and not (isinstance(t, int) and t >= NT - 2)

        @block.tensor
        def _(pe):
            if n_in:
                pe.wait_ge(weights_in, n_in)
            if peer:
                for j in range(NB):
                    pre_pe(pe, 0, 0, j)
            for j in range(NB):
                front_pe(pe, 0, j)
                if peer:
                    pre_pe(pe, 1, 1, j)

            def tile(t, par):
                for j in range(NB):
                    block_pe(pe, t, par, j, (t, j - 1) if j else None if is_first(t) else (t - 1, NB - 1))
                    if not is_last_tile(t):
                        front_pe(pe, t + 1, j)
                    if has_pre(t):
                        pre_pe(pe, t + 2, par, j)

            all_tiles(pe, tile)
            down_pe(pe, NT - 1, NB - 1)

        @block.scalar
        def _(act):
            if peer:
                for j in range(NB):
                    pre_act(act, 0, 0, j)
            for j in range(NB):
                front_act(act, 0, 0, j)
                if peer:
                    pre_act(act, 1, 1, j)

            def tile(t, par):
                for j in range(NB):
                    if next_quad(t, j):
                        split_act(act, next_quad(t, j))
                    block_act(act, t, j)
                    if not is_last_tile(t):
                        front_act(act, t + 1, 1 - par, j)
                    if has_pre(t):
                        pre_act(act, t + 2, par, j)

            if gated:
                split_act(act, 0)
            all_tiles(act, tile)

        @block.vector
        def _(dve):
            if peer:
                for j in range(NB):
                    pre_dve(dve, 0, 0, j)
            for j in range(NB):
                front_dve(dve, 0, 0, j)
                if peer:
                    pre_dve(dve, 1, 1, j)
            if peer:
                hand_over_dve(dve, 0, 0)

            def tile(t, par):
                for j in range(NB):
                    if next_quad(t, j):
                        split_dve(dve, next_quad(t, j))
                    early = peer and j == 0
                    if early and not is_last_tile(t):
                        front_dve(dve, t + 1, 1 - par, j)
                    block_dve(dve, t, par, j)
                    if j == 0 and not is_first(t):
                        residual_dve(dve, t - 1)
                    if not early and not is_last_tile(t):
                        front_dve(dve, t + 1, 1 - par, j)
                    if has_pre(t):
                        pre_dve(dve, t + 2, par, j)

            if gated:
                split_dve(dve, 0)
            all_tiles(dve, tile)
            residual_dve(dve, NT - 1)

        @block.gpsimd
        def _(pool):
            if peer:
                nc.gpsimd.memset(bdk[:], 0.0).then_inc(bdk_zero, 1)
            if gated:
                nc.gpsimd.memset(cw[:], 0.0).then_inc(cw_zeroed, 1)
                pool.wait_ge(cw_zeroed, 1)
                for n in range(2):
                    nc.gpsimd.memset(cw[:, :, 32 * n + E:32 * n + E + 1], 1.0).then_inc(cw_init, 1)
            if peer:
                for j in range(NB):
                    pre_pool(pool, 0, j)
            for j in range(NB):
                front_pool(pool, 0, j)
                if peer:
                    pre_pool(pool, 1, j)

            def tile(t, par):
                for j in range(NB):
                    if split:
                        block_pool(pool, t, j)
                    if not is_last_tile(t):
                        front_pool(pool, t + 1, j)
                    if has_pre(t):
                        pre_pool(pool, t + 2, j)

            all_tiles(pool, tile)
    st.close()


def self_attention_stage(core):
    nc, args, bank, x = core.nc, core.args, core.bank, core.x
    st = Stage(core, "mha")
    sb, sem = st.sb, st.sem
    NH, HD = 16, 128
    SCALE = float(HD) ** -0.5
    EPS = 1e-6
    QUAD = 4

    wqs, wks = ([sb(f"{n}_{part}", [P, C, NH * HD], FP32R) for part in ("hi", "lo")] for n in ("wq", "wk"))
    wv = sb("wv", [P, C, NH * HD])
    raw = sb("raw", [P, 2 * C, QUAD * HD])
    hTs = [sb(n, [P, C, TILE], FP32R) for n in ("hT_hi", "hT_lo")]
    wo = sb("wo", [P, NH, D])
    ln1, ln2, causal = sb("ln1", [P, C]), sb("ln2", [P, C]), sb("causal", [P, P])
    hT, hTf = sb("hT", [P, C, TILE]), sb("hTf", [P, C, TILE])
    xr = sb("xr", [P, GT, D])
    stats, mv, mvb = sb("stats", [P, GT, 6]), sb("mv", [P, GT, 2]), sb("mvb", [P, GT, 2])
    ve, rstd, rstdb, ms, r1, rr = (sb(n, [P, GT]) for n in ("ve", "rstd", "rstdb", "ms", "r1", "rr"))
    qs, ks = sb("qs", [P, 2, TILE]), sb("ks", [P, 2, TILE])
    vs = sb("vs", [P, 2, GT, QUAD * HD])
    pr = sb("pr", [P, 2, GT, P])
    pT, oT = sb("pT", [P, 2, TILE]), sb("oT", [P, 2, TILE])
    smax, ssum = sb("smax", [P, GT]), sb("ssum", [P, GT])
    x1 = sb("x1", [P, GT, D])
    stats2, mv2 = sb("stats2", [P, GT, 6]), sb("mv2", [P, GT, 2])
    ms2, r2 = sb("ms2", [P, GT]), sb("r2", [P, GT])
    tT = sb("tT", [P, C, TILE])
    Q, K, V, Sc, PT, O, Y = bank[0], bank[1], bank[2], bank[3], bank[4], bank[5], bank[6:8]

    weights_in, passed = sem("weights_in"), st.passed()
    raw_in, wv_in, wo_in = [sem(f"raw_in{n}") for n in range(2 * C)], [sem(f"wv_in{n}") for n in range(NH // QUAD)], sem("wo_in")
    hi_made, lo_made, hi_handed = sem("hi_made"), sem("lo_made"), sem("hi_handed")
    var_ready, rstd_ready, ms_ready, r1_ready, xr_ready = (sem(n) for n in ("var_ready", "rstd_ready", "ms_ready", "r1_ready", "xr_ready"))
    v_filled, v_emptied = sem("v_filled"), sem("v_emptied")
    hT_ready = sem("hT_ready")
    q_ready, k_ready, qs_ready, ks_ready = sem("q_ready"), sem("k_ready"), sem("qs_ready"), sem("ks_ready")
    s_ready, s_read, e_ready, p_ready = sem("s_ready"), sem("s_read"), sem("e_ready"), sem("p_ready")
    pT_ready, pTs_ready, o_ready, oT_ready, out_done = (sem(n) for n in ("pT_ready", "pTs_ready", "o_ready", "oT_ready", "out_done"))
    shifted = sem("shifted")
    y_used, ms2_ready, r2_ready, tn_ready, stored = (sem(n) for n in ("y_used", "ms2_ready", "r2_ready", "tn_ready", "stored"))
    norm_chain, soft_chain, tail_chain = Chain(sem("norm_chain"), 3), Chain(sem("soft_chain"), NH * 4), Chain(sem("tail_chain"), 6)

    ms_eps, r1_raw = sem("ms_eps"), sem("r1_raw")
    f_filled, f_emptied = sem("f_filled"), sem("f_emptied")
    t_filled, t_emptied = sem("t_filled"), sem("t_emptied")

    def group_x(t, g):
        return x[:, bass.ds(t * (GT * D) + g * D, D)]

    TAIL_DVE, TAIL, FRONT = 3, 5, 9

    def front_dve(dve, t):
        norm_chain.begin(t)
        for g in range(GT):
            i = nc.vector.bn_stats(stats[:, g, :], group_x(t, g))
        i.then_inc(norm_chain.sem, 1)
        dve.wait_ge(norm_chain.sem, norm_chain.next())
        dve.sem_inc(passed, 1)
        for g in range(GT):
            i = nc.vector.bn_aggr(mv[:, g, :], stats[:, g, :])
        i.then_inc(norm_chain.sem, 1)
        dve.wait_ge(norm_chain.sem, norm_chain.next())
        nc.vector.tensor_scalar(ve[:], mv[:, :, 1], LN_EPS, None, ALU.add).then_inc(var_ready, 1)
        dve.wait_ge(rstd_ready, t + 1)
        nc.vector.tensor_tensor(out=ms[:], in0=rstd[:], in1=rstd[:], op=ALU.mult).then_inc(norm_chain.sem, 1)
        dve.wait_ge(norm_chain.sem, norm_chain.next())
        nc.vector.tensor_tensor(out=ms[:], in0=ms[:], in1=mv[:, :, 1], op=ALU.mult).then_inc(ms_ready, 1)
        dve.wait_ge(r1_ready, t + 1)
        if some(t * C):
            dve.wait_ge(f_filled, t * C)
        for g in range(GT):
            i = nc.vector.tensor_scalar(xr[:, g, :], group_x(t, g), mv[:, g, 0:1], rr[:, g:g + 1], ALU.subtract, ALU.mult)
        i.then_inc(xr_ready, 1)
        norm_chain.end()

    def front_pool(pool, t):
        pool.wait_ge(var_ready, t + 1)
        nc.gpsimd.tensor_tensor(out=rstd[:], in0=ve[:], in1=core.neghalf[:, 0:GT], op=ALU.pow).then_inc(rstd_ready, 1)
        pool.wait_ge(ms_ready, t + 1)
        pool.sem_inc(passed, 1)
        nc.gpsimd.tensor_scalar(ms[:], ms[:], EPS, None, ALU.add).then_inc(ms_eps, 1)
        pool.wait_ge(ms_eps, t + 1)
        nc.gpsimd.tensor_tensor(out=r1[:], in0=ms[:], in1=core.neghalf[:, 0:GT], op=ALU.pow).then_inc(r1_raw, 1)
        pool.wait_ge(r1_raw, t + 1)
        nc.gpsimd.tensor_tensor(out=rr[:], in0=r1[:], in1=rstd[:], op=ALU.mult).then_inc(r1_ready, 1)

    def front_pe(pe, t):
        pe.wait_ge(xr_ready, t + 1)
        if some((t - 1) * NH + FRONT + 1):
            pe.wait_ge(v_emptied, (t - 1) * NH + FRONT + 1)
        for c in range(C):
            if some(t * C + c):
                pe.wait_ge(f_emptied, t * C + c)
            for g in range(GT):
                i = nc.tensor.transpose(V[:, g * P:(g + 1) * P], xr[:, g, c * P:(c + 1) * P], core.ident[:])
            i.then_inc(f_filled, 1)

    def front_act(act, t):
        if some(t):
            act.wait_ge(hT_ready, t)
        for c in range(C):
            act.wait_ge(f_filled, t * C + c + 1)
            nc.scalar.activation(hTf[:, c, :], V[:], ACT.Copy, scale=ln1[:, c:c + 1]).then_inc(f_emptied, 1)

    def hand_over_dve(dve, t):
        dve.wait_ge(f_emptied, (t + 1) * C)
        if some(t * NH):
            dve.wait_ge(v_filled, t * NH)
        if some(t * NH):
            dve.wait_ge(k_ready, t * NH)
        nc.vector.tensor_copy(hTs[0][:], hTf[:]).then_inc(hi_handed, 1)
        nc.vector.tensor_copy(hT[:], hTf[:])
        dve.wait_ge(hi_handed, t + 1)
        nc.vector.tensor_tensor(out=hTs[1][:], in0=hTf[:], in1=hTs[0][:], op=ALU.subtract).then_inc(hT_ready, 1)

    def keep_stats_dve(dve, t):
        nc.vector.tensor_copy(mvb[:], mv[:])
        nc.vector.tensor_copy(rstdb[:], rstd[:]).then_inc(mvb_ready, 1)

    mvb_ready = sem("mvb_ready")

    SPLIT = [(w, c) for w in (wqs, wks) for c in range(C)]

    def load_quad_sp(sp, quad):
        cols = slice(quad * QUAD * HD, (quad + 1) * QUAD * HD)
        for n, (w, c) in enumerate(SPLIT):
            if quad:
                sp.wait_ge(lo_made, (quad - 1) * len(SPLIT) + n + 1)
            src = args["a_wq" if w is wqs else "a_wk"]
            sp.dma_start(raw[:, n, :], src[c * P:(c + 1) * P, cols]).then_inc(raw_in[n], 16)
        sp.dma_start(wv[:, :, cols], args["a_wv"].rearrange("(c p) h -> p c h", p=P)[:, :, cols]).then_inc(wv_in[quad], 16)

    def split_act(act, quad):
        cols = slice(quad * QUAD * HD, (quad + 1) * QUAD * HD)
        for n, (w, c) in enumerate(SPLIT):
            act.wait_ge(raw_in[n], 16 * (quad + 1))
            nc.scalar.activation(w[0][:, c, cols], raw[:, n, :], ACT.Copy).then_inc(hi_made, 1)

    def split_dve(dve, quad):
        cols = slice(quad * QUAD * HD, (quad + 1) * QUAD * HD)
        for n, (w, c) in enumerate(SPLIT):
            dve.wait_ge(hi_made, quad * len(SPLIT) + n + 1)
            nc.vector.tensor_tensor(out=w[1][:, c, cols], in0=raw[:, n, :], in1=w[0][:, c, cols], op=ALU.subtract).then_inc(lo_made, 1)

    def next_quad(t, s):
        return s // QUAD + 1 if isinstance(t, int) and t == 0 and s % QUAD == 0 and s < NH - QUAD else None

    def project_pe(pe, t, s):
        total = t * NH + s
        if s == 0:
            pe.wait_ge(hT_ready, t + 1)
        if isinstance(t, int) and t == 0 and s % QUAD == 0:
            pe.wait_ge(lo_made, (s // QUAD + 1) * len(SPLIT))
            pe.wait_ge(wv_in[s // QUAD], 16)
        for w, out, ready, copied in ((wqs, Q, q_ready, qs_ready), (wks, K, k_ready, ks_ready)):
            if some(total):
                pe.wait_ge(copied, total)
            for n, (pw, ph) in enumerate(((0, 0), (0, 1), (1, 0))):
                for c in range(C):
                    i = nc.tensor.matmul(out[:], w[pw][:, c, s * HD:(s + 1) * HD], hTs[ph][:, c, :],
                                         start=(n == 0 and c == 0), stop=(n == 2 and c == C - 1))
            i.then_inc(ready, 1)
        if some(total):
            pe.wait_ge(v_emptied, total)
        if s == TAIL + 1 and not (isinstance(t, int) and t == 0):
            pe.wait_ge(t_emptied, t * C)
        if s == FRONT + 1 and not (isinstance(t, int) and t == NT - 1):
            pe.wait_ge(f_emptied, (t + 2) * C)
        g, first = s % QUAD, s - s % QUAD
        for c in range(C):
            i = nc.tensor.matmul(V[:], hT[:, c, g * P:(g + 1) * P], wv[:, c, first * HD:(first + QUAD) * HD],
                                 start=(c == 0), stop=(c == C - 1))
        i.then_inc(v_filled, 1)

    def project_act(act, t, s):
        n = t * NH + s
        act.wait_ge(q_ready, n + 1)
        if some(n - 1):
            act.wait_ge(s_ready, n - 1)
        nc.scalar.activation(qs[:, s % 2, :], Q[:], ACT.Copy).then_inc(qs_ready, 1)
        if s % QUAD == 0:
            if some(n - QUAD):
                act.wait_ge(o_ready, n - QUAD)
        act.wait_ge(v_filled, n + 1)
        nc.scalar.activation(vs[:, (s // QUAD) % 2, s % QUAD, :], V[:], ACT.Copy).then_inc(v_emptied, 1)

    def project_dve(dve, t, s):
        n = t * NH + s
        dve.wait_ge(k_ready, n + 1)
        if some(n - 1):
            dve.wait_ge(s_ready, n - 1)
        nc.vector.tensor_copy(ks[:, s % 2, :], K[:]).then_inc(ks_ready, 1)

    def scores_pe(pe, t, s):
        n = t * NH + s
        pe.wait_ge(qs_ready, n + 1)
        pe.wait_ge(ks_ready, n + 1)
        if some(n):
            pe.wait_ge(s_read, n)
        for g in range(GT):
            i = nc.tensor.matmul(Sc[:, g * P:(g + 1) * P], qs[:, s % 2, g * P:(g + 1) * P], ks[:, s % 2, g * P:(g + 1) * P],
                                 start=True, stop=True)
        i.then_inc(s_ready, 1)

    def softmax_dve(dve, t, s):
        n, wide, p_ = t * NH + s, [P, GT, P], pr[:, s % 2, :, :]
        soft_chain.begin(t, 4 * s)
        dve.wait_ge(s_ready, n + 1)
        if some(n - 1):
            dve.wait_ge(pT_ready, n - 1)
        i = nc.vector.scalar_tensor_tensor(out=p_, in0=Sc[:].rearrange("p (g k) -> p g k", k=P), scalar=SCALE,
                                           in1=causal[:].unsqueeze(1).broadcast_to(wide), op0=ALU.mult, op1=ALU.add)
        i.then_inc(s_read, 1)
        dve.wait_ge(s_read, n + 1)
        nc.vector.tensor_reduce(out=smax[:], in_=p_, axis=AX.X, op=ALU.max).then_inc(soft_chain.sem, 1)
        dve.wait_ge(soft_chain.sem, soft_chain.next())
        nc.vector.tensor_tensor(out=p_, in0=p_, in1=smax[:].unsqueeze(2).broadcast_to(wide),
                                op=ALU.subtract).then_inc(shifted, 1)

    def exp_act(act, t, s):
        n, p_ = t * NH + s, pr[:, s % 2, :, :]
        act.wait_ge(shifted, n + 1)
        nc.scalar.activation(p_, p_, ACT.Exp).then_inc(e_ready, 1)

    def normalize_dve(dve, t, s):
        n, wide, p_ = t * NH + s, [P, GT, P], pr[:, s % 2, :, :]
        dve.wait_ge(e_ready, n + 1)
        nc.vector.tensor_reduce(out=ssum[:], in_=p_, axis=AX.X, op=ALU.add).then_inc(soft_chain.sem, 1)
        dve.wait_ge(soft_chain.sem, soft_chain.next())
        nc.vector.reciprocal(ssum[:], ssum[:]).then_inc(soft_chain.sem, 1)
        dve.wait_ge(soft_chain.sem, soft_chain.next())
        nc.vector.tensor_tensor(out=p_, in0=p_, in1=ssum[:].unsqueeze(2).broadcast_to(wide), op=ALU.mult).then_inc(soft_chain.sem, 1)
        dve.wait_ge(soft_chain.sem, soft_chain.next())
        dve.sem_inc(p_ready, 1)
        if s == NH - 1:
            soft_chain.end()

    def transpose_pe(pe, t, s):
        n = t * NH + s
        pe.wait_ge(p_ready, n + 1)
        if some(n):
            pe.wait_ge(pTs_ready, n)
        for g in range(GT):
            i = nc.tensor.transpose(PT[:, g * P:(g + 1) * P], pr[:, s % 2, g, :], core.ident[:])
        i.then_inc(pT_ready, 1)

    def transposed_act(act, t, s):
        n = t * NH + s
        act.wait_ge(pT_ready, n + 1)
        if some(n - 1):
            act.wait_ge(o_ready, n - 1)
        nc.scalar.activation(pT[:, s % 2, :], PT[:], ACT.Copy).then_inc(pTs_ready, 1)

    def apply_pe(pe, t, s):
        n = t * NH + s
        pe.wait_ge(pTs_ready, n + 1)
        if s % QUAD == 0:
            pe.wait_ge(v_emptied, t * NH + s + QUAD)
        if some(n):
            pe.wait_ge(oT_ready, n)
        h = s % QUAD
        for g in range(GT):
            i = nc.tensor.matmul(O[:, g * P:(g + 1) * P], vs[:, (s // QUAD) % 2, g, h * HD:(h + 1) * HD],
                                 pT[:, s % 2, g * P:(g + 1) * P], start=True, stop=True)
        i.then_inc(o_ready, 1)

    def applied_act(act, t, s):
        n = t * NH + s
        act.wait_ge(o_ready, n + 1)
        if some(n - 1):
            act.wait_ge(out_done, n - 1)
        nc.scalar.activation(oT[:, s % 2, :], O[:], ACT.Copy).then_inc(oT_ready, 1)

    def out_pe(pe, t, s):
        n = t * NH + s
        pe.wait_ge(oT_ready, n + 1)
        if s == 0:
            if isinstance(t, int) and t == 0:
                pe.wait_ge(wo_in, 16)
            if some(t):
                pe.wait_ge(y_used, t)
        for g in range(GT):
            i = nc.tensor.matmul(Y[g // 2][:, (g % 2) * D:(g % 2 + 1) * D], oT[:, s % 2, g * P:(g + 1) * P], wo[:, s, :],
                                 start=(s == 0 and g % 2 == 0), stop=(s == NH - 1), skip_group_check=True)
        i.then_inc(out_done, 1)

    def tail_dve(dve, t):
        tail_chain.begin(t)
        dve.wait_ge(out_done, (t + 1) * NH)
        dve.wait_ge(mvb_ready, t + 1)
        for g in range(GT):
            i = nc.vector.tensor_scalar(x1[:, g, :], group_x(t, g), mvb[:, g, 0:1], rstdb[:, g:g + 1], ALU.subtract, ALU.mult)
        i.then_inc(tail_chain.sem, 1)
        dve.wait_ge(tail_chain.sem, tail_chain.next())
        for n in range(2):
            half = x1[:, 2 * n:2 * n + 2, :].rearrange("p g d -> p (g d)")
            i = nc.vector.tensor_tensor(out=half, in0=Y[n][:], in1=half, op=ALU.add)
        i.then_inc(tail_chain.sem, 1)
        dve.wait_ge(tail_chain.sem, tail_chain.next())
        dve.sem_inc(y_used, 1)
        xt = x[:, bass.ds(t * (GT * D), GT * D)]
        nc.vector.tensor_tensor(out=xt, in0=xt, in1=x1[:].rearrange("p g d -> p (g d)"), op=ALU.add)
        for g in range(GT):
            i = nc.vector.bn_stats(stats2[:, g, :], x1[:, g, :])
        i.then_inc(tail_chain.sem, 1)
        dve.wait_ge(tail_chain.sem, tail_chain.next())
        dve.sem_inc(passed, 1)
        for g in range(GT):
            i = nc.vector.bn_aggr(mv2[:, g, :], stats2[:, g, :])
        i.then_inc(tail_chain.sem, 1)
        dve.wait_ge(tail_chain.sem, tail_chain.next())
        nc.vector.tensor_tensor(out=ms2[:], in0=mv2[:, :, 0], in1=mv2[:, :, 0], op=ALU.mult).then_inc(tail_chain.sem, 1)
        dve.wait_ge(tail_chain.sem, tail_chain.next())
        nc.vector.tensor_tensor(out=ms2[:], in0=ms2[:], in1=mv2[:, :, 1], op=ALU.add).then_inc(tail_chain.sem, 1)
        dve.wait_ge(tail_chain.sem, tail_chain.next())
        nc.vector.tensor_scalar(ms2[:], ms2[:], EPS, None, ALU.add).then_inc(ms2_ready, 1)
        dve.wait_ge(r2_ready, t + 1)
        for g in range(GT):
            i = nc.vector.tensor_scalar(x1[:, g, :], x1[:, g, :], r2[:, g:g + 1], None, ALU.mult)
        i.then_inc(tn_ready, 1)
        tail_chain.end()
        if not (isinstance(t, int) and t == NT - 1):
            keep_stats_dve(dve, t + 1)

    def tail_pool(pool, t):
        pool.wait_ge(ms2_ready, t + 1)
        nc.gpsimd.tensor_tensor(out=r2[:], in0=ms2[:], in1=core.neghalf[:, 0:GT], op=ALU.pow).then_inc(r2_ready, 1)

    def tail_pe(pe, t):
        pe.wait_ge(tn_ready, t + 1)
        pe.wait_ge(v_emptied, (t + 1) * NH + TAIL + 1 if not (isinstance(t, int) and t == NT - 1) else NT * NH)
        for c in range(C):
            if c:
                pe.wait_ge(t_emptied, t * C + c)
            for g in range(GT):
                i = nc.tensor.transpose(V[:, g * P:(g + 1) * P], x1[:, g, c * P:(c + 1) * P], core.ident[:])
            i.then_inc(t_filled, 1)

    def tail_act(act, t):
        act.wait_ge(stored, 16 * (t + 1))
        for c in range(C):
            act.wait_ge(t_filled, t * C + c + 1)
            nc.scalar.activation(tT[:, c, :], V[:], ACT.Copy, scale=ln2[:, c:c + 1]).then_inc(t_emptied, 1)

    def tail_sp(sp, t):
        sp.wait_ge(t_emptied, (t + 1) * C)
        sp.dma_start(args["t_scratch"].rearrange("(c p) n -> p c n", p=P)[:, :, bass.ds(t * TILE, TILE)], tT[:]).then_inc(stored, 16)

    def prev(t, s, l):
        if s >= l:
            return t, s - l
        if isinstance(t, int) and t == 0:
            return None
        return t - 1, NH + s - l

    def after(t, s, l, f, eng):
        p = prev(t, s, l)
        if p is not None:
            f(eng, *p)

    def step_pe(pe, t, s):
        project_pe(pe, t, s)
        after(t, s, 1, scores_pe, pe)
        after(t, s, 2, transpose_pe, pe)
        after(t, s, 3, apply_pe, pe)
        after(t, s, 4, out_pe, pe)

    def step_act(act, t, s):
        if next_quad(t, s):
            split_act(act, next_quad(t, s))
        project_act(act, t, s)
        after(t, s, 2, transposed_act, act)
        after(t, s, 1, exp_act, act)
        after(t, s, 3, applied_act, act)

    def step_dve(dve, t, s):
        if next_quad(t, s):
            split_dve(dve, next_quad(t, s))
        project_dve(dve, t, s)
        if s == NH - 1 and not (isinstance(t, int) and t == NT - 1):
            hand_over_dve(dve, t + 1)
        after(t, s, 1, softmax_dve, dve)
        after(t, s, 1, normalize_dve, dve)

    loads = [(ln1[:], args["ln1"]), (ln2[:], args["ln2"]), (causal[:], args["causal"])]
    n_in = 16 * len(loads)
    def tiles(eng, step, front, tail, tail_at=TAIL):
        def tile(t):
            for s in range(NH):
                step(eng, t, s)
                if s == tail_at and not (isinstance(t, int) and t == 0):
                    tail(eng, t - 1)
                if s == FRONT and not (isinstance(t, int) and t == NT - 1):
                    front(eng, t + 1)
        tile(0)
        with eng.Fori(1, NT - 1) as t:
            tile(t)
        tile(NT - 1)

    with nc.Block() as block:
        @block.sync
        def _(sp):
            for out, in_ in loads:
                sp.dma_start(out, in_).then_inc(weights_in, 16)
            load_quad_sp(sp, 0)
            load_quad_sp(sp, 1)
            sp.dma_start(wo[:], args["a_wo"].rearrange("(n p) d -> p n d", p=P)).then_inc(wo_in, 16)
            for quad in range(2, NH // QUAD):
                load_quad_sp(sp, quad)
            tail_sp(sp, 0)
            with sp.Fori(1, NT) as t:
                tail_sp(sp, t)
            sp.wait_ge(stored, 16 * (NT + 1))

        @block.tensor
        def _(pe):
            front_pe(pe, 0)
            tiles(pe, step_pe, front_pe, tail_pe)
            scores_pe(pe, NT - 1, NH - 1)
            for l in (2, 1):
                transpose_pe(pe, NT - 1, NH - l)
            for l in (3, 2, 1):
                apply_pe(pe, NT - 1, NH - l)
                out_pe(pe, NT - 1, NH - l - 1)
            out_pe(pe, NT - 1, NH - 1)
            tail_pe(pe, NT - 1)

        @block.scalar
        def _(act):
            act.sem_inc(stored, 16)
            act.wait_ge(weights_in, n_in)
            front_act(act, 0)
            split_act(act, 0)
            tiles(act, step_act, front_act, tail_act)
            transposed_act(act, NT - 1, NH - 2)
            exp_act(act, NT - 1, NH - 1)
            applied_act(act, NT - 1, NH - 3)
            transposed_act(act, NT - 1, NH - 1)
            applied_act(act, NT - 1, NH - 2)
            applied_act(act, NT - 1, NH - 1)
            tail_act(act, NT - 1)

        @block.vector
        def _(dve):
            dve.wait_ge(weights_in, n_in)
            front_dve(dve, 0)
            hand_over_dve(dve, 0)
            split_dve(dve, 0)
            keep_stats_dve(dve, 0)
            tiles(dve, step_dve, front_dve, tail_dve, tail_at=TAIL_DVE)
            softmax_dve(dve, NT - 1, NH - 1)
            normalize_dve(dve, NT - 1, NH - 1)
            tail_dve(dve, NT - 1)

        @block.gpsimd
        def _(pool):
            front_pool(pool, 0)
            front_pool(pool, 1)
            with pool.Fori(1, NT - 1) as t:
                tail_pool(pool, t - 1)
                front_pool(pool, t + 1)
            tail_pool(pool, NT - 2)
            tail_pool(pool, NT - 1)
    st.close()


UNIT = 256
NU = T // UNIT
GU = UNIT // P


def unit_loop(eng, work):
    work(eng, 0, 0)
    with eng.Fori(0, NU // 2 - 1) as pair:
        work(eng, pair * 2 + 1, 1)
        work(eng, pair * 2 + 2, 0)
    work(eng, NU - 1, 1)


def is_first(t):
    return isinstance(t, int) and t == 0


def is_last(t):
    return isinstance(t, int) and t == NU - 1


def quantize_weights_block(core, name, srcs):
    nc, bank = core.nc, core.bank
    st = Stage(core, name)
    sb, sem = st.sb, st.sem
    n_w = len(srcs)
    w, wr, qw = sb("w", [P, n_w * C, D]), sb("wr", [P, n_w * C, D]), sb("qw", [P, n_w * C, D], BF16)
    sw, rs = sb("sw", [P, n_w * C]), sb("rs", [P, n_w * C])
    diag, ones = sb("diag", [P, n_w * C, P]), sb("ones", [P, P])
    w_in, q_done, one_done, tr, tr_out, bc = (sem(n) for n in ("w_in", "q_done", "one_done", "tr", "tr_out", "bc"))
    chain = Chain(sem("chain"), 6)
    with nc.Block() as block:
        @block.sync
        def _(sp):
            for n, (src, _, _) in enumerate(srcs):
                sp.dma_start(w[:, n * C:(n + 1) * C, :], src.rearrange("(c p) i -> p c i", p=P)).then_inc(w_in, 16)

        @block.gpsimd
        def _(pool):
            nc.gpsimd.memset(ones[:], 1.0).then_inc(one_done, 1)

        @block.vector
        def _(dve):
            chain.begin(0)
            dve.wait_ge(w_in, 16 * n_w)
            nc.vector.tensor_reduce(out=sw[:], in_=w[:], axis=AX.X, op=ALU.max, apply_absolute_value=True).then_inc(chain.sem, 1)
            dve.wait_ge(chain.sem, chain.next())
            nc.vector.tensor_scalar(sw[:], sw[:], 1.0 / 127.0, 1e-8, ALU.mult, ALU.max).then_inc(chain.sem, 1)
            dve.wait_ge(chain.sem, chain.next())
            nc.vector.reciprocal(rs[:], sw[:]).then_inc(chain.sem, 1)
            dve.wait_ge(chain.sem, chain.next())
            for m in range(n_w * C):
                i = nc.vector.tensor_scalar(wr[:, m, :], w[:, m, :], rs[:, m:m + 1], MAGIC, ALU.mult, ALU.add)
            i.then_inc(chain.sem, 1)
            dve.wait_ge(chain.sem, chain.next())
            nc.vector.tensor_scalar(qw[:], wr[:], MAGIC, None, ALU.subtract).then_inc(chain.sem, 1)
            dve.wait_ge(chain.sem, chain.next())
            for m in range(n_w * C):
                i = nc.vector.tensor_scalar(diag[:, m, :], core.ident[:], sw[:, m:m + 1], None, ALU.mult)
            i.then_inc(chain.sem, 1)
            dve.wait_ge(chain.sem, chain.next())
            chain.end()
            dve.sem_inc(q_done, 1)
            for n, (_, qT, scale) in enumerate(srcs):
                dve.wait_ge(tr, n + 1)
                nc.vector.tensor_copy(qT[:].rearrange("p c o -> p (c o)"), bank[n][:].bitcast(BF16)[:, 0:C * D])
                nc.vector.tensor_copy(scale[:], bank[2 + n][:, 0:D]).then_inc(tr_out, 1)

        @block.tensor
        def _(pe):
            pe.wait_ge(q_done, 1)
            pe.wait_ge(one_done, 1)
            for n in range(n_w):
                for ci in range(C):
                    for co in range(C):
                        nc.tensor.transpose(bank[n][:].bitcast(BF16)[:, ci * D + co * P:ci * D + (co + 1) * P],
                                            qw[:, n * C + co, ci * P:(ci + 1) * P], core.identb[:])
                for co in range(C):
                    i = nc.tensor.matmul(bank[2 + n][:, co * P:(co + 1) * P], ones[:], diag[:, n * C + co, :], start=True, stop=True)
                i.then_inc(tr, 1)
    st.close()


def head_attention_stage(core, name, quant):
    nc, args, bank, x = core.nc, core.args, core.bank, core.x
    st = Stage(core, name)
    sb, sem = st.sb, st.sem
    NH, HD, BU = 16, 16, UNIT // S
    H8 = NH // C
    wdt = BF16 if quant else FP32

    wqT, woT = sb("wqT", [P, C, D], wdt), sb("woT", [P, C, D], wdt)
    wkT, wvT = sb("wkT", [P, C, D]), sb("wvT", [P, C, D])
    hmask = sb("hmask", [P, H8])
    ctxT = [sb(f"ctxT{i}", [P, C, BU, 2, S]) for i in range(2)]
    xn = sb("xn", [P, GU, D])
    stats, mv = sb("stats", [P, GU, 6]), sb("mv", [P, GU, 2])
    ve, rstd = sb("ve", [P, GU]), sb("rstd", [P, GU])
    hT = sb("hT", [P, C, UNIT], wdt)
    qT = [sb(f"qT{i}", [P, C, UNIT]) for i in range(2)]
    kT = sb("kT", [P, C, UNIT])
    km = sb("km", [P, C, BU, H8, S])
    vbd = [sb(f"vbd{i}", [P, BU, NH // 2, 2, HD]) for i in range(2)]
    pr = [sb(f"pr{g}", [P, NH, S]) for g in range(GU)]
    pT = sb("pT", [P, NH // 2, P])
    smax, rsum = sb("smax", [P, GU, NH]), sb("rsum", [P, GU, NH])
    o = sb("o", [P, D])
    oT = sb("oT", [P, C, P], wdt)
    y = sb("y", [P, D])

    weights_in, passed = sem("weights_in"), st.passed()
    ctx_in = [sem(f"ctx_in{i}") for i in range(2)]
    zeroed = sem("zeroed")
    var_ready, rstd_ready, xn_ready = sem("var_ready"), sem("rstd_ready"), sem("xn_ready")
    filled = [sem(f"filled{i}") for i in range(2)]
    emptied = [sem(f"emptied{i}") for i in range(2)]
    km_ready, scored, s_read, shifted, e_ready = (sem(n) for n in ("km_ready", "scored", "s_read", "shifted", "e_ready"))
    sums_ready, pT_ready, pTs_ready, o_ready, o_read = (sem(n) for n in ("sums_ready", "pT_ready", "pTs_ready", "o_ready", "o_read"))
    on_ready, oT_filled, oT_ready, y_ready, y_used = (sem(n) for n in ("on_ready", "oT_filled", "oT_ready", "y_ready", "y_used"))
    soft_chain = Chain(sem("soft_chain"), GU * 4)
    out_chain = Chain(sem("out_chain"), GU * (6 if quant else 1))
    if quant:
        swq, swo = sb("swq", [P, D]), sb("swo", [P, D])
        bq, bk, bv, bo = sb("bq", [P, D]), sb("bk", [P, C]), sb("bv", [P, D]), sb("bo", [P, D])
        sx, rsx = sb("sx", [P, GU]), sb("rsx", [P, GU])
        sxu = sb("sxu", [P, GU])
        qx, qf = sb("qx", [P, GU, D], BF16), sb("qf", [P, GU, D])
        so, rso, oq = sb("so", [P, 1]), sb("rso", [P, 1]), sb("oq", [P, D], BF16)
        mask = [sb(f"mask{i}", [P, GU, S]) for i in range(2)]
        qf_ready = sem("qf_ready")
        norm_chain = Chain(sem("norm_chain"), 7)
        q_chain = Chain(sem("q_chain"), 1)
        quantize_weights_block(core, name + "_qw", [(args["wq"], wqT, swq), (args["wo"], woT, swo)])
    else:
        wgT, norm_w = sb("wgT", [P, C, D]), sb("norm_w", [P, C])
        ms, r1, rr = sb("ms", [P, GU]), sb("r1", [P, GU]), sb("rr", [P, GU])
        gate = [sb(f"gate{i}", [P, GU, D]) for i in range(2)]
        keep = sb("keep", [P, NG, S], U8)
        neg, valid = sb("neg", [P, GU, S]), sb("valid", [P, GU])
        ms_ready, ms_eps, r1_raw, rr_ready = sem("ms_ready"), sem("ms_eps"), sem("r1_raw"), sem("rr_ready")
        norm_chain = Chain(sem("norm_chain"), 3)
        m_chain = Chain(sem("m_chain"), 1)
    KEYS, INPUT, QUERIES, V0, V1, LAST = range(6)
    SB = [bank[0:2], bank[2:4]]
    OB = [bank[4], bank[5]]
    FB = [bank[6], bank[7]]

    def fwait_filled(eng, t, k):
        eng.wait_ge(filled[k % 2], t * 3 + k // 2 + 1)

    def fbank(pe, t, k):
        if some(t * 3 + k // 2):
            pe.wait_ge(emptied[k % 2], t * 3 + k // 2)
        return FB[k % 2]

    def group_x(t, g):
        return x[:, bass.ds(t * (GU * D) + g * D, D)]

    def norm_dve(dve, t):
        norm_chain.begin(t)
        for g in range(GU):
            i = nc.vector.bn_stats(stats[:, g, :], group_x(t, g))
        i.then_inc(norm_chain.sem, 1)
        dve.wait_ge(norm_chain.sem, norm_chain.next())
        dve.sem_inc(passed, 1)
        for g in range(GU):
            i = nc.vector.bn_aggr(mv[:, g, :], stats[:, g, :])
        i.then_inc(norm_chain.sem, 1)
        dve.wait_ge(norm_chain.sem, norm_chain.next())
        nc.vector.tensor_scalar(ve[:], mv[:, :, 1], LN_EPS, None, ALU.add).then_inc(var_ready, 1)
        dve.wait_ge(rstd_ready, t + 1)
        if quant:
            for g in range(GU):
                i = nc.vector.tensor_scalar(xn[:, g, :], group_x(t, g), mv[:, g, 0:1], rstd[:, g:g + 1], ALU.subtract, ALU.mult)
            i.then_inc(norm_chain.sem, 1)
            dve.wait_ge(norm_chain.sem, norm_chain.next())
            nc.vector.tensor_reduce(out=sx[:], in_=xn[:], axis=AX.X, op=ALU.max, apply_absolute_value=True).then_inc(norm_chain.sem, 1)
            dve.wait_ge(norm_chain.sem, norm_chain.next())
            nc.vector.tensor_scalar(sx[:], sx[:], 1.0 / 127.0, 1e-8, ALU.mult, ALU.max).then_inc(norm_chain.sem, 1)
            dve.wait_ge(norm_chain.sem, norm_chain.next())
            nc.vector.reciprocal(rsx[:], sx[:]).then_inc(norm_chain.sem, 1)
            dve.wait_ge(norm_chain.sem, norm_chain.next())
            for g in range(GU):
                i = nc.vector.tensor_scalar(xn[:, g, :], xn[:, g, :], rsx[:, g:g + 1], MAGIC, ALU.mult, ALU.add)
            i.then_inc(norm_chain.sem, 1)
            dve.wait_ge(norm_chain.sem, norm_chain.next())
            if some((t - 1) * 3 + INPUT // 2 + 1):
                dve.wait_ge(filled[INPUT % 2], (t - 1) * 3 + INPUT // 2 + 1)
            nc.vector.tensor_scalar(qx[:], xn[:], MAGIC, None, ALU.subtract).then_inc(xn_ready, 1)
        else:
            nc.vector.tensor_tensor(out=ms[:], in0=rstd[:], in1=rstd[:], op=ALU.mult).then_inc(norm_chain.sem, 1)
            dve.wait_ge(norm_chain.sem, norm_chain.next())
            nc.vector.tensor_tensor(out=ms[:], in0=ms[:], in1=mv[:, :, 1], op=ALU.mult).then_inc(ms_ready, 1)
            dve.wait_ge(rr_ready, t + 1)
            if some((t - 1) * 3 + INPUT // 2 + 1):
                dve.wait_ge(filled[INPUT % 2], (t - 1) * 3 + INPUT // 2 + 1)
            for g in range(GU):
                i = nc.vector.tensor_scalar(xn[:, g, :], group_x(t, g), mv[:, g, 0:1], rr[:, g:g + 1], ALU.subtract, ALU.mult)
            i.then_inc(xn_ready, 1)
        norm_chain.end()

    def norm_pool(pool, t):
        pool.wait_ge(var_ready, t + 1)
        nc.gpsimd.tensor_tensor(out=rstd[:], in0=ve[:], in1=core.neghalf[:, 0:GU], op=ALU.pow).then_inc(rstd_ready, 1)
        if not quant:
            pool.wait_ge(ms_ready, t + 1)
            pool.sem_inc(passed, 1)
            nc.gpsimd.tensor_scalar(ms[:], ms[:], 1e-6, None, ALU.add).then_inc(ms_eps, 1)
            pool.wait_ge(ms_eps, t + 1)
            nc.gpsimd.tensor_tensor(out=r1[:], in0=ms[:], in1=core.neghalf[:, 0:GU], op=ALU.pow).then_inc(r1_raw, 1)
            pool.wait_ge(r1_raw, t + 1)
            nc.gpsimd.tensor_tensor(out=rr[:], in0=r1[:], in1=rstd[:], op=ALU.mult).then_inc(rr_ready, 1)

    def keys_pe(pe, t, par):
        pe.wait_ge(ctx_in[par], (t // 2 + 1) * n_ctx)
        F = fbank(pe, t, KEYS)
        for co in range(C):
            for ci in range(C):
                i = nc.tensor.matmul(F[:, co * UNIT:(co + 1) * UNIT], wkT[:, ci, co * P:(co + 1) * P], ctxT[par][:, ci, :, 0, :],
                                     start=(ci == 0), stop=(ci == C - 1))
        i.then_inc(filled[KEYS % 2], 1)

    def keys_act(act, t):
        fwait_filled(act, t, KEYS)
        if some(t):
            act.wait_ge(km_ready, t)
        for co in range(C):
            i = nc.scalar.activation(kT[:, co, :], FB[KEYS % 2][:, co * UNIT:(co + 1) * UNIT], ACT.Identity,
                                     bias=bk[:, co:co + 1] if quant else 0.0)
        i.then_inc(emptied[KEYS % 2], 1)

    def keys_pool(pool, t):
        pool.wait_ge(emptied[KEYS % 2], t * 3 + KEYS // 2 + 1)
        if some(t * GU):
            pool.wait_ge(scored, t * GU)
        for c in range(C):
            i = nc.gpsimd.tensor_tensor(out=km[:, c, :, :, :],
                                        in0=kT[:, c, :].rearrange("p (b k) -> p b k", k=S).unsqueeze(2).broadcast_to([P, BU, H8, S]),
                                        in1=hmask[:].unsqueeze(1).unsqueeze(3).broadcast_to([P, BU, H8, S]), op=ALU.mult)
        i.then_inc(km_ready, 1)

    def input_pe(pe, t):
        pe.wait_ge(xn_ready, t + 1)
        F = fbank(pe, t, INPUT)
        src, idt = (qx, core.identb) if quant else (xn, core.ident)
        F = F[:].bitcast(BF16) if quant else F
        for c in range(C):
            for g in range(GU):
                i = nc.tensor.transpose(F[:, c * UNIT + g * P:c * UNIT + (g + 1) * P], src[:, g, c * P:(c + 1) * P], idt[:])
        i.then_inc(filled[INPUT % 2], 1)

    def input_act(act, t):
        fwait_filled(act, t, INPUT)
        if some((t - 1) * 3 + QUERIES // 2 + 1):
            act.wait_ge(filled[QUERIES % 2], (t - 1) * 3 + QUERIES // 2 + 1)
        if quant:
            nc.scalar.activation(hT[:].rearrange("p c t -> p (c t)"), FB[INPUT % 2][:].bitcast(BF16)[:, 0:C * UNIT],
                                 ACT.Copy).then_inc(emptied[INPUT % 2], 1)
        else:
            if some(t * 3):
                act.wait_ge(filled[LAST % 2], t * 3)
            for c in range(C):
                i = nc.scalar.activation(hT[:, c, :], FB[INPUT % 2][:, c * UNIT:(c + 1) * UNIT], ACT.Copy, scale=norm_w[:, c:c + 1])
            i.then_inc(emptied[INPUT % 2], 1)

    def queries_pe(pe, t):
        pe.wait_ge(emptied[INPUT % 2], t * 3 + INPUT // 2 + 1)
        F = fbank(pe, t, QUERIES)
        if quant:
            for g in range(GU):
                for c in range(C):
                    i = nc.tensor.matmul(F[:, g * D:(g + 1) * D], hT[:, c, g * P:(g + 1) * P], wqT[:, c, :],
                                         start=(c == 0), stop=(c == C - 1))
        else:
            for co in range(C):
                for ci in range(C):
                    i = nc.tensor.matmul(F[:, co * UNIT:(co + 1) * UNIT], wqT[:, ci, co * P:(co + 1) * P], hT[:, ci, :],
                                         start=(ci == 0), stop=(ci == C - 1))
        i.then_inc(filled[QUERIES % 2], 1)

    def queries_dve(dve, t):
        q_chain.begin(t)
        fwait_filled(dve, t, QUERIES)
        if some(t * 3):
            dve.wait_ge(filled[LAST % 2], t * 3)
        F = FB[QUERIES % 2]
        for g in range(GU):
            i = nc.vector.scalar_tensor_tensor(out=qf[:, g, :], in0=F[:, g * D:(g + 1) * D], scalar=sx[:, g:g + 1], in1=swq[:],
                                               op0=ALU.mult, op1=ALU.mult)
        i.then_inc(q_chain.sem, 1)
        dve.wait_ge(q_chain.sem, q_chain.next())
        dve.sem_inc(emptied[QUERIES % 2], 1)
        nc.vector.tensor_tensor(out=qf[:], in0=qf[:], in1=bq[:].unsqueeze(1).broadcast_to([P, GU, D]), op=ALU.add).then_inc(qf_ready, 1)

    def queries_act(act, t, par):
        fwait_filled(act, t, QUERIES)
        if some((t - 1) * GU):
            act.wait_ge(scored, (t - 1) * GU)
        nc.scalar.activation(qT[par][:].rearrange("p c t -> p (c t)"), FB[QUERIES % 2][:], ACT.Copy).then_inc(emptied[QUERIES % 2], 1)

    def values_pe(pe, t, par, n):
        F = fbank(pe, t, V0 + n)
        for b in range(2):
            for c in range(C):
                tok = ctxT[par][:, c, 2 * n + b, :, :].rearrange("p j k -> p (j k)")
                i = nc.tensor.matmul(F[:, b * D:(b + 1) * D], tok, wvT[:, c, :],
                                     start=(c == 0), stop=(c == C - 1))
        i.then_inc(filled[(V0 + n) % 2], 1)

    def values_act(act, t, par, n):
        fwait_filled(act, t, V0 + n)
        if some((t - 1) * GU):
            act.wait_ge(o_ready, (t - 1) * GU)
        act.wait_ge(zeroed, 1)
        v = FB[(V0 + n) % 2][:].rearrange("p (b h j d) -> p b h j d", b=2, j=2, d=HD)
        for j in range(2):
            i = nc.scalar.activation(vbd[par][64 * j:64 * j + 64, 2 * n:2 * n + 2, :, j, :], v[64 * j:64 * j + 64, :, :, j, :], ACT.Copy)
        i.then_inc(emptied[(V0 + n) % 2], 1)

    def last_pe(pe, t):
        F = fbank(pe, t, LAST)
        if quant:
            pe.wait_ge(qf_ready, t + 1)
            for c in range(C):
                for g in range(GU):
                    i = nc.tensor.transpose(F[:, c * UNIT + g * P:c * UNIT + (g + 1) * P], qf[:, g, c * P:(c + 1) * P], core.ident[:])
        else:
            for g in range(GU):
                for c in range(C):
                    i = nc.tensor.matmul(F[:, g * D:(g + 1) * D], hT[:, c, g * P:(g + 1) * P], wgT[:, c, :],
                                         start=(c == 0), stop=(c == C - 1))
        i.then_inc(filled[LAST % 2], 1)

    def last_act(act, t, par):
        fwait_filled(act, t, LAST)
        if quant:
            if some((t - 1) * GU):
                act.wait_ge(scored, (t - 1) * GU)
            nc.scalar.activation(qT[par][:].rearrange("p c t -> p (c t)"), FB[LAST % 2][:], ACT.Copy).then_inc(emptied[LAST % 2], 1)
        else:
            if some((t - 1) * GU):
                act.wait_ge(y_used, (t - 1) * GU)
            nc.scalar.activation(gate[par][:].rearrange("p g d -> p (g d)"), FB[LAST % 2][:], ACT.Tanh,
                                 scale=0.5).then_inc(emptied[LAST % 2], 1)

    def scores_pe(pe, t, par, g):
        if g == 0:
            pe.wait_ge(km_ready, t + 1)
            pe.wait_ge(emptied[(LAST if quant else QUERIES) % 2], t * 3 + (LAST if quant else QUERIES) // 2 + 1)
        if some((t - 1) * GU + g + 1):
            pe.wait_ge(pTs_ready, (t - 1) * GU + g + 1)
        for c in range(C):
            for b in range(2):
                i = nc.tensor.matmul(SB[g][c][64 * b:64 * b + 64, :], qT[par][:, c, (2 * g + b) * S:(2 * g + b + 1) * S],
                                     km[:, c, 2 * g + b, :, :].rearrange("p h k -> p (h k)"), start=True, stop=True)
        i.then_inc(scored, 1)

    def softmax_dve(dve, t, par, g):
        n = t * GU + g
        soft_chain.begin(t, g)
        if not quant and g == 0:
            m_chain.begin(t)
            kp = keep[:, bass.ds(t * GU, GU), :]
            nc.vector.tensor_reduce(out=valid[:], in_=kp, axis=AX.X, op=ALU.max)
            nc.vector.tensor_scalar(neg[:], kp, 1.0, BIG, ALU.subtract, ALU.mult).then_inc(m_chain.sem, 1)
            dve.wait_ge(m_chain.sem, m_chain.next())
        dve.wait_ge(scored, n + 1)
        if quant and g == 0:
            dve.wait_ge(ctx_in[par], (t // 2 + 1) * n_ctx)
        if some(n - 1):
            dve.wait_ge(pT_ready, n - 1)
        add = mask[par][:, g, :] if quant else neg[:, g, :]
        for c in range(C):
            i = nc.vector.scalar_tensor_tensor(out=pr[g][:, c * H8:(c + 1) * H8, :], in0=SB[g][c][:].rearrange("p (h k) -> p h k", k=S),
                                               scalar=float(HD) ** -0.5, in1=add.unsqueeze(1).broadcast_to([P, H8, S]),
                                               op0=ALU.mult, op1=ALU.add)
        i.then_inc(s_read, 1)
        dve.wait_ge(s_read, n + 1)
        nc.vector.tensor_reduce(out=smax[:, g, :], in_=pr[g][:], axis=AX.X, op=ALU.max).then_inc(soft_chain.sem, 1)
        dve.wait_ge(soft_chain.sem, soft_chain.next())
        nc.vector.tensor_tensor(out=pr[g][:], in0=pr[g][:], in1=smax[:, g, :].unsqueeze(2).broadcast_to([P, NH, S]),
                                op=ALU.subtract).then_inc(shifted, 1)

    def exp_act(act, t, g):
        act.wait_ge(shifted, t * GU + g + 1)
        nc.scalar.activation(pr[g][:], pr[g][:], ACT.Exp).then_inc(e_ready, 1)

    def sums_dve(dve, t, g):
        soft_chain.begin(t, GU + 3 * g)
        dve.wait_ge(e_ready, t * GU + g + 1)
        nc.vector.tensor_reduce(out=rsum[:, g, :], in_=pr[g][:], axis=AX.X, op=ALU.add).then_inc(soft_chain.sem, 1)
        dve.wait_ge(soft_chain.sem, soft_chain.next())
        nc.vector.reciprocal(rsum[:, g, :], rsum[:, g, :]).then_inc(soft_chain.sem, 1)
        dve.wait_ge(soft_chain.sem, soft_chain.next())
        if not quant:
            nc.vector.tensor_scalar(rsum[:, g, :], rsum[:, g, :], valid[:, g:g + 1], None, ALU.mult).then_inc(soft_chain.sem, 1)
            dve.wait_ge(soft_chain.sem, soft_chain.next())
        else:
            soft_chain.k += 1
            dve.sem_inc(soft_chain.sem, 1)

    def transpose_pe(pe, t, g):
        n = t * GU + g
        pe.wait_ge(e_ready, n + 1)
        pe.wait_ge(s_read, n + 1)
        for p in range(NH // 2):
            i = nc.tensor.transpose(SB[g][p // 4][:, (p % 4) * P:(p % 4 + 1) * P],
                                    pr[g][:, 2 * p:2 * p + 2, :].rearrange("p h k -> p (h k)"), core.ident[:])
        i.then_inc(pT_ready, 1)

    def transposed_act(act, t, g):
        n = t * GU + g
        act.wait_ge(pT_ready, n + 1)
        if some(n):
            act.wait_ge(o_ready, n)
        for c in range(C):
            i = nc.scalar.activation(pT[:, 4 * c:4 * c + 4, :], SB[g][c][:].rearrange("p (h q) -> p h q", q=P), ACT.Copy)
        i.then_inc(pTs_ready, 1)

    def apply_pe(pe, t, par, g):
        n = t * GU + g
        pe.wait_ge(pTs_ready, n + 1)
        if some(n - 1):
            pe.wait_ge(y_used, n - 1)
        pe.wait_ge(emptied[V1 % 2], t * 3 + V1 // 2 + 1)
        pe.wait_ge(emptied[V0 % 2], t * 3 + V0 // 2 + 1)
        for p in range(NH // 2):
            for b in range(2):
                i = nc.tensor.matmul(OB[g][64 * b:64 * b + 64, p * 2 * HD:(p + 1) * 2 * HD], pT[:, p, 64 * b:64 * b + 64],
                                     vbd[par][:, 2 * g + b, p, :, :].rearrange("p j d -> p (j d)"), start=True, stop=True)
        i.then_inc(o_ready, 1)

    def result_dve(dve, t, g):
        n = t * GU + g
        out_chain.begin(t, g * out_chain.per_tile // GU)
        dve.wait_ge(o_ready, n + 1)
        i = nc.vector.tensor_tensor(out=o[:].rearrange("p (h d) -> p h d", d=HD),
                                    in0=OB[g][:, 0:D].rearrange("p (h d) -> p h d", d=HD),
                                    in1=rsum[:, g, :].unsqueeze(2).broadcast_to([P, NH, HD]), op=ALU.mult)
        if not quant:
            i.then_inc(on_ready, 1)
            return
        i.then_inc(out_chain.sem, 1)
        dve.wait_ge(out_chain.sem, out_chain.next())
        nc.vector.tensor_tensor(out=o[:], in0=o[:], in1=bv[:], op=ALU.add).then_inc(out_chain.sem, 1)
        dve.wait_ge(out_chain.sem, out_chain.next())
        nc.vector.tensor_reduce(out=so[:], in_=o[:], axis=AX.X, op=ALU.max, apply_absolute_value=True).then_inc(out_chain.sem, 1)
        dve.wait_ge(out_chain.sem, out_chain.next())
        nc.vector.tensor_scalar(so[:], so[:], 1.0 / 127.0, 1e-8, ALU.mult, ALU.max).then_inc(out_chain.sem, 1)
        dve.wait_ge(out_chain.sem, out_chain.next())
        nc.vector.reciprocal(rso[:], so[:]).then_inc(out_chain.sem, 1)
        dve.wait_ge(out_chain.sem, out_chain.next())
        nc.vector.tensor_scalar(o[:], o[:], rso[:], MAGIC, ALU.mult, ALU.add).then_inc(out_chain.sem, 1)
        dve.wait_ge(out_chain.sem, out_chain.next())
        nc.vector.tensor_scalar(oq[:], o[:], MAGIC, None, ALU.subtract).then_inc(on_ready, 1)

    def result_pe(pe, t, g):
        n = t * GU + g
        pe.wait_ge(on_ready, n + 1)
        src, idt = (oq, core.identb) if quant else (o, core.ident)
        F = OB[g][:].bitcast(BF16) if quant else OB[g]
        for c in range(C):
            i = nc.tensor.transpose(F[:, c * P:(c + 1) * P], src[:, c * P:(c + 1) * P], idt[:])
        i.then_inc(oT_filled, 1)

    def result_act(act, t, g):
        n = t * GU + g
        act.wait_ge(oT_filled, n + 1)
        F = OB[g][:].bitcast(BF16) if quant else OB[g]
        nc.scalar.activation(oT[:].rearrange("p c t -> p (c t)"), F[:, 0:C * P], ACT.Copy).then_inc(oT_ready, 1)

    def out_pe(pe, t, g):
        pe.wait_ge(oT_ready, t * GU + g + 1)
        for c in range(C):
            i = nc.tensor.matmul(OB[g][:, D:2 * D], oT[:, c, :], woT[:, c, :], start=(c == 0), stop=(c == C - 1))
        i.then_inc(y_ready, 1)

    def residual_dve(dve, t, par, g):
        n = t * GU + g
        dve.wait_ge(y_ready, n + 1)
        Yg = OB[g][:, D:2 * D]
        if quant:
            y_chain.begin(t, 2 * g)
            nc.vector.scalar_tensor_tensor(out=y[:], in0=Yg, scalar=so[:], in1=swo[:], op0=ALU.mult, op1=ALU.mult).then_inc(y_chain.sem, 1)
            dve.wait_ge(y_chain.sem, y_chain.next())
            nc.vector.tensor_tensor(out=y[:], in0=y[:], in1=bo[:], op=ALU.add).then_inc(y_chain.sem, 1)
            dve.wait_ge(y_chain.sem, y_chain.next())
            nc.vector.tensor_tensor(out=group_x(t, g), in0=group_x(t, g), in1=y[:], op=ALU.add).then_inc(y_used, 1)
        else:
            y_chain.begin(t, g)
            nc.vector.scalar_tensor_tensor(out=y[:], in0=gate[par][:, g, :], scalar=1.0, in1=Yg, op0=ALU.add, op1=ALU.mult).then_inc(y_chain.sem, 1)
            dve.wait_ge(y_chain.sem, y_chain.next())
            nc.vector.scalar_tensor_tensor(out=group_x(t, g), in0=y[:], scalar=0.5, in1=group_x(t, g),
                                           op0=ALU.mult, op1=ALU.add).then_inc(y_used, 1)

    y_chain = Chain(sem("y_chain"), GU * (2 if quant else 1))

    loads = [(wkT[:], args["wkT" if quant else "z_wkT"].rearrange("(c p) o -> p c o", p=P)),
             (wvT[:], args["wvT" if quant else "z_wvT"].rearrange("(c p) o -> p c o", p=P)),
             (hmask[:], args["hmask"])]
    if quant:
        loads += [(bq[:], args["bq"]), (bk[:], args["bk"]), (bv[:], args["bv"]), (bo[:], args["bo"])]
    else:
        loads += [(wqT[:], args["z_wqT"].rearrange("(c p) o -> p c o", p=P)), (woT[:], args["z_woT"].rearrange("(c p) o -> p c o", p=P)),
                  (wgT[:], args["z_wgT"].rearrange("(c p) o -> p c o", p=P)), (norm_w[:], args["norm_w"]),
                  (keep[:], args["keep"].rearrange("p (g k) -> p g k", k=S))]
    n_in, n_ctx = 16 * len(loads), 16 * (2 * C + (1 if quant else 0))

    def load_ctx(sp, t, par):
        if some((t - 2) * 3 + V1 // 2 + 1):
            sp.wait_ge(emptied[V1 % 2], (t - 2) * 3 + V1 // 2 + 1)
        sp.sem_inc(passed, 1)
        if some((t - 2) * 3 + V0 // 2 + 1):
            sp.wait_ge(emptied[V0 % 2], (t - 2) * 3 + V0 // 2 + 1)
        sp.sem_inc(passed, 1)
        if quant:
            if some((t - 1) * GU):
                sp.wait_ge(s_read, (t - 1) * GU)
            sp.sem_inc(passed, 1)
        src = args["ctxT"].rearrange("(c p) n -> p c n", p=P)[:, :, bass.ds(t * UNIT, UNIT)]
        for c in range(C):
            for j in range(2):
                sp.dma_start(ctxT[par][:, c, :, j, :], src[:, c, :].rearrange("p (b k) -> p b k", k=S)).then_inc(ctx_in[par], 16)
        if quant:
            sp.dma_start(mask[par][:], args["mask"].rearrange("(g p) k -> p g k", p=P)[:, bass.ds(t * GU, GU), :]).then_inc(ctx_in[par], 16)

    def unit_pe(pe, t, par):
        nxt = 1 - par
        scores_pe(pe, t, par, 0)
        scores_pe(pe, t, par, 1)
        if not is_last(t):
            keys_pe(pe, t + 1, nxt)
        if not is_last(t) and quant:
            input_pe(pe, t + 1)
            queries_pe(pe, t + 1)
        if not is_first(t):
            result_pe(pe, t - 1, 0)
            out_pe(pe, t - 1, 0)
        if not is_last(t) and not quant:
            input_pe(pe, t + 1)
            queries_pe(pe, t + 1)
        transpose_pe(pe, t, 0)
        if not is_first(t):
            result_pe(pe, t - 1, 1)
        if not is_last(t):
            values_pe(pe, t + 1, nxt, 0)
        if not is_first(t):
            out_pe(pe, t - 1, 1)
        if not is_last(t) and quant:
            last_pe(pe, t + 1)
        apply_pe(pe, t, par, 0)
        if not is_last(t):
            values_pe(pe, t + 1, nxt, 1)
        transpose_pe(pe, t, 1)
        if not is_last(t) and not quant:
            last_pe(pe, t + 1)
        apply_pe(pe, t, par, 1)

    def unit_act(act, t, par):
        nxt = 1 - par
        if not is_last(t):
            keys_act(act, t + 1)
        if not is_last(t) and quant:
            input_act(act, t + 1)
        exp_act(act, t, 0)
        if not is_first(t):
            result_act(act, t - 1, 0)
        if not is_last(t) and not quant:
            input_act(act, t + 1)
            queries_act(act, t + 1, nxt)
        exp_act(act, t, 1)
        transposed_act(act, t, 0)
        if not is_first(t):
            result_act(act, t - 1, 1)
        if not is_last(t):
            values_act(act, t + 1, nxt, 0)
            if quant:
                last_act(act, t + 1, nxt)
            values_act(act, t + 1, nxt, 1)
        transposed_act(act, t, 1)
        if not is_last(t) and not quant:
            last_act(act, t + 1, nxt)

    def unit_dve(dve, t, par):
        if quant and not is_last(t):
            norm_dve(dve, t + 1)
        softmax_dve(dve, t, par, 0)
        if not is_first(t):
            result_dve(dve, t - 1, 0)
        if not quant and not is_last(t):
            norm_dve(dve, t + 1)
        softmax_dve(dve, t, par, 1)
        if quant and not is_last(t):
            queries_dve(dve, t + 1)
        if not is_first(t):
            residual_dve(dve, t - 1, 1 - par, 0)
            result_dve(dve, t - 1, 1)
        sums_dve(dve, t, 0)
        if not is_first(t):
            residual_dve(dve, t - 1, 1 - par, 1)
        sums_dve(dve, t, 1)

    def unit_pool(pool, t, par):
        if not is_last(t):
            norm_pool(pool, t + 1)
            keys_pool(pool, t + 1)

    with nc.Block() as block:
        @block.sync
        def _(sp):
            for out, in_ in loads:
                sp.dma_start(out, in_).then_inc(weights_in, 16)
            load_ctx(sp, 0, 0)
            load_ctx(sp, 1, 1)
            with sp.Fori(1, NU // 2) as pair:
                load_ctx(sp, pair * 2, 0)
                load_ctx(sp, pair * 2 + 1, 1)

        @block.tensor
        def _(pe):
            pe.wait_ge(weights_in, n_in)
            keys_pe(pe, 0, 0)
            input_pe(pe, 0)
            queries_pe(pe, 0)
            values_pe(pe, 0, 0, 0)
            values_pe(pe, 0, 0, 1)
            last_pe(pe, 0)
            unit_loop(pe, unit_pe)
            for g in range(GU):
                result_pe(pe, NU - 1, g)
                out_pe(pe, NU - 1, g)

        @block.scalar
        def _(act):
            act.wait_ge(weights_in, n_in)
            keys_act(act, 0)
            input_act(act, 0)
            if not quant:
                queries_act(act, 0, 0)
            values_act(act, 0, 0, 0)
            values_act(act, 0, 0, 1)
            last_act(act, 0, 0)
            unit_loop(act, unit_act)
            for g in range(GU):
                result_act(act, NU - 1, g)

        @block.vector
        def _(dve):
            dve.wait_ge(weights_in, n_in)
            dve.wait_ge(core.x_in, 64)
            norm_dve(dve, 0)
            if quant:
                queries_dve(dve, 0)
            unit_loop(dve, unit_dve)
            for g in range(GU):
                result_dve(dve, NU - 1, g)
                residual_dve(dve, NU - 1, 1, g)

        @block.gpsimd
        def _(pool):
            pool.wait_ge(weights_in, n_in)
            nc.gpsimd.memset(vbd[0][:], 0.0)
            nc.gpsimd.memset(vbd[1][:], 0.0).then_inc(zeroed, 1)
            norm_pool(pool, 0)
            keys_pool(pool, 0)
            unit_loop(pool, unit_pool)
    st.close()


def linear_attention_stage(core):
    nc, args, bank, x = core.nc, core.args, core.bank, core.x
    st = Stage(core, "lin")
    sb, sem = st.sb, st.sem
    HD, H8, BU = 16, 8, UNIT // S
    W = P + H8

    wqT, wgT, woT = sb("wqT", [P, C, D]), sb("wgT", [P, C, D]), sb("woT", [P, C, D])
    wkvT = sb("wkvT", [P, C, 2 * D])
    bg, hmask, bdmask = sb("bg", [P, D]), sb("hmask", [P, H8]), sb("bdmask", [P, P])
    ctxT = [sb(f"ctxT{i}", [P, C, UNIT]) for i in range(2)]
    xn = sb("xn", [P, GU, D])
    stats, mv = sb("stats", [P, GU, 6]), sb("mv", [P, GU, 2])
    ve, rstd = sb("ve", [P, GU]), sb("rstd", [P, GU])
    hT = sb("hT", [P, C, UNIT])
    low = sb("low", [P, 2 * UNIT])
    qT = [sb(f"qT{i}", [P, C * UNIT]) for i in range(2)]
    ks = [sb(f"ks{i}", [P, GU * D]) for i in range(2)]
    vs = [sb(f"vs{i}", [P, GU, C, P + 1]) for i in range(2)]
    graw = sb("graw", [P, GU, D])
    gate = [sb(f"gate{i}", [P, GU, D]) for i in range(2)]
    kv = sb("kv", [P, BU, C, W])
    rz = sb("rz", [P, C, H8])
    o, oT = sb("o", [P, GU, D]), sb("oT", [P, GU, C * P])

    weights_in, passed = sem("weights_in"), st.passed()
    ctx_in = [sem(f"ctx_in{i}") for i in range(2)]
    var_ready, rstd_ready, xn_ready, ones_ready = sem("var_ready"), sem("rstd_ready"), sem("xn_ready"), sem("ones_ready")
    filled = [sem(f"filled{i}") for i in range(2)]
    emptied = [sem(f"emptied{i}") for i in range(2)]
    low_ready, low_exp, graw_ready, gate_ready = sem("low_ready"), sem("low_exp"), sem("graw_ready"), sem("gate_ready")
    kv_filled, kv_ready, o_ready, on_ready, oT_filled, oT_ready, y_ready, y_used = (
        sem(n) for n in ("kv_filled", "kv_ready", "o_ready", "on_ready", "oT_filled", "oT_ready", "y_ready", "y_used"))
    norm_chain = Chain(sem("norm_chain"), 2)
    out_chain = Chain(sem("out_chain"), GU * 3)
    KEYS, INPUT, VALUES, QUERIES, GATE = 0, 1, 2, 3, 4
    ORDER = {0: [KEYS, VALUES, GATE], 1: [INPUT, QUERIES]}
    KV = [bank[0], bank[1], bank[2], bank[3]]
    OB = [bank[4], bank[5]]
    FB = [bank[6], bank[7]]

    def use(t, k):
        own = ORDER[k % 2]
        return t * len(own) + own.index(k)

    def filled_wait(eng, t, k):
        if some(use(t, k) + 1):
            eng.wait_ge(filled[k % 2], use(t, k) + 1)

    def emptied_wait(eng, t, k):
        eng.wait_ge(emptied[k % 2], use(t, k) + 1)

    def fbank(pe, t, k):
        if some(use(t, k)):
            pe.wait_ge(emptied[k % 2], use(t, k))
        return FB[k % 2]

    def group_x(t, g):
        return x[:, bass.ds(t * (GU * D) + g * D, D)]

    def norm_dve(dve, t):
        norm_chain.begin(t)
        for g in range(GU):
            i = nc.vector.bn_stats(stats[:, g, :], group_x(t, g))
        i.then_inc(norm_chain.sem, 1)
        dve.wait_ge(norm_chain.sem, norm_chain.next())
        dve.sem_inc(passed, 1)
        for g in range(GU):
            i = nc.vector.bn_aggr(mv[:, g, :], stats[:, g, :])
        i.then_inc(norm_chain.sem, 1)
        dve.wait_ge(norm_chain.sem, norm_chain.next())
        nc.vector.tensor_scalar(ve[:], mv[:, :, 1], LN_EPS, None, ALU.add).then_inc(var_ready, 1)
        dve.wait_ge(rstd_ready, t + 1)
        if some(use(t - 1, INPUT) + 1):
            dve.wait_ge(filled[INPUT % 2], use(t - 1, INPUT) + 1)
        for g in range(GU):
            i = nc.vector.tensor_scalar(xn[:, g, :], group_x(t, g), mv[:, g, 0:1], rstd[:, g:g + 1], ALU.subtract, ALU.mult)
        i.then_inc(xn_ready, 1)
        norm_chain.end()

    def norm_pool(pool, t):
        pool.wait_ge(var_ready, t + 1)
        nc.gpsimd.tensor_tensor(out=rstd[:], in0=ve[:], in1=core.neghalf[:, 0:GU], op=ALU.pow).then_inc(rstd_ready, 1)

    def keys_pe(pe, t, par):
        pe.wait_ge(ctx_in[par], (t // 2 + 1) * 16)
        F = fbank(pe, t, KEYS)
        for g in range(GU):
            for c in range(C):
                i = nc.tensor.matmul(F[:, g * D:(g + 1) * D], ctxT[par][:, c, g * P:(g + 1) * P], wkvT[:, c, 0:D],
                                     start=(c == 0), stop=(c == C - 1))
        i.then_inc(filled[KEYS % 2], 1)

    def values_pe(pe, t, par):
        F = fbank(pe, t, VALUES)
        for g in range(GU):
            for c in range(C):
                i = nc.tensor.matmul(F[:, g * D:(g + 1) * D], ctxT[par][:, c, g * P:(g + 1) * P], wkvT[:, c, D:2 * D],
                                     start=(c == 0), stop=(c == C - 1))
        i.then_inc(filled[VALUES % 2], 1)

    def values_act(act, t, par):
        filled_wait(act, t, VALUES)
        act.wait_ge(ones_ready, 2)
        if some((t - 1) * BU):
            act.wait_ge(kv_filled, (t - 1) * BU)
        nc.scalar.activation(vs[par][:, :, :, 0:P], FB[VALUES % 2][:].rearrange("p (g c d) -> p g c d", g=GU, c=C),
                             ACT.Copy).then_inc(emptied[VALUES % 2], 1)

    def input_pe(pe, t):
        pe.wait_ge(xn_ready, t + 1)
        F = fbank(pe, t, INPUT)
        for c in range(C):
            for g in range(GU):
                i = nc.tensor.transpose(F[:, c * UNIT + g * P:c * UNIT + (g + 1) * P], xn[:, g, c * P:(c + 1) * P], core.ident[:])
        i.then_inc(filled[INPUT % 2], 1)

    def input_act(act, t):
        filled_wait(act, t, INPUT)
        filled_wait(act, t - 1, GATE)
        nc.scalar.activation(hT[:].rearrange("p c t -> p (c t)"), FB[INPUT % 2][:], ACT.Copy).then_inc(emptied[INPUT % 2], 1)

    def queries_pe(pe, t):
        emptied_wait(pe, t, INPUT)
        F = fbank(pe, t, QUERIES)
        for co in range(C):
            for ci in range(C):
                i = nc.tensor.matmul(F[:, co * UNIT:(co + 1) * UNIT], wqT[:, ci, co * P:(co + 1) * P], hT[:, ci, :],
                                     start=(ci == 0), stop=(ci == C - 1))
        i.then_inc(filled[QUERIES % 2], 1)

    def gate_pe(pe, t):
        F = fbank(pe, t, GATE)
        for g in range(GU):
            for c in range(C):
                i = nc.tensor.matmul(F[:, g * D:(g + 1) * D], hT[:, c, g * P:(g + 1) * P], wgT[:, c, :],
                                     start=(c == 0), stop=(c == C - 1))
        i.then_inc(filled[GATE % 2], 1)

    def map_dve(dve, t, k, m, out):
        n = 2 * t + m
        filled_wait(dve, t, k)
        if some(use(t, KEYS) + 1 if m else use(t - 1, QUERIES) + 1):
            dve.wait_ge(emptied[KEYS % 2 if m else QUERIES % 2], use(t, KEYS) + 1 if m else use(t - 1, QUERIES) + 1)
        nc.vector.tensor_scalar(low[:], FB[k % 2][:], 0.0, None, ALU.min).then_inc(low_ready, 1)
        dve.wait_ge(low_exp, n + 1)
        if some((t - 1) * (GU if k == QUERIES else BU)):
            dve.wait_ge(o_ready if k == QUERIES else kv_filled, (t - 1) * (GU if k == QUERIES else BU))
        nc.vector.scalar_tensor_tensor(out=out[:], in0=FB[k % 2][:], scalar=0.0, in1=low[:], op0=ALU.max,
                                       op1=ALU.add).then_inc(emptied[k % 2], 1)

    def map_act(act, t, m):
        act.wait_ge(low_ready, 2 * t + m + 1)
        nc.scalar.activation(low[:], low[:], ACT.Exp).then_inc(low_exp, 1)

    def gate_dve(dve, t):
        filled_wait(dve, t, GATE)
        if some(t):
            dve.wait_ge(gate_ready, t)
        nc.vector.tensor_tensor(out=graw[:], in0=FB[GATE % 2][:].rearrange("p (g d) -> p g d", d=D),
                                in1=bg[:].unsqueeze(1).broadcast_to([P, GU, D]), op=ALU.add).then_inc(emptied[GATE % 2], 1)

    def gate_act(act, t, par):
        emptied_wait(act, t, GATE)
        if some((t - 1) * GU):
            act.wait_ge(on_ready, (t - 1) * GU)
        nc.scalar.activation(gate[par][:], graw[:], ACT.Tanh, scale=0.5).then_inc(gate_ready, 1)

    def summary_pe(pe, t, par):
        emptied_wait(pe, t, KEYS)
        emptied_wait(pe, t, VALUES)
        for b in range(BU):
            g, half = b // 2, slice(64 * (b % 2), 64 * (b % 2) + 64)
            if some((t - 1) * BU + b + 1):
                pe.wait_ge(kv_ready, (t - 1) * BU + b + 1)
            for c in range(C):
                i = nc.tensor.matmul(KV[b][:, c * (P + 1):(c + 1) * (P + 1)], ks[par][half, g * D + c * P:g * D + (c + 1) * P],
                                     vs[par][half, g, c, :], start=True, stop=True)
            i.then_inc(kv_filled, 1)

    def summary_dve(dve, t):
        if some(t * GU):
            dve.wait_ge(o_ready, t * GU)
        for b in range(BU):
            dve.wait_ge(kv_filled, t * BU + b + 1)
            prod = KV[b][:, 0:C * (P + 1)].rearrange("p (c w) -> p c w", w=P + 1)
            nc.vector.tensor_tensor(out=kv[:, b, :, 0:P], in0=prod[:, :, 0:P], in1=bdmask[:].unsqueeze(1).broadcast_to([P, C, P]), op=ALU.mult)
            nc.vector.tensor_tensor(out=kv[:, b, :, P:W], in0=prod[:, :, P:P + 1].broadcast_to([P, C, H8]),
                                    in1=hmask[:].unsqueeze(1).broadcast_to([P, C, H8]), op=ALU.mult).then_inc(kv_ready, 1)

    def apply_pe(pe, t, par, g):
        n = t * GU + g
        pe.wait_ge(kv_ready, t * BU + 2 * g + 2)
        if some(n - 1):
            pe.wait_ge(y_used, n - 1)
        for b in (2 * g, 2 * g + 1):
            for c in range(C):
                i = nc.tensor.matmul(OB[g][64 * (b % 2):64 * (b % 2) + 64, c * W:(c + 1) * W],
                                     qT[par][:, c * UNIT + b * S:c * UNIT + (b + 1) * S], kv[:, b, c, :], start=True, stop=True)
        i.then_inc(o_ready, 1)

    def result_dve(dve, t, par, g):
        n = t * GU + g
        out_chain.begin(t, 3 * g)
        dve.wait_ge(o_ready, n + 1)
        res = OB[g][:, 0:C * W].rearrange("p (c w) -> p c w", w=W)
        nc.vector.tensor_scalar(rz[:], res[:, :, P:W], 1e-6, None, ALU.add).then_inc(out_chain.sem, 1)
        dve.wait_ge(out_chain.sem, out_chain.next())
        nc.vector.reciprocal(rz[:], rz[:]).then_inc(out_chain.sem, 1)
        dve.wait_ge(out_chain.sem, out_chain.next())
        o4 = o[:, g, :].rearrange("p (c h d) -> p c h d", c=C, d=HD)
        nc.vector.tensor_tensor(out=o4, in0=res[:, :, 0:P].rearrange("p c (h d) -> p c h d", d=HD),
                                in1=rz[:].unsqueeze(3).broadcast_to([P, C, H8, HD]), op=ALU.mult).then_inc(out_chain.sem, 1)
        dve.wait_ge(out_chain.sem, out_chain.next())
        dve.wait_ge(gate_ready, t + 1)
        nc.vector.scalar_tensor_tensor(out=o[:, g, :], in0=gate[par][:, g, :], scalar=1.0, in1=o[:, g, :], op0=ALU.add,
                                       op1=ALU.mult).then_inc(on_ready, 1)

    def result_pe(pe, t, g):
        pe.wait_ge(on_ready, t * GU + g + 1)
        for c in range(C):
            i = nc.tensor.transpose(OB[g][:, c * P:(c + 1) * P], o[:, g, c * P:(c + 1) * P], core.ident[:])
        i.then_inc(oT_filled, 1)

    def result_act(act, t, g):
        act.wait_ge(oT_filled, t * GU + g + 1)
        nc.scalar.activation(oT[:, g, :], OB[g][:, 0:C * P], ACT.Copy).then_inc(oT_ready, 1)

    def out_pe(pe, t, g):
        pe.wait_ge(oT_ready, t * GU + g + 1)
        for c in range(C):
            i = nc.tensor.matmul(OB[g][:, D:2 * D], oT[:, g, c * P:(c + 1) * P], woT[:, c, :], start=(c == 0), stop=(c == C - 1))
        i.then_inc(y_ready, 1)

    def residual_dve(dve, t, g):
        dve.wait_ge(y_ready, t * GU + g + 1)
        nc.vector.scalar_tensor_tensor(out=group_x(t, g), in0=OB[g][:, D:2 * D], scalar=0.5, in1=group_x(t, g),
                                       op0=ALU.mult, op1=ALU.add).then_inc(y_used, 1)

    loads = [(w[:], args[n].rearrange("(c p) o -> p c o", p=P)) for w, n in ((wqT, "l_wqT"), (wgT, "l_wgT"), (woT, "l_woT"), (wkvT, "l_wkvT"))]
    loads += [(bg[:], args["bg"]), (hmask[:], args["hmask"]), (bdmask[:], args["bdmask"])]
    n_in = 16 * len(loads)

    def load_ctx(sp, t, par):
        if some(use(t - 2, VALUES) + 1):
            sp.wait_ge(emptied[VALUES % 2], use(t - 2, VALUES) + 1)
        sp.sem_inc(passed, 1)
        sp.dma_start(ctxT[par][:], args["ctxT"].rearrange("(c p) n -> p c n", p=P)[:, :, bass.ds(t * UNIT, UNIT)]).then_inc(ctx_in[par], 16)

    def unit_pe(pe, t, par):
        nxt = 1 - par
        summary_pe(pe, t, par)
        if not is_first(t):
            for g in range(GU):
                result_pe(pe, t - 1, g)
        if not is_last(t):
            keys_pe(pe, t + 1, nxt)
        if not is_first(t):
            for g in range(GU):
                out_pe(pe, t - 1, g)
        if not is_last(t):
            input_pe(pe, t + 1)
            values_pe(pe, t + 1, nxt)
            queries_pe(pe, t + 1)
        apply_pe(pe, t, par, 0)
        apply_pe(pe, t, par, 1)
        if not is_last(t):
            gate_pe(pe, t + 1)

    def unit_act(act, t, par):
        nxt = 1 - par
        if not is_first(t):
            for g in range(GU):
                result_act(act, t - 1, g)
        if not is_last(t):
            map_act(act, t + 1, 0)
            input_act(act, t + 1)
            values_act(act, t + 1, nxt)
            map_act(act, t + 1, 1)
            gate_act(act, t + 1, nxt)

    def unit_dve(dve, t, par):
        nxt = 1 - par
        if not is_last(t):
            norm_dve(dve, t + 1)
        summary_dve(dve, t)
        if not is_last(t):
            map_dve(dve, t + 1, KEYS, 0, ks[nxt])
        if not is_first(t):
            for g in range(GU):
                residual_dve(dve, t - 1, g)
        if not is_last(t):
            map_dve(dve, t + 1, QUERIES, 1, qT[nxt])
        for g in range(GU):
            result_dve(dve, t, par, g)
        if not is_last(t):
            gate_dve(dve, t + 1)

    def unit_pool(pool, t, par):
        if not is_last(t):
            norm_pool(pool, t + 1)

    with nc.Block() as block:
        @block.sync
        def _(sp):
            for out, in_ in loads:
                sp.dma_start(out, in_).then_inc(weights_in, 16)
            load_ctx(sp, 0, 0)
            load_ctx(sp, 1, 1)
            with sp.Fori(1, NU // 2) as pair:
                load_ctx(sp, pair * 2, 0)
                load_ctx(sp, pair * 2 + 1, 1)

        @block.tensor
        def _(pe):
            pe.wait_ge(weights_in, n_in)
            keys_pe(pe, 0, 0)
            input_pe(pe, 0)
            values_pe(pe, 0, 0)
            queries_pe(pe, 0)
            gate_pe(pe, 0)
            unit_loop(pe, unit_pe)
            for g in range(GU):
                result_pe(pe, NU - 1, g)
            for g in range(GU):
                out_pe(pe, NU - 1, g)

        @block.scalar
        def _(act):
            act.wait_ge(weights_in, n_in)
            map_act(act, 0, 0)
            input_act(act, 0)
            values_act(act, 0, 0)
            map_act(act, 0, 1)
            gate_act(act, 0, 0)
            unit_loop(act, unit_act)
            for g in range(GU):
                result_act(act, NU - 1, g)

        @block.vector
        def _(dve):
            dve.wait_ge(weights_in, n_in)
            norm_dve(dve, 0)
            map_dve(dve, 0, KEYS, 0, ks[0])
            map_dve(dve, 0, QUERIES, 1, qT[0])
            gate_dve(dve, 0)
            unit_loop(dve, unit_dve)
            for g in range(GU):
                residual_dve(dve, NU - 1, g)

        @block.gpsimd
        def _(pool):
            for i in range(2):
                nc.gpsimd.memset(vs[i][:], 1.0).then_inc(ones_ready, 1)
            norm_pool(pool, 0)
            unit_loop(pool, unit_pool)
    st.close()


def memory_attention_stage(core):
    nc, args, bank, x = core.nc, core.args, core.bank, core.x
    st = Stage(core, "mem")
    sb, sem = st.sb, st.sem
    ctxT = [sb(f"ctxT{i}", [P, C, UNIT]) for i in range(2)]
    ctx = [sb(f"ctx{i}", [P, GU, D]) for i in range(2)]
    keep = sb("keep", [P, NG, S], U8)
    neg, valid = sb("neg", [P, GU, S]), sb("valid", [P, GU])
    xn = sb("xn", [P, GU, D])
    stats, mv = sb("stats", [P, GU, 6]), sb("mv", [P, GU, 2])
    ve, rstd = sb("ve", [P, GU]), sb("rstd", [P, GU])
    hT = sb("hT", [P, C, UNIT])
    pr = sb("pr", [P, GU, S])
    smax, rsum = sb("smax", [P, GU]), sb("rsum", [P, GU])
    pbd = sb("pbd", [P, GU, P])
    pT = sb("pT", [P, UNIT])

    weights_in, passed = sem("weights_in"), st.passed()
    ctx_in = [sem(f"ctx_in{i}") for i in range(2)]
    var_ready, rstd_ready, xn_ready, zeroed = sem("var_ready"), sem("rstd_ready"), sem("xn_ready"), sem("zeroed")
    hT_filled, hT_ready, scored, s_read, shifted, e_ready = (sem(n) for n in ("hT_filled", "hT_ready", "scored", "s_read", "shifted", "e_ready"))
    p_ready, pT_filled, pT_ready, y_ready, y_used = (sem(n) for n in ("p_ready", "pT_filled", "pT_ready", "y_ready", "y_used"))
    norm_chain, soft_chain = Chain(sem("norm_chain"), 2), Chain(sem("soft_chain"), 5)
    FB, SB, TB, YB = bank[0], bank[1], bank[2], bank[3]

    def group_x(t, g):
        return x[:, bass.ds(t * (GU * D) + g * D, D)]

    def norm_dve(dve, t):
        norm_chain.begin(t)
        for g in range(GU):
            i = nc.vector.bn_stats(stats[:, g, :], group_x(t, g))
        i.then_inc(norm_chain.sem, 1)
        dve.wait_ge(norm_chain.sem, norm_chain.next())
        dve.sem_inc(passed, 1)
        for g in range(GU):
            i = nc.vector.bn_aggr(mv[:, g, :], stats[:, g, :])
        i.then_inc(norm_chain.sem, 1)
        dve.wait_ge(norm_chain.sem, norm_chain.next())
        nc.vector.tensor_scalar(ve[:], mv[:, :, 1], LN_EPS, None, ALU.add).then_inc(var_ready, 1)
        dve.wait_ge(rstd_ready, t + 1)
        if some(t):
            dve.wait_ge(hT_filled, t)
        for g in range(GU):
            i = nc.vector.tensor_scalar(xn[:, g, :], group_x(t, g), mv[:, g, 0:1], rstd[:, g:g + 1], ALU.subtract, ALU.mult)
        i.then_inc(xn_ready, 1)
        norm_chain.end()

    def norm_pool(pool, t):
        pool.wait_ge(var_ready, t + 1)
        nc.gpsimd.tensor_tensor(out=rstd[:], in0=ve[:], in1=core.neghalf[:, 0:GU], op=ALU.pow).then_inc(rstd_ready, 1)

    def input_pe(pe, t):
        pe.wait_ge(xn_ready, t + 1)
        if some(t):
            pe.wait_ge(hT_ready, t)
        for c in range(C):
            for g in range(GU):
                i = nc.tensor.transpose(FB[:, c * UNIT + g * P:c * UNIT + (g + 1) * P], xn[:, g, c * P:(c + 1) * P], core.ident[:])
        i.then_inc(hT_filled, 1)

    def input_act(act, t):
        act.wait_ge(hT_filled, t + 1)
        if some(t):
            act.wait_ge(scored, t)
        nc.scalar.activation(hT[:].rearrange("p c t -> p (c t)"), FB[:], ACT.Copy).then_inc(hT_ready, 1)

    def scores_pe(pe, t, par):
        pe.wait_ge(hT_ready, t + 1)
        pe.wait_ge(ctx_in[par], (t // 2 + 1) * 32)
        if some(t):
            pe.wait_ge(s_read, t)
        for b in range(2 * GU):
            for c in range(C):
                i = nc.tensor.matmul(SB[64 * (b % 2):64 * (b % 2) + 64, (b // 2) * S:(b // 2 + 1) * S], hT[:, c, b * S:(b + 1) * S],
                                     ctxT[par][:, c, b * S:(b + 1) * S], start=(c == 0), stop=(c == C - 1))
        i.then_inc(scored, 1)

    def softmax_dve(dve, t):
        soft_chain.begin(t)
        kp, wide = keep[:, bass.ds(t * GU, GU), :], [P, GU, S]
        nc.vector.tensor_reduce(out=valid[:], in_=kp, axis=AX.X, op=ALU.max)
        nc.vector.tensor_scalar(neg[:], kp, 1.0, BIG, ALU.subtract, ALU.mult).then_inc(soft_chain.sem, 1)
        dve.wait_ge(soft_chain.sem, soft_chain.next())
        dve.wait_ge(scored, t + 1)
        nc.vector.scalar_tensor_tensor(out=pr[:], in0=SB[:, 0:GU * S].rearrange("p (g k) -> p g k", k=S), scalar=float(D) ** -0.5,
                                       in1=neg[:], op0=ALU.mult, op1=ALU.add).then_inc(s_read, 1)
        dve.wait_ge(s_read, t + 1)
        nc.vector.tensor_reduce(out=smax[:], in_=pr[:], axis=AX.X, op=ALU.max).then_inc(soft_chain.sem, 1)
        dve.wait_ge(soft_chain.sem, soft_chain.next())
        nc.vector.tensor_tensor(out=pr[:], in0=pr[:], in1=smax[:].unsqueeze(2).broadcast_to(wide), op=ALU.subtract).then_inc(shifted, 1)

    def exp_act(act, t):
        act.wait_ge(shifted, t + 1)
        nc.scalar.activation(pr[:], pr[:], ACT.Exp).then_inc(e_ready, 1)

    def normalize_dve(dve, t):
        soft_chain.begin(t, 2)
        dve.wait_ge(e_ready, t + 1)
        nc.vector.tensor_reduce(out=rsum[:], in_=pr[:], axis=AX.X, op=ALU.add).then_inc(soft_chain.sem, 1)
        dve.wait_ge(soft_chain.sem, soft_chain.next())
        nc.vector.reciprocal(rsum[:], rsum[:]).then_inc(soft_chain.sem, 1)
        dve.wait_ge(soft_chain.sem, soft_chain.next())
        nc.vector.tensor_tensor(out=rsum[:], in0=rsum[:], in1=valid[:], op=ALU.mult).then_inc(soft_chain.sem, 1)
        dve.wait_ge(soft_chain.sem, soft_chain.next())
        if some(t):
            dve.wait_ge(pT_filled, t)
        dve.wait_ge(zeroed, 1)
        for b in range(2):
            half = slice(64 * b, 64 * b + 64)
            i = nc.vector.tensor_tensor(out=pbd[half, :, 64 * b:64 * b + 64], in0=pr[half, :, :],
                                        in1=rsum[half, :].unsqueeze(2).broadcast_to([64, GU, S]), op=ALU.mult)
        i.then_inc(p_ready, 1)

    def transpose_pe(pe, t):
        pe.wait_ge(p_ready, t + 1)
        if some(t):
            pe.wait_ge(pT_ready, t)
        for g in range(GU):
            i = nc.tensor.transpose(TB[:, g * P:(g + 1) * P], pbd[:, g, :], core.ident[:])
        i.then_inc(pT_filled, 1)

    def transposed_act(act, t):
        act.wait_ge(pT_filled, t + 1)
        if some(t):
            act.wait_ge(y_ready, t)
        nc.scalar.activation(pT[:], TB[:, 0:UNIT], ACT.Copy).then_inc(pT_ready, 1)

    def readout_pe(pe, t, par):
        pe.wait_ge(pT_ready, t + 1)
        if some(t):
            pe.wait_ge(y_used, t)
        for g in range(GU):
            i = nc.tensor.matmul(YB[:, g * D:(g + 1) * D], pT[:, g * P:(g + 1) * P], ctx[par][:, g, :], start=True, stop=True)
        i.then_inc(y_ready, 1)

    def residual_dve(dve, t):
        dve.wait_ge(y_ready, t + 1)
        xt = x[:, bass.ds(t * (GU * D), GU * D)]
        nc.vector.tensor_tensor(out=xt, in0=YB[:], in1=xt, op=ALU.add).then_inc(y_used, 1)

    def load_ctx(sp, t, par):
        if some(t - 1):
            sp.wait_ge(y_ready, t - 1)
        sp.sem_inc(passed, 1)
        sp.dma_start(ctxT[par][:], args["ctxT"].rearrange("(c p) n -> p c n", p=P)[:, :, bass.ds(t * UNIT, UNIT)]).then_inc(ctx_in[par], 16)
        sp.dma_start(ctx[par][:], args["ctx"].rearrange("(g p) d -> p g d", p=P)[:, bass.ds(t * GU, GU), :]).then_inc(ctx_in[par], 16)

    def unit_pe(pe, t, par):
        scores_pe(pe, t, par)
        if not is_last(t):
            input_pe(pe, t + 1)
        transpose_pe(pe, t)
        readout_pe(pe, t, par)

    def unit_act(act, t, par):
        exp_act(act, t)
        if not is_last(t):
            input_act(act, t + 1)
        transposed_act(act, t)

    def unit_dve(dve, t, par):
        if not is_last(t):
            norm_dve(dve, t + 1)
        softmax_dve(dve, t)
        normalize_dve(dve, t)
        residual_dve(dve, t)

    def unit_pool(pool, t, par):
        if not is_last(t):
            norm_pool(pool, t + 1)

    with nc.Block() as block:
        @block.sync
        def _(sp):
            sp.dma_start(keep[:], args["keep"].rearrange("p (g k) -> p g k", k=S)).then_inc(weights_in, 16)
            load_ctx(sp, 0, 0)
            load_ctx(sp, 1, 1)
            with sp.Fori(1, NU // 2) as pair:
                load_ctx(sp, pair * 2, 0)
                load_ctx(sp, pair * 2 + 1, 1)

        @block.tensor
        def _(pe):
            input_pe(pe, 0)
            unit_loop(pe, unit_pe)

        @block.scalar
        def _(act):
            input_act(act, 0)
            unit_loop(act, unit_act)

        @block.vector
        def _(dve):
            dve.wait_ge(weights_in, 16)
            norm_dve(dve, 0)
            unit_loop(dve, unit_dve)

        @block.gpsimd
        def _(pool):
            nc.gpsimd.memset(pbd[:], 0.0).then_inc(zeroed, 1)
            norm_pool(pool, 0)
            unit_loop(pool, unit_pool)
    st.close()


def build_program(nc, args, stages):
    ctx = ExitStack()
    with ctx:
        core = Core(nc, ctx, args)
        load_block(core)
        if 0 in stages:
            head_attention_stage(core, "att8", quant=True)
        if 1 in stages:
            ffn_stage(core, "peer", "peer", "ln", blocks=16)
        if 2 in stages:
            linear_attention_stage(core)
        if 3 in stages:
            ffn_stage(core, "ffn4", "relu", "ln", blocks=8)
        if 4 in stages:
            memory_attention_stage(core)
        if 5 in stages:
            self_attention_stage(core)
            ffn_stage(core, "moe2a", "gated", "scratch", blocks=13, top_k=6)
            ffn_stage(core, "moe2b", "gated", "scratch", blocks=12, top_k=6, first=13)
        if 6 in stages:
            head_attention_stage(core, "att32", quant=False)
        if 7 in stages:
            ffn_stage(core, "moe3", "gated", "ln", blocks=16, top_k=2, store=True)


def lay_out(i):
    import numpy as np
    i = {k: np.asarray(v) for k, v in i.items()}
    c = np.ascontiguousarray
    a = {"x": i["x"].reshape(T, D)}
    a["ctx"] = i["ctx_2048"].reshape(T, D)
    for w in ("Wq", "Wg", "Wo", "Wkv"):
        a["l_" + w.lower() + "T"] = c(i["L1_xattn_" + w].T)
    a["bg"] = c(np.broadcast_to(i["L1_xattn_bg"], (P, D)))
    a["bdmask"] = (np.arange(P)[:, None] // 16 == np.arange(P)[None, :] // 16).astype(np.float32)
    a["ctxT"] = c(i["ctx_2048"].reshape(T, D).T)
    a["mask"] = i["mask_BxSxS2_ff0"].reshape(T, S)
    a["keep"] = c(np.repeat(i["mask_BxS2_bk0"], S, axis=0).reshape(NG, P, S).transpose(1, 0, 2).reshape(P, NG * S))
    a["hmask"] = (np.arange(P)[:, None] // 16 == np.arange(8)[None, :]).astype(np.float32)
    a["wq"], a["wo"] = i["L0_xattn_wq"], i["L0_xattn_wo"]
    a["wkT"], a["wvT"] = c(i["L0_xattn_wk"].T), c(i["L0_xattn_wv"].T)
    a["bk"] = c(i["L0_xattn_bk"].reshape(C, P).T)
    for w in ("bq", "bv", "bo"):
        a[w] = c(np.broadcast_to(i["L0_xattn_" + w], (P, D)))
    for w in ("wq", "wk", "wv", "wo", "wg"):
        a["z_" + w + "T"] = c(i["L3_xattn_" + w].T)
    a["norm_w"] = c(i["L3_xattn_norm_w"].reshape(C, P).T)
    a["p_wq"] = i["L0_ffn_Wq"]
    a["p_keys"] = c(i["L0_ffn_keys"].transpose(2, 3, 0, 1).reshape(P, 4, P))
    a["e_downT"] = c(i["L0_ffn_e_down"].T)
    a["e_up"] = i["L0_ffn_e_up"]
    a["up_q"] = c(i["L1_ffn_w_up_q"].T)
    a["up_s"] = c(np.repeat(i["L1_ffn_w_up_scale"].T, 64, axis=0))
    a["down_q"] = c(i["L1_ffn_w_down_q"].T)
    a["down_s"] = c(np.repeat(i["L1_ffn_w_down_scale"].T, 64, axis=0))
    a["up_aT"] = c(i["L1_ffn_w_up_lora_a"].T)
    a["up_b"] = i["L1_ffn_w_up_lora_b"]
    a["down_aT"] = c(i["L1_ffn_w_down_lora_a"].T)
    a["down_b"] = i["L1_ffn_w_down_lora_b"]
    a["bup"] = c(i["L1_ffn_b_up"].reshape(-1, P).T)
    a["bdn"] = c(np.broadcast_to(i["L1_ffn_b_down"], (P, D)))

    def selection(rows, per):
        s = np.zeros((2, 32, rows), np.float32)
        s[:, np.minimum(np.arange(rows) // per, 16), np.arange(rows)] = 1.0
        s = s.reshape(64, rows)
        return s

    for w in ("q", "k", "v", "o"):
        a["a_w" + w] = i["L2_ffn_w" + w]
    a["ln1"] = c(i["L2_ffn_ln1_w"].reshape(C, P).T)
    a["ln2"] = c(i["L2_ffn_ln2_w"].reshape(C, P).T)
    q = np.arange(P)
    a["causal"] = np.where((q[:, None] // S == q[None, :] // S) & (q[:, None] >= q[None, :]), 0.0, -1e9).astype(np.float32)
    rows = 25 * P

    def padded(v):
        out = np.zeros((rows, D), np.float32)
        out[:len(v)] = v
        return out

    a["moe2_wg"] = c(padded(np.concatenate([i["L2_ffn_eg_w"].reshape(-1, D), i["L2_ffn_sg_w"]])).T)
    a["moe2_wu"] = c(padded(np.concatenate([i["L2_ffn_eu_w"].reshape(-1, D), i["L2_ffn_su_w"]])).T)
    a["moe2_wd"] = padded(np.concatenate([i["L2_ffn_ed_w"].transpose(0, 2, 1).reshape(-1, D), i["L2_ffn_sd_w"].T]))
    a["moe2_gate"] = c(i["L2_ffn_gate_w"].T)
    a["moe2_sel"] = selection(rows, 176)
    a["moe3_wg"] = c(i["L3_ffn_wg"].transpose(1, 0, 2).reshape(D, -1))
    a["moe3_wu"] = c(i["L3_ffn_wu"].transpose(1, 0, 2).reshape(D, -1))
    a["moe3_wd"] = c(i["L3_ffn_wd"].reshape(-1, D))
    a["moe3_gate"] = c(i["L3_ffn_gate_w"].T)
    a["moe3_sel"] = selection(2048, 128)
    return a


def build(nc, inputs, stages=tuple(range(8))):
    arrays, args = {}, {}
    for name, v in lay_out(inputs).items():
        arrays[f"in_{name}_dram"] = v
        args[name] = nc.dram_tensor(f"in_{name}_dram", v.shape, mybir.dt.from_np(v.dtype), kind="ExternalInput").ap()
    args["t_scratch"] = nc.dram_tensor("t_scratch", (D, T), FP32, kind="Internal").ap()
    args["out"] = nc.dram_tensor("out_0_dram", (T, D), FP32, kind="ExternalOutput").ap()
    build_program(nc, args, stages)
    return arrays


def kernel(**inputs):
    import concourse.bacc as _bacc
    from concourse.bass_utils import run_bass_kernel_spmd as _run
    nc = _bacc.Bacc("TRN2", target_bir_lowering=False, num_devices=1)
    arrays = build(nc, inputs)
    r = _run(nc, [arrays], core_ids=[0])
    return r.results[0]["out_0_dram"].reshape(B, S, D)
```
